# Optimizing a Trainium2 kernel written in Bass

```python
import numpy as np
import jax
import jax.numpy as jnp

def _softmax(x, axis=-1):
    return jax.nn.softmax(x, axis=axis)

def _gelu(x):
    return jax.nn.gelu(x, approximate=True)

def _silu(x):
    return jax.nn.silu(x)

def _sigmoid(x):
    return jax.nn.sigmoid(x)

def _layernorm(x, axis=-1, eps=1e-05):
    m = jnp.mean(x, axis=axis, keepdims=True)
    v = jnp.var(x, axis=axis, keepdims=True)
    return (x - m) / jnp.sqrt(v + eps)

def _scatter_add(tgt, idx, src, axis=0):
    return tgt.at[idx].add(src)

def _segment_sum(src, seg, n):
    return jax.ops.segment_sum(src, seg, n)
kernel_name = 'mk_flamingo_gated_d2_seqx_r2_78be30'

def setup_inputs(seed: int=0):
    np.random.seed(seed)
    _w = jnp.asarray

    def _rec_inputs():
        import jax
        import jax.numpy as jnp
        _rk = jax.random.key(seed)
        x = -0.0002928 + 1 * jax.random.normal(jax.random.fold_in(_rk, 1), (8, 100, 512), jnp.float32)
        _lenS = 100 - jax.random.randint(jax.random.fold_in(_rk, 7), (8,), 0, max(1, 100 // 4) + 1, jnp.int32)
        _lenS2 = 722 - jax.random.randint(jax.random.fold_in(_rk, 8), (8,), 0, max(1, 722 // 4) + 1, jnp.int32)
        _ctx_1024P = jax.random.normal(jax.random.fold_in(_rk, 11), (8, 16, 512), jnp.float32)
        _ctx_1024c = jax.random.dirichlet(jax.random.fold_in(_rk, 511), 0.3 * jnp.ones((16,), jnp.float32), (8, 722))
        _ctx_1024t = jnp.einsum('bsk,bkd->bsd', _ctx_1024c, _ctx_1024P)
        _ctx_1024t = _ctx_1024t * jax.lax.rsqrt(jnp.mean(jnp.square(_ctx_1024t)) + 1e-12) * 0.953939
        ctx_1024 = 4.13588e-05 + 0.999923 * (_ctx_1024t + 0.3 * jax.random.normal(jax.random.fold_in(_rk, 611), (8, 722, 512), jnp.float32))
        _g = jax.random.normal(jax.random.fold_in(_rk, 9001), (2, 2), jnp.float32)
        _g = jnp.sign(_g) * jnp.maximum(jnp.abs(_g), 1.0) + (_g == 0) * 1.0
        g_xattn = _g[0]
        g_ffn = _g[1]
        return (x, ctx_1024, g_xattn, g_ffn)
    x, ctx_1024, g_xattn, g_ffn = _rec_inputs()

    def _L0_xattn_setup():
        import jax, jax.numpy as jnp
        import numpy as np
        D_MODEL = 512
        NUM_HEADS = 16
        DEPTH = D_MODEL // NUM_HEADS
        B, LQ, LKV = (4, 512, 1024)

        def _xavier(key, shape):
            fan_in, fan_out = (shape[1], shape[0])
            limit = float(np.sqrt(6.0 / (fan_in + fan_out)))
            return jax.random.uniform(key, shape, jnp.float32, -limit, limit)

        def _split_heads(x, b):
            return x.reshape(b, -1, NUM_HEADS, DEPTH).transpose(0, 2, 1, 3)
        key = jax.random.key(seed)
        ks = jax.random.split(key, 6)
        return {'query': jax.random.normal(ks[0], (B, LQ, D_MODEL), jnp.float32), 'value': jax.random.normal(ks[1], (B, LKV, D_MODEL), jnp.float32), 'wq_w': _xavier(ks[2], (D_MODEL, D_MODEL)), 'wk_w': _xavier(ks[3], (D_MODEL, D_MODEL)), 'wv_w': _xavier(ks[4], (D_MODEL, D_MODEL)), 'dense_w': _xavier(ks[5], (D_MODEL, D_MODEL)), 'wq_b': jnp.zeros((D_MODEL,), jnp.float32), 'wk_b': jnp.zeros((D_MODEL,), jnp.float32), 'wv_b': jnp.zeros((D_MODEL,), jnp.float32), 'dense_b': jnp.zeros((D_MODEL,), jnp.float32)}
    _L0_xattn_all = _L0_xattn_setup()
    _L0_xattn_in = {k: v for k, v in _L0_xattn_all.items() if k in ('wq_w', 'wk_w', 'wv_w', 'dense_w', 'wq_b', 'wk_b', 'wv_b', 'dense_b')}
    del _L0_xattn_all

    def _L0_ffn_setup():
        import jax, jax.numpy as jnp
        import numpy as np
        HIDDEN = 512
        INNER = 2048

        def _weight_quant(w):
            scale = 1.0 / jnp.clip(jnp.mean(jnp.abs(w)), 1e-05)
            wq = jnp.clip(jnp.round(w * scale), -1.0, 1.0) / scale
            return w + jax.lax.stop_gradient(wq - w)

        def _act_quant(x):
            scale = 127.0 / jnp.clip(jnp.max(jnp.abs(x), axis=-1, keepdims=True), 1e-05)
            xq = jnp.clip(jnp.round(x * scale), -128.0, 127.0) / scale
            return x + jax.lax.stop_gradient(xq - x)

        def _bitlinear(x, w):
            return jnp.einsum('bsi,oi->bso', _act_quant(x), _weight_quant(w))
        key = jax.random.key(seed)
        k0, k1, k2, k3 = jax.random.split(key, 4)
        x = jax.random.normal(k0, (4, 1024, HIDDEN), dtype=jnp.float32)
        w_gate = jax.random.normal(k1, (INNER, HIDDEN), dtype=jnp.float32) / np.sqrt(HIDDEN)
        w_up = jax.random.normal(k2, (INNER, HIDDEN), dtype=jnp.float32) / np.sqrt(HIDDEN)
        w_down = jax.random.normal(k3, (HIDDEN, INNER), dtype=jnp.float32) / np.sqrt(INNER)
        return {'x': x, 'w_gate': w_gate, 'w_up': w_up, 'w_down': w_down}
    _L0_ffn_all = _L0_ffn_setup()
    _L0_ffn_in = {k: v for k, v in _L0_ffn_all.items() if k in ('w_gate', 'w_up', 'w_down')}
    del _L0_ffn_all

    def _L1_xattn_setup():
        import jax, jax.numpy as jnp
        import numpy as np
        import math
        B, S, D, H = (1, 1024, 512, 16)
        DK = D // H
        DH = 64
        LOG_T_MIN = math.log(0.1)
        LOG_T_MAX = math.log(10.0)

        def _linear(x, W, b):
            return x @ W.T + b
        key = jax.random.key(seed)
        ks = jax.random.split(key, 20)
        p = 0.02
        return {'query': jax.random.normal(ks[0], (B, S, D), jnp.float32), 'key': jax.random.normal(ks[1], (B, S, D), jnp.float32), 'value': jax.random.normal(ks[2], (B, S, D), jnp.float32), 'Wq': jax.random.normal(ks[3], (D, D), jnp.float32) * p, 'bq': jax.random.normal(ks[4], (D,), jnp.float32) * p, 'Wk': jax.random.normal(ks[5], (D, D), jnp.float32) * p, 'bk': jax.random.normal(ks[6], (D,), jnp.float32) * p, 'Wv': jax.random.normal(ks[7], (D, D), jnp.float32) * p, 'bv': jax.random.normal(ks[8], (D,), jnp.float32) * p, 'Wo': jax.random.normal(ks[9], (D, D), jnp.float32) * p, 'bo': jax.random.normal(ks[10], (D,), jnp.float32) * p, 'w1': jax.random.normal(ks[11], (DH, 3), jnp.float32) * 0.3, 'b1': jax.random.normal(ks[12], (DH,), jnp.float32) * 0.1, 'w2': jax.random.normal(ks[13], (DH, DH), jnp.float32) * 0.1, 'b2': jax.random.normal(ks[14], (DH,), jnp.float32) * 0.1, 'w3': jax.random.normal(ks[15], (1, DH), jnp.float32) * 0.1, 'b3': jnp.full((1,), (LOG_T_MIN + LOG_T_MAX) / 2, jnp.float32)}
    _L1_xattn_all = _L1_xattn_setup()
    _L1_xattn_in = {k: v for k, v in _L1_xattn_all.items() if k in ('Wq', 'bq', 'Wk', 'bk', 'Wv', 'bv', 'Wo', 'bo', 'w1', 'b1', 'w2', 'b2', 'w3', 'b3')}
    del _L1_xattn_all

    def _L1_ffn_setup():
        import jax, jax.numpy as jnp
        import numpy as np
        CAPACITY = 2
        B, S, D, E, I = (4, 2048, 512, 8, 2048)
        key = jax.random.key(seed)
        k0, k1, k2, k3, k4 = jax.random.split(key, 5)
        x = jax.random.normal(k0, (B, S, D), dtype=jnp.float32)
        gate_w = jax.random.normal(k1, (E, D), dtype=jnp.float32) * 0.006
        w_gate = jax.random.normal(k2, (E, I, D), dtype=jnp.float32) * (1.0 / np.sqrt(D))
        w_up = jax.random.normal(k3, (E, I, D), dtype=jnp.float32) * (1.0 / np.sqrt(D))
        w_down = jax.random.normal(k4, (E, D, I), dtype=jnp.float32) * (1.0 / np.sqrt(I))
        return {'x': x, 'gate_w': gate_w, 'w_gate': w_gate, 'w_up': w_up, 'w_down': w_down}
    _L1_ffn_all = _L1_ffn_setup()
    _L1_ffn_in = {k: v for k, v in _L1_ffn_all.items() if k in ('gate_w', 'w_gate', 'w_up', 'w_down')}
    del _L1_ffn_all
    return {'x': x, 'ctx_1024': ctx_1024, 'g_xattn': g_xattn, 'g_ffn': g_ffn, 'L0_xattn_wq_w': _L0_xattn_in['wq_w'], 'L0_xattn_wk_w': _L0_xattn_in['wk_w'], 'L0_xattn_wv_w': _L0_xattn_in['wv_w'], 'L0_xattn_dense_w': _L0_xattn_in['dense_w'], 'L0_xattn_wq_b': _L0_xattn_in['wq_b'], 'L0_xattn_wk_b': _L0_xattn_in['wk_b'], 'L0_xattn_wv_b': _L0_xattn_in['wv_b'], 'L0_xattn_dense_b': _L0_xattn_in['dense_b'], 'L0_ffn_w_gate': _L0_ffn_in['w_gate'], 'L0_ffn_w_up': _L0_ffn_in['w_up'], 'L0_ffn_w_down': _L0_ffn_in['w_down'], 'L1_xattn_Wq': _L1_xattn_in['Wq'], 'L1_xattn_bq': _L1_xattn_in['bq'], 'L1_xattn_Wk': _L1_xattn_in['Wk'], 'L1_xattn_bk': _L1_xattn_in['bk'], 'L1_xattn_Wv': _L1_xattn_in['Wv'], 'L1_xattn_bv': _L1_xattn_in['bv'], 'L1_xattn_Wo': _L1_xattn_in['Wo'], 'L1_xattn_bo': _L1_xattn_in['bo'], 'L1_xattn_w1': _L1_xattn_in['w1'], 'L1_xattn_b1': _L1_xattn_in['b1'], 'L1_xattn_w2': _L1_xattn_in['w2'], 'L1_xattn_b2': _L1_xattn_in['b2'], 'L1_xattn_w3': _L1_xattn_in['w3'], 'L1_xattn_b3': _L1_xattn_in['b3'], 'L1_ffn_gate_w': _L1_ffn_in['gate_w'], 'L1_ffn_w_gate': _L1_ffn_in['w_gate'], 'L1_ffn_w_up': _L1_ffn_in['w_up'], 'L1_ffn_w_down': _L1_ffn_in['w_down']}

def reference(x, ctx_1024, g_xattn, g_ffn, L0_xattn_wq_w, L0_xattn_wk_w, L0_xattn_wv_w, L0_xattn_dense_w, L0_xattn_wq_b, L0_xattn_wk_b, L0_xattn_wv_b, L0_xattn_dense_b, L0_ffn_w_gate, L0_ffn_w_up, L0_ffn_w_down, L1_xattn_Wq, L1_xattn_bq, L1_xattn_Wk, L1_xattn_bk, L1_xattn_Wv, L1_xattn_bv, L1_xattn_Wo, L1_xattn_bo, L1_xattn_w1, L1_xattn_b1, L1_xattn_w2, L1_xattn_b2, L1_xattn_w3, L1_xattn_b3, L1_ffn_gate_w, L1_ffn_w_gate, L1_ffn_w_up, L1_ffn_w_down):
    import jax
    import jax.numpy as jnp

    def _L0_xattn_ref(query, value, wq_w, wk_w, wv_w, dense_w, wq_b, wk_b, wv_b, dense_b):
        import jax, jax.numpy as jnp
        import numpy as np
        D_MODEL = 512
        NUM_HEADS = 16
        DEPTH = D_MODEL // NUM_HEADS
        B, LQ, LKV = (4, 512, 1024)

        def _xavier(key, shape):
            fan_in, fan_out = (shape[1], shape[0])
            limit = float(np.sqrt(6.0 / (fan_in + fan_out)))
            return jax.random.uniform(key, shape, jnp.float32, -limit, limit)

        def _split_heads(x, b):
            return x.reshape(b, -1, NUM_HEADS, DEPTH).transpose(0, 2, 1, 3)
        b = query.shape[0]
        q = query @ wq_w.T + wq_b
        k = value @ wk_w.T + wk_b
        v = value @ wv_w.T + wv_b
        q = _split_heads(q, b)
        k = _split_heads(k, b)
        v = _split_heads(v, b)
        scale = jnp.sqrt(jnp.asarray(DEPTH, q.dtype))
        scores = jnp.einsum('bhqd,bhkd->bhqk', q, k) / scale
        attn = jax.nn.softmax(scores, axis=-1)
        ctx = jnp.einsum('bhqk,bhkd->bhqd', attn, v)
        ctx = ctx.transpose(0, 2, 1, 3).reshape(b, -1, D_MODEL)
        return ctx @ dense_w.T + dense_b

    def _L0_ffn_ref(x, w_gate, w_up, w_down):
        import jax, jax.numpy as jnp
        import numpy as np
        HIDDEN = 512
        INNER = 2048

        def _weight_quant(w):
            scale = 1.0 / jnp.clip(jnp.mean(jnp.abs(w)), 1e-05)
            wq = jnp.clip(jnp.round(w * scale), -1.0, 1.0) / scale
            return w + jax.lax.stop_gradient(wq - w)

        def _act_quant(x):
            scale = 127.0 / jnp.clip(jnp.max(jnp.abs(x), axis=-1, keepdims=True), 1e-05)
            xq = jnp.clip(jnp.round(x * scale), -128.0, 127.0) / scale
            return x + jax.lax.stop_gradient(xq - x)

        def _bitlinear(x, w):
            return jnp.einsum('bsi,oi->bso', _act_quant(x), _weight_quant(w))
        gate = jax.nn.silu(_bitlinear(x, w_gate))
        up = _bitlinear(x, w_up)
        return _bitlinear(gate * up, w_down)

    def _L1_xattn_ref(query, key, value, Wq, bq, Wk, bk, Wv, bv, Wo, bo, w1, b1, w2, b2, w3, b3):
        import jax, jax.numpy as jnp
        import numpy as np
        import math
        B, S, D, H = (1, 1024, 512, 16)
        DK = D // H
        DH = 64
        LOG_T_MIN = math.log(0.1)
        LOG_T_MAX = math.log(10.0)

        def _linear(x, W, b):
            return x @ W.T + b
        b, sq, d = query.shape
        sk = key.shape[1]
        h, dk = (H, DK)
        Q = _linear(query, Wq, bq).reshape(b, sq, h, dk).transpose(0, 2, 1, 3)
        K = _linear(key, Wk, bk).reshape(b, sk, h, dk).transpose(0, 2, 1, 3)
        V = _linear(value, Wv, bv).reshape(b, sk, h, dk).transpose(0, 2, 1, 3)
        qk = jnp.einsum('bhqd,bhkd->bhqk', Q, K)
        scores = qk / math.sqrt(dk)
        mean_sim = scores.mean(axis=(-2, -1))
        max_sim = scores.max(axis=-1).mean(axis=-1)
        probs = jax.nn.softmax(scores, axis=-1)
        entropy_proxy = jnp.var(probs, axis=-1, ddof=1).mean(axis=-1)
        feats = jnp.stack([mean_sim, max_sim, entropy_proxy], axis=-1)
        hidden = jax.nn.gelu(_linear(feats, w1, b1), approximate=False)
        hidden = jax.nn.gelu(_linear(hidden, w2, b2), approximate=False)
        log_t = jnp.clip(_linear(hidden, w3, b3), LOG_T_MIN, LOG_T_MAX)
        t = jnp.exp(log_t)[..., None]
        attn_scores = qk / (2.0 * t)
        attn = jax.nn.softmax(attn_scores, axis=-1)
        attn = jnp.nan_to_num(attn, nan=0.0)
        out = jnp.einsum('bhqk,bhkd->bhqd', attn, V)
        out = out.transpose(0, 2, 1, 3).reshape(b, sq, d)
        return _linear(out, Wo, bo)

    def _L1_ffn_ref(x, gate_w, w_gate, w_up, w_down):
        import jax, jax.numpy as jnp
        import numpy as np
        CAPACITY = 2
        B, S, D = x.shape
        E = gate_w.shape[0]
        k = S // E * CAPACITY
        logits = jnp.einsum('bsd,ed->bse', x, gate_w)
        affinity = jax.nn.softmax(logits, axis=-1)
        affinity = jnp.transpose(affinity, (0, 2, 1))
        gating, idx = jax.lax.top_k(affinity, k)
        bidx = jnp.arange(B)[:, None, None]
        x_in = x[bidx, idx]
        h = jax.nn.silu(jnp.einsum('bekd,eid->beki', x_in, w_gate)) * jnp.einsum('bekd,eid->beki', x_in, w_up)
        x_e = jnp.einsum('beki,edi->bekd', h, w_down)
        out = jnp.zeros_like(x).at[bidx, idx].add(gating[..., None] * x_e)
        return out
    x = x + jnp.tanh(g_xattn[0]) * _L0_xattn_ref(_layernorm(x, axis=-1), ctx_1024, L0_xattn_wq_w, L0_xattn_wk_w, L0_xattn_wv_w, L0_xattn_dense_w, L0_xattn_wq_b, L0_xattn_wk_b, L0_xattn_wv_b, L0_xattn_dense_b)
    x = x + jnp.tanh(g_ffn[0]) * _L0_ffn_ref(_layernorm(x, axis=-1), L0_ffn_w_gate, L0_ffn_w_up, L0_ffn_w_down)
    x = x + jnp.tanh(g_xattn[1]) * _L1_xattn_ref(_layernorm(x, axis=-1), ctx_1024, ctx_1024, L1_xattn_Wq, L1_xattn_bq, L1_xattn_Wk, L1_xattn_bk, L1_xattn_Wv, L1_xattn_bv, L1_xattn_Wo, L1_xattn_bo, L1_xattn_w1, L1_xattn_b1, L1_xattn_w2, L1_xattn_b2, L1_xattn_w3, L1_xattn_b3)
    x = x + jnp.tanh(g_ffn[1]) * _L1_ffn_ref(_layernorm(x, axis=-1), L1_ffn_gate_w, L1_ffn_w_gate, L1_ffn_w_up, L1_ffn_w_down)
    return x

_drawn_inputs = setup_inputs


def setup_inputs(seed=0):
    import zlib

    import numpy as np

    out = dict(_drawn_inputs(seed))
    spreads = {'g_ffn': (-1.0, 0.6),
     'L0_xattn_wq_b': (0.0, 0.404),
     'L0_xattn_wk_b': (0.0, 2.0),
     'L0_xattn_wv_b': (0.0, 0.1),
     'L0_xattn_dense_b': (0.0, 0.1)}
    factors = {'L1_xattn_bq': 8.0,
     'L1_xattn_bk': 64.0,
     'L1_xattn_bv': 7.042,
     'L1_xattn_bo': 3.14,
     'L1_xattn_w1': 8.0,
     'L1_xattn_b1': 52.069,
     'L1_xattn_w2': 8.0,
     'L1_xattn_b2': 200.0,
     'L1_xattn_w3': 8.0}
    for name, (base, spread) in spreads.items():
        noise = np.random.default_rng([zlib.crc32(name.encode()), seed]).standard_normal(out[name].shape)
        drawn = base * np.exp(spread * noise) if base else spread * noise
        out[name] = jnp.asarray(drawn.astype(out[name].dtype))
    for name, factor in factors.items():
        out[name] = (out[name] * factor).astype(out[name].dtype)
    return out
```

```python
from contextlib import ExitStack

import concourse.bass as bass
from concourse import mybir

F32 = mybir.dt.float32
F32R = mybir.dt.float32r
BF16 = mybir.dt.bfloat16
ALU = mybir.AluOpType
ACT = mybir.ActivationFunctionType
AX = mybir.AxisListType.X

P = 128
NB, NQ, D = 8, 100, 512
NK = 722
NH, DH = 16, 32
DC = D // P
HPC = P // DH
KC = (NK + P - 1) // P
KFULL = NK // P
KREST = NK - KFULL * P
KHALF = NK // 2
KEVEN = KHALF + KHALF % 2
NKPAD = KHALF + KEVEN
BANK = 512
INNER = 2048
NE = 8
CAP = NQ // NE * 2
SLOTS = NB * CAP
LN_EPS = 1e-5
ROUND = 12582912.0
QMAX = 127.0
LOG_T_MIN, LOG_T_MAX = -2.302585092994046, 2.302585092994046


FREE = 1


def ksize(j):
    return P if j < KFULL else KREST


SPLIT = ((0, 0), (0, 1), (1, 0))


def one(ap, i):
    return ap[:, bass.ds(i, 1)]


def rows(v):
    return v.rearrange("(a n) -> a n", a=1)


def spread(v, n):
    return rows(v).broadcast_to([n, v.shape[0]])


class Mem:

    def __init__(self, nc, ctx, tag):
        self.nc, self.ctx, self.tag, self.sems = nc, ctx, tag, []
        ctx.callback(self.leave)

    def leave(self):
        if self.sems:
            self.nc.clear_and_free_semaphores(self.sems)
            self.nc.all_engine_barrier()

    def sb(self, name, shape, dt=F32):
        return self.ctx.enter_context(self.nc.sbuf_tensor(f"{self.tag}_{name}", shape, dt))

    def ps(self, name, shape, dt=F32):
        return self.ctx.enter_context(self.nc.psum_tensor(f"{self.tag}_{name}", shape, dt))

    def sem(self, name):
        self.sems.append(self.nc.alloc_semaphore(f"{self.tag}_{name}"))
        return self.sems[-1]


class Chain:

    def __init__(self, eng, sem):
        self.eng, self.sem, self.n, self.base = eng, sem, 0, 0

    def __call__(self, ins):
        ins.then_inc(self.sem, 1)
        self.n += 1
        self.eng.wait_ge(self.sem, self.base + self.n)

    def loop(self, i, per):
        self.base, self.n = self.before + i * per, 0

    def enter(self):
        self.before, self.n, self.base = self.n, 0, 0

    def leave(self, passes, per):
        if self.n != per:
            raise ValueError(f"{self.n} results in a pass, {per} were said")
        self.base, self.n = 0, self.before + passes * per


def setup_stage(nc, S, x, g_xattn, g_ffn):
    with ExitStack() as ctx:
        m = Mem(nc, ctx, "setup")
        gates = m.sb("gates", [P, 4])
        x_in, ident_zero, ident_done, gates_done = (m.sem(n) for n in ("x_in", "ident_zero", "ident_done", "gates_done"))
        with nc.Block() as block:

            @block.sync
            def _(sp):
                sp.dma_start(gates[:, 0:2], spread(g_xattn, P)).then_inc(x_in, 16)
                sp.dma_start(gates[:, 2:4], spread(g_ffn, P)).then_inc(x_in, 16)
                sp.dma_start(S.X[0:NQ], x.rearrange("b q d -> q b d")).then_inc(x_in, 16)
                sp.wait_ge(x_in, 48)

            @block.gpsimd
            def _(pool):
                nc.gpsimd.memset(S.ident[:], 0.0).then_inc(ident_zero, 1)
                nc.gpsimd.memset(S.ones[:], 1.0).then_inc(ident_zero, 1)
                pool.wait_ge(ident_zero, 2)
                nc.gpsimd.affine_select(out=S.ident[:], in_=S.ident[:], compare_op=ALU.not_equal, fill=1.0,
                                        base=0, pattern=[[-1, P]], channel_multiplier=1).then_inc(ident_done, 1)

            @block.vector
            def _(dve):
                dve.wait_ge(ident_done, 1)
                nc.vector.tensor_copy(S.identb[:], S.ident[:]).then_inc(gates_done, 1)

            @block.scalar
            def _(act):
                act.wait_ge(x_in, 48)
                nc.scalar.activation(S.tanh_g[:], gates[:], ACT.Tanh).then_inc(gates_done, 1)


def attention_stage(nc, S, layer, ctx_dram, wq, bq, wk, bk, wv, bv, wo, bo, mlp=None):
    L1 = mlp is not None
    tag = f"at{layer}"
    with ExitStack() as ctx:
        m = Mem(nc, ctx, tag)
        sb, ps, sem = m.sb, m.ps, m.sem
        wqT, woT = sb("wqT", [P, DC, D]), sb("woT", [P, DC, D])
        wkT, wvT = sb("wkT", [P, 2, DC, D], F32R), sb("wvT", [P, 2, DC, D], F32R)
        bias_q, bias_k, bias_v = (sb(f"bias_{n}", [P, DC]) for n in "qkv")
        bias_o = sb("bias_o", [P, D])
        stats = sb("stats", [P, NB, 6])
        mean_var = sb("mean_var", [P, NB, 2])
        std, rstd = sb("std", [P, NB]), sb("rstd", [P, NB])
        xn = sb("xn", [P, D])
        ctx_nat = sb("ctx_nat", [P, KC, D])
        ctxT = sb("ctxT", [P, 2, DC, NKPAD], F32R)
        QT = sb("QT", [P, DC, NQ])
        Qm = sb("Qm", [P, 2, DC, HPC, NQ], F32R)
        KT = sb("KT", [P, 2, DC, NKPAD], F32R)
        V = sb("V", [P, KC, D])
        group = sb("group", [P, HPC])
        NP = NH if L1 else 3
        probs = sb("probs", [P, NP, NK])
        probsT = sb("probsT", [P, 2, KC, NQ])
        xnT = probsT[:, 0, 0:DC, :]
        neg_max, denom, rdenom = (sb(n, [P, NH]) for n in ("neg_max", "denom", "rdenom"))
        OT = QT
        y = xn
        ksum = sb("ksum", [P, DC, 2])
        if L1:
            w1, b1, w2, b2, w3, b3 = mlp
            DM = w1.shape[0]
            scores = probs
            junk = probsT[:].rearrange("p a j q -> p (a j q)")[:, 0:NK]
            w_nat = scores[:].rearrange("p h k -> p (h k)")[:, 0:2 * DC * D].rearrange("p (a o i) -> p a o i", a=2, o=DC)
            maxs, denom1, sqsum, varr = (sb(n, [P, NH]) for n in ("maxs", "denom1", "sqsum", "varr"))
            qsum, ksum1, qk4 = sb("qsum", [P, DC]), sb("ksum1", [P, DC]), sb("qk4", [P, DC])
            qk_heads = sb("qk_heads", [P, DC, HPC])
            w1_all = sb("w1_all", [P, DM, 3])
            w1_scaled = sb("w1_scaled", [P, 3, DM])
            w2_nat, w2T = sb("w2_nat", [DM, DM]), sb("w2T", [DM, P])
            w3_col, w3_all = sb("w3_col", [DM, 1]), sb("w3_all", [DM, P])
            b1_col, b2_col, b3_all = sb("b1_col", [DM, 1]), sb("b2_col", [DM, 1]), sb("b3_all", [P, 1])
            hid1, hid2 = sb("hid1", [DM, NH]), sb("hid2", [DM, NH])
            log_t, inv_t, ratio, bias2 = (sb(n, [P, NH]) for n in ("log_t", "inv_t", "ratio", "bias2"))
        else:
            w_nat = sb("w_nat", [P, 2, DC, D])
        wide = ps("wide", [P, 4, BANK])
        tb = ps("tb", [P, 2, BANK])
        ob = ps("ob", [P, BANK])
        mb = ps("mb", [P, BANK])

        w_in = [sem("w_in0"), sem("w_in1")]
        whigh_ready, wT_ready, wT_mm = (sem(n) for n in ("whigh_ready", "wT_ready", "wT_mm"))
        small_in, ctx_in, dve_own, act_own = (sem(n) for n in ("small_in", "ctx_in", "dve_own", "act_own"))
        var_ready, std_ready, pre_done = (sem(n) for n in ("var_ready", "std_ready", "pre_done"))
        proj_mm, high_done, proj_done = (sem(n) for n in ("proj_mm", "high_done", "proj_done"))
        qhigh_done, qm_ready = sem("qhigh_done"), sem("qm_ready")
        xn_ready, v_mm, v_act, v_dve = (sem(n) for n in ("xn_ready", "v_mm", "v_act", "v_dve"))
        score_mm, max_ready, exp_done = (sem(n) for n in ("score_mm", "max_ready", "exp_done"))
        rd_ready, p_ready = sem("rd_ready"), sem("p_ready")
        pT_mm0, pT_mm1, pT_act, pT_dve = (sem(n) for n in ("pT_mm0", "pT_mm1", "pT_act", "pT_dve"))
        pv_mm, ot_ready, y_mm, x_done, group_own = (sem(n) for n in ("pv_mm", "ot_ready", "y_mm", "x_done", "group_own"))
        if L1:
            stat_ready, h1_mm, h1_act, h2_mm, h2_act, t_mm, clip_ready, inv_ready, ratio_ready, first_exp = (
                sem(n) for n in ("stat_ready", "h1_mm", "h1_act", "h2_mm", "h2_act", "t_mm", "clip_ready",
                                 "inv_ready", "ratio_ready", "first_exp"))
            w2_mm = sem("w2_mm")
        S_FREE = max_ready if L1 else exp_done
        NSMALL = 4 + (6 if L1 else 0)
        NG = 16
        G_XN, G_Q, G_K = 6, 7, 8
        sizes = [ksize(j) for j in range(KC)]
        scale = float(DH) ** -0.5

        with nc.Block() as block:

            @block.sync
            def _(sp):
                for n, w in enumerate((wq, wk, wv, wo)):
                    if n >= 2:
                        sp.wait_ge(wT_mm, 4 * (n - 1))
                    sp.dma_start(w_nat[:, n % 2], w.rearrange("(o p) i -> p o i", p=P)).then_inc(w_in[n % 2], 16)
                for bias, col in ((bq, bias_q), (bk, bias_k), (bv, bias_v)):
                    sp.dma_start(col[:], bias.rearrange("(c p) -> p c", p=P), allow_slow_non_contiguous=True).then_inc(small_in, 16)
                sp.dma_start(bias_o[:], spread(bo, P)).then_inc(small_in, 16)
                if L1:
                    sp.dma_start(w1_all[:], w1.rearrange("(a o) j -> a o j", a=1).broadcast_to([P, DM, 3])).then_inc(small_in, 16)
                    sp.dma_start(w2_nat[:], w2).then_inc(small_in, 16)
                    sp.dma_start(w3_col[:], w3.rearrange("a d -> d a"), allow_slow_non_contiguous=True).then_inc(small_in, 16)
                    sp.dma_start(b1_col[:], b1.rearrange("(d a) -> d a", a=1), allow_slow_non_contiguous=True).then_inc(small_in, 16)
                    sp.dma_start(b2_col[:], b2.rearrange("(d a) -> d a", a=1), allow_slow_non_contiguous=True).then_inc(small_in, 16)
                    sp.dma_start(b3_all[:], spread(b3, P)).then_inc(small_in, 16)

                def load_ctx(b):
                    src = ctx_dram[bass.ds(b, 1)].rearrange("a k d -> (a k) d")
                    sp.dma_start(ctx_nat[:, 0:KFULL], src[0:KFULL * P].rearrange("(j p) d -> p j d", p=P)).then_inc(ctx_in, 16)
                    sp.dma_start(ctx_nat[0:KREST, KFULL], src[KFULL * P:NK]).then_inc(ctx_in, 16)

                load_ctx(0)
                with sp.Fori(0, NB - 1) as b:
                    sp.wait_ge(proj_mm, b * NG + KC)
                    load_ctx(b + 1)
                sp.wait_ge(ctx_in, 32 * NB)

            @block.tensor
            def _(pe):
                pe.sem_inc(pT_mm1, FREE)
                for n in range(4):
                    pe.wait_ge(w_in[n % 2], 16 * (n // 2 + 1))
                    for i in range(DC):
                        if n >= 1:
                            pe.wait_ge(wT_ready, DC * (n - 1) + i + 1)
                        for o in range(DC):
                            last = nc.tensor.transpose(wide[:, i, o * P:(o + 1) * P], w_nat[:, n % 2, o, i * P:(i + 1) * P], S.ident[:])
                        last.then_inc(wT_mm, 1)
                pe.wait_ge(wT_ready, 4 * DC)
                pe.wait_ge(pre_done, 1)
                if L1:
                    nc.tensor.transpose(mb[0:DM, 0:DM], w2_nat[:], S.ident[0:DM, 0:DM]).then_inc(w2_mm, 1)
                    pe.wait_ge(pre_done, 2)

                with pe.Fori(0, NB) as b:

                    def free_bank(g):
                        if g < 4:
                            pe.wait_ge(S_FREE, FREE + b * NH)
                        else:
                            pe.wait_ge(proj_done, b * NG + g - 4 + 1)

                    pe.wait_ge(ctx_in, 32 * b + 32)
                    for j in range(KC):
                        free_bank(j)
                        for c in range(DC):
                            last = nc.tensor.transpose(wide[:, j % 4, c * P:c * P + sizes[j]],
                                                       ctx_nat[0:sizes[j], j, c * P:(c + 1) * P], S.ident[0:sizes[j], 0:sizes[j]])
                        last.then_inc(proj_mm, 1)
                    free_bank(G_XN)
                    pe.wait_ge(xn_ready, b + 1)
                    for c in range(DC):
                        last = nc.tensor.transpose(wide[:, G_XN % 4, c * P:c * P + NQ], xn[0:NQ, c * P:(c + 1) * P], S.ident[0:NQ, 0:NQ])
                    last.then_inc(proj_mm, 1)
                    free_bank(G_Q)
                    pe.wait_ge(proj_done, b * NG + G_XN + 1)
                    for o in range(DC):
                        for i in range(DC):
                            last = nc.tensor.matmul(wide[:, G_Q % 4, o * P:o * P + NQ], wqT[:, i, o * P:(o + 1) * P], xnT[:, i, :],
                                                    start=(i == 0), stop=(i == DC - 1))
                    last.then_inc(proj_mm, 1)
                    for k in range(2 * DC):
                        g, o, half = G_K + k, k // 2, k % 2
                        free_bank(g)
                        for i in range(DC):
                            for n, (sw, sc) in enumerate(SPLIT):
                                last = nc.tensor.matmul(wide[:, g % 4, 0:KEVEN], wkT[:, sw, i, o * P:(o + 1) * P],
                                                        ctxT[:, sc, i, half * KHALF:half * KHALF + KEVEN],
                                                        start=(i == 0 and n == 0), stop=(i == DC - 1 and n == 2))
                        last.then_inc(proj_mm, 1)

                    def values(j):
                        if j < 2:
                            pe.wait_ge(pT_act if j == 0 else pT_dve, FREE + b * NH)
                        else:
                            pe.wait_ge(v_act if j % 2 == 0 else v_dve, b * 3 + j // 2)
                        for i in range(DC):
                            for n, (sc, sw) in enumerate(SPLIT):
                                last = nc.tensor.matmul(tb[0:sizes[j], j % 2, :], ctxT[:, sc, i, j * P:j * P + sizes[j]], wvT[:, sw, i, :],
                                                        start=(i == 0 and n == 0), stop=(i == DC - 1 and n == 2))
                        last.then_inc(v_mm, 1)

                    def score(h):
                        if h < 2:
                            pe.wait_ge(qm_ready, b + 1)
                            pe.wait_ge(proj_done, b * NG + NG)
                        else:
                            pe.wait_ge(S_FREE, FREE + b * NH + h - 1)
                        c, r = h // HPC, h % HPC
                        for half in range(2):
                            for n, (sq, sk) in enumerate(SPLIT):
                                last = nc.tensor.matmul(wide[0:NQ, 2 * (h % 2) + half, 0:KEVEN], Qm[:, sq, c, r, :],
                                                        KT[:, sk, c, half * KHALF:half * KHALF + KEVEN], start=(n == 0), stop=(n == 2))
                        last.then_inc(score_mm, 1)

                    def transpose_probs(h):
                        pe.wait_ge(p_ready, b * NH + h + 1)
                        for half, mm in enumerate((pT_mm0, pT_mm1)):
                            if h == 0:
                                pe.wait_ge(v_act if half == 0 else v_dve, b * 3 + 3)
                            else:
                                pe.wait_ge(pT_act if half == 0 else pT_dve, FREE + b * NH + h)
                            for t in range(3):
                                j = 3 * half + t
                                last = nc.tensor.transpose(tb[0:sizes[j], half, t * NQ:(t + 1) * NQ],
                                                           probs[0:NQ, h % NP, j * P:j * P + sizes[j]], S.ident[0:NQ, 0:NQ])
                            last.then_inc(mm, 1)

                    def weigh_values(h):
                        pe.wait_ge(pT_act, FREE + b * NH + h + 1)
                        pe.wait_ge(pT_dve, FREE + b * NH + h + 1)
                        if h == 0:
                            pe.wait_ge(x_done, FREE + b)
                        c, r = h // HPC, DH * (h % HPC)
                        for j in range(KC):
                            last = nc.tensor.matmul(ob[r:r + DH, c * NQ:(c + 1) * NQ], V[0:sizes[j], j, h * DH:(h + 1) * DH],
                                                    probsT[0:sizes[j], h % 2, j, :], start=(j == 0), stop=(j == KC - 1))
                        if h == NH - 1:
                            last.then_inc(pv_mm, 1)

                    if not L1:
                        for j in range(KC):
                            values(j)
                        for h in range(NH + 3):
                            if h < NH:
                                score(h)
                            if 2 <= h < NH + 2:
                                transpose_probs(h - 2)
                            if h >= 3:
                                weigh_values(h - 3)
                    else:
                        for h in range(NH):
                            score(h)
                            if h % 2 == 1 and h // 2 < KC:
                                values(h // 2)
                        pe.wait_ge(stat_ready, b + 1)
                        nc.tensor.matmul(mb[0:DM, 0:NH], w1_scaled[:, 0, :], qk_heads[:].rearrange("p c g -> p (c g)"), start=True, stop=False)
                        nc.tensor.matmul(mb[0:DM, 0:NH], w1_scaled[0:NQ, 1, :], maxs[0:NQ, :], start=False, stop=False)
                        nc.tensor.matmul(mb[0:DM, 0:NH], w1_scaled[0:NQ, 2, :], varr[0:NQ, :], start=False, stop=True).then_inc(h1_mm, 1)
                        pe.wait_ge(h1_act, b + 1)
                        nc.tensor.matmul(mb[0:P, 0:NH], w2T[:], hid1[:], start=True, stop=True).then_inc(h2_mm, 1)
                        pe.wait_ge(h2_act, b + 1)
                        nc.tensor.matmul(mb[0:P, 0:NH], w3_all[:], hid2[:], start=True, stop=True).then_inc(t_mm, 1)
                        for h in range(NH + 1):
                            if h < NH:
                                transpose_probs(h)
                            if h >= 1:
                                weigh_values(h - 1)

                    pe.wait_ge(ot_ready, b + 1)
                    for c in range(DC):
                        last = nc.tensor.matmul(ob[0:NQ, :], OT[:, c, :], woT[:, c, :], start=(c == 0), stop=(c == DC - 1))
                    last.then_inc(y_mm, 1)

            @block.scalar
            def _(act):
                act.sem_inc(exp_done, FREE)
                act.sem_inc(pT_act, FREE)
                for n in (1, 2):
                    for i in range(DC):
                        act.wait_ge(wT_mm, DC * n + i + 1)
                        nc.scalar.copy((wkT, wvT)[n - 1][:, 0, i, :], wide[:, i, :]).then_inc(whigh_ready, 1)
                act.wait_ge(var_ready, 1)
                nc.scalar.activation(std[0:NQ, :], std[0:NQ, :], ACT.Sqrt).then_inc(std_ready, 1)

                with act.Fori(0, NB) as b:
                    for g in range(NG):
                        if g == G_XN:
                            continue
                        if g == G_Q:
                            act.wait_ge(proj_done, b * NG + G_Q + 1)
                            for r in range(HPC):
                                last = nc.scalar.activation(Qm[:, 0, :, r, :], QT[:], ACT.Copy, scale=group[:, r:r + 1])
                            last.then_inc(qhigh_done, 1)
                            continue
                        act.wait_ge(proj_mm, b * NG + g + 1)
                        bank = wide[:, g % 4, :]
                        if g < KC:
                            nc.scalar.copy(ctxT[:, 0, :, g * P:g * P + sizes[g]],
                                           bank.rearrange("p (c k) -> p c k", c=DC)[:, :, 0:sizes[g]]).then_inc(high_done, 1)
                        else:
                            o, half = (g - G_K) // 2, g % 2
                            nc.scalar.activation(KT[:, 0, o, half * KHALF:(half + 1) * KHALF], bank[:, 0:KHALF], ACT.Identity,
                                                 bias=bias_k[:, o:o + 1], accum_out=ksum[:, o, half:half + 1]).then_inc(high_done, 1)

                    def values_out(j):
                        act.wait_ge(v_mm, b * KC + j + 1)
                        nc.scalar.copy(V[0:sizes[j], j, :], tb[0:sizes[j], j % 2, :]).then_inc(v_act, 1)

                    def probsT_out(h):
                        act.wait_ge(pT_mm0, b * NH + h + 1)
                        nc.scalar.activation(probsT[:, h % 2, 0:3, :], tb[:, 0, 0:3 * NQ].rearrange("p (j q) -> p j q", j=3),
                                             ACT.Relu if L1 else ACT.Copy).then_inc(pT_act, 1)

                    if not L1:
                        for j in range(0, KC, 2):
                            values_out(j)
                        for h in range(NH + 2):
                            if h < NH:
                                act.wait_ge(max_ready, FREE + b * NH + h + 1)
                                act.wait_ge(pT_mm1, FREE + b * NH + max(h - NP + 1, 0))
                                nc.scalar.activation(probs[0:NQ, h % NP, :].rearrange("p (s k) -> p s k", s=2),
                                                     wide[0:NQ, 2 * (h % 2):2 * (h % 2) + 2, 0:KHALF], ACT.Exp,
                                                     bias=neg_max[0:NQ, h:h + 1], accum_out=denom[0:NQ, h:h + 1]).then_inc(exp_done, 1)
                            if h >= 2:
                                probsT_out(h - 2)
                    else:
                        for h in range(NH):
                            act.wait_ge(max_ready, FREE + b * NH + h + 1)
                            if h >= 1:
                                act.wait_ge(act_own, b * 2 * NH + 2 * h)
                            nc.scalar.activation(junk[0:NQ, :], scores[0:NQ, h, :], ACT.Exp, bias=neg_max[0:NQ, h:h + 1],
                                                 accum_out=denom1[0:NQ, h:h + 1]).then_inc(act_own, 1)
                            act.wait_ge(act_own, b * 2 * NH + 2 * h + 1)
                            nc.scalar.activation(junk[0:NQ, :], junk[0:NQ, :], ACT.Square,
                                                 accum_out=sqsum[0:NQ, h:h + 1]).then_inc(act_own, 1)
                            if h % 4 == 1 and h // 2 < KC:
                                values_out(h // 2)
                        act.wait_ge(act_own, b * 2 * NH + 2 * NH)
                        nc.scalar.copy(junk[0:1, 0:1], junk[0:1, 0:1]).then_inc(first_exp, 1)
                        act.wait_ge(h1_mm, b + 1)
                        nc.scalar.activation(hid1[:], mb[0:DM, 0:NH], ACT.Gelu, bias=b1_col[:]).then_inc(h1_act, 1)
                        act.wait_ge(h2_mm, b + 1)
                        nc.scalar.activation(hid2[:], mb[0:DM, 0:NH], ACT.Gelu, bias=b2_col[:]).then_inc(h2_act, 1)
                        act.wait_ge(clip_ready, b + 1)
                        nc.scalar.activation(inv_t[0:NQ, :], log_t[0:NQ, :], ACT.Exp, scale=-1.0).then_inc(inv_ready, 1)
                        act.wait_ge(ratio_ready, b + 1)
                        for h in range(NH + 2):
                            if h < NH:
                                nc.scalar.activation(probs[0:NQ, h % NP, :], scores[0:NQ, h, :], ACT.Exp, bias=bias2[0:NQ, h:h + 1],
                                                     scale=ratio[0:NQ, h:h + 1], accum_out=denom[0:NQ, h:h + 1]).then_inc(exp_done, 1)
                            if h >= 2:
                                probsT_out(h - 2)

            @block.gpsimd
            def _(pool):
                nc.gpsimd.memset(group[:], 1.0).then_inc(group_own, 1)
                pool.wait_ge(group_own, 1)
                nc.gpsimd.affine_select(out=group[:], in_=group[:], compare_op=ALU.is_ge, fill=0.0, base=0,
                                        pattern=[[-DH, HPC]], channel_multiplier=1).then_inc(group_own, 1)
                pool.wait_ge(group_own, 2)
                nc.gpsimd.affine_select(out=group[:], in_=group[:], compare_op=ALU.is_ge, fill=0.0, base=DH - 1,
                                        pattern=[[DH, HPC]], channel_multiplier=-1).then_inc(group_own, 1)
                with pool.Fori(0, NB) as b:
                    for h in range(NH):
                        pool.wait_ge(rd_ready, b * NH + h + 1)
                        p = probs[0:NQ, h % NP, :]
                        nc.gpsimd.tensor_tensor(p, p, rdenom[0:NQ, h:h + 1].broadcast_to([NQ, NK]), ALU.mult).then_inc(p_ready, 1)

            @block.vector
            def _(dve):
                dve.sem_inc(max_ready, FREE)
                dve.sem_inc(pT_dve, FREE)
                dve.sem_inc(x_done, FREE)
                link = Chain(dve, dve_own)
                for n in range(4):
                    for i in range(DC):
                        if n in (1, 2):
                            w = (wkT, wvT)[n - 1]
                            dve.wait_ge(whigh_ready, DC * (n - 1) + i + 1)
                            nc.vector.tensor_tensor(w[:, 1, i, :], wide[:, i, :], w[:, 0, i, :].bitcast(F32), ALU.subtract).then_inc(wT_ready, 1)
                        else:
                            dve.wait_ge(wT_mm, DC * n + i + 1)
                            nc.vector.tensor_copy((woT if n else wqT)[:, i, :], wide[:, i, :]).then_inc(wT_ready, 1)
                for b in range(NB):
                    last = nc.vector.bn_stats(stats[0:NQ, b, :], S.X[0:NQ, b, :])
                link(last)
                for b in range(NB):
                    last = nc.vector.bn_aggr(mean_var[0:NQ, b, :], stats[0:NQ, b, :])
                link(last)
                nc.vector.tensor_scalar(std[0:NQ, :], mean_var[0:NQ, :, 1], LN_EPS, None, ALU.add).then_inc(var_ready, 1)
                nc.vector.memset(tb[:], 0.0)
                for n in range(2):
                    nc.vector.memset(ctxT[:, n, :, NK:NKPAD].bitcast(F32), 0.0)
                    nc.vector.memset(KT[:, n, :, NK:NKPAD].bitcast(F32), 0.0)
                dve.wait_ge(small_in, 16 * NSMALL)
                link(nc.vector.tensor_scalar(bias_q[:], bias_q[:], scale, None, ALU.mult))
                dve.wait_ge(group_own, 3)
                if L1:
                    for j, f in enumerate((1.0 / (NQ * NK), 1.0 / NQ, 1.0 / NQ)):
                        nc.vector.tensor_scalar(w1_scaled[:, j, :], w1_all[:, :, j], f, None, ALU.mult)
                    nc.vector.tensor_copy(w3_all[:], w3_col[:].broadcast_to([DM, P]))
                dve.wait_ge(std_ready, 1)
                last = nc.vector.reciprocal(rstd[0:NQ, :], std[0:NQ, :])
                last.then_inc(pre_done, 1)
                dve.wait_ge(pre_done, 1)
                if L1:
                    dve.wait_ge(w2_mm, 1)
                    nc.vector.memset(w2T[:, DM:P], 0.0)
                    nc.vector.tensor_copy(w2T[:, 0:DM], mb[0:DM, 0:DM]).then_inc(pre_done, 1)

                link.enter()
                per = 1 + (3 + NH + 3 + 2 if L1 else 0)
                with dve.Fori(0, NB) as b:
                    link.loop(b, per)
                    dve.wait_ge(x_done, FREE + b)
                    nc.vector.tensor_scalar(xn[0:NQ, :].rearrange("p (a d) -> p a d", a=1), one(S.X[0:NQ], b), one(mean_var[0:NQ], b)[:, :, 0:1].rearrange("p a c -> p (a c)"),
                                            one(rstd[0:NQ], b), ALU.subtract, ALU.mult).then_inc(xn_ready, 1)
                    for g in range(NG):
                        if g == G_XN or g == G_Q:
                            dve.wait_ge(proj_mm, b * NG + g + 1)
                        else:
                            dve.wait_ge(high_done, b * (NG - 2) + (g + 1 if g < KC else g - 1))
                        bank = wide[:, g % 4, :]
                        if g < KC:
                            k = slice(g * P, g * P + sizes[g])
                            nc.vector.tensor_tensor(ctxT[:, 1, :, k], bank.rearrange("p (c k) -> p c k", c=DC)[:, :, 0:sizes[g]],
                                                    ctxT[:, 0, :, k].bitcast(F32), ALU.subtract).then_inc(proj_done, 1)
                        elif g == G_XN:
                            nc.vector.tensor_copy(xnT[:], bank.rearrange("p (c k) -> p c k", c=DC)[:, :, 0:NQ]).then_inc(proj_done, 1)
                        elif g == G_Q:
                            for o in range(DC):
                                last = nc.vector.tensor_scalar(QT[:, o, :], bank[:, o * P:o * P + NQ], scale, bias_q[:, o:o + 1],
                                                               ALU.mult, ALU.add)
                            last.then_inc(proj_done, 1)
                        else:
                            o, half = (g - G_K) // 2, g % 2
                            k = slice(half * KHALF, (half + 1) * KHALF)
                            nc.vector.scalar_tensor_tensor(out=KT[:, 1, o, k], in0=bank[:, 0:KHALF], scalar=bias_k[:, o:o + 1],
                                                           in1=KT[:, 0, o, k].bitcast(F32), op0=ALU.add, op1=ALU.subtract).then_inc(proj_done, 1)
                            if g == G_K + 1:
                                dve.wait_ge(qhigh_done, b + 1)
                                for r in range(HPC):
                                    last = nc.vector.scalar_tensor_tensor(out=Qm[:, 1, :, r, :], in0=QT[:], scalar=group[:, r:r + 1],
                                                                          in1=Qm[:, 0, :, r, :].bitcast(F32), op0=ALU.mult, op1=ALU.subtract)
                                last.then_inc(qm_ready, 1)

                    def values_out(j):
                        dve.wait_ge(v_mm, b * KC + j + 1)
                        nc.vector.tensor_copy(V[0:sizes[j], j, :], tb[0:sizes[j], j % 2, :]).then_inc(v_dve, 1)

                    def probsT_out(h):
                        dve.wait_ge(pT_mm1, FREE + b * NH + h + 1)
                        nc.vector.tensor_scalar(probsT[:, h % 2, 3:6, :], tb[:, 1, 0:3 * NQ].rearrange("p (j q) -> p j q", j=3),
                                                0.0, None, ALU.max).then_inc(pT_dve, 1)

                    def invert(h):
                        dve.wait_ge(exp_done, FREE + b * NH + h + 1)
                        nc.vector.reciprocal(rdenom[0:NQ, h:h + 1], denom[0:NQ, h:h + 1]).then_inc(rd_ready, 1)

                    if not L1:
                        for j in range(1, KC, 2):
                            values_out(j)
                        for h in range(NH + 2):
                            if h < NH:
                                dve.wait_ge(score_mm, b * NH + h + 1)
                                nc.vector.tensor_reduce(neg_max[0:NQ, h:h + 1].unsqueeze(2), wide[0:NQ, 2 * (h % 2):2 * (h % 2) + 2, 0:KHALF],
                                                        axis=mybir.AxisListType.XY, op=ALU.max, negate=True).then_inc(max_ready, 1)
                            if 1 <= h <= NH:
                                invert(h - 1)
                            if h >= 2:
                                probsT_out(h - 2)
                    else:
                        nc.vector.tensor_reduce(qsum[:], QT[:], axis=AX, op=ALU.add)
                        link(nc.vector.tensor_reduce(ksum1[:], ksum[:], axis=AX, op=ALU.add))
                        link(nc.vector.tensor_tensor(qk4[:], qsum[:], ksum1[:], ALU.mult))
                        link(nc.vector.tensor_tensor(qk_heads[:], qk4[:].unsqueeze(2).broadcast_to([P, DC, HPC]),
                                                     group[:].unsqueeze(1).broadcast_to([P, DC, HPC]), ALU.mult))
                        for h in range(NH):
                            dve.wait_ge(score_mm, b * NH + h + 1)
                            link(nc.vector.tensor_scalar(scores[0:NQ, h, :].rearrange("p (s k) -> p s k", s=2),
                                                         wide[0:NQ, 2 * (h % 2):2 * (h % 2) + 2, 0:KHALF], 0.0, -3.0e38,
                                                         ALU.add, ALU.max, accum_out=maxs[0:NQ, h:h + 1]))
                            nc.vector.tensor_scalar(neg_max[0:NQ, h:h + 1], maxs[0:NQ, h:h + 1], -1.0, None, ALU.mult).then_inc(max_ready, 1)
                            if h % 4 == 3 and h // 2 < KC:
                                values_out(h // 2)
                        dve.wait_ge(first_exp, b + 1)
                        link(nc.vector.reciprocal(denom1[0:NQ, :], denom1[0:NQ, :]))
                        link(nc.vector.tensor_tensor(sqsum[0:NQ, :], sqsum[0:NQ, :], denom1[0:NQ, :], ALU.mult))
                        link(nc.vector.tensor_tensor(sqsum[0:NQ, :], sqsum[0:NQ, :], denom1[0:NQ, :], ALU.mult))
                        nc.vector.tensor_scalar(varr[0:NQ, :], sqsum[0:NQ, :], -1.0 / NK, 1.0 / (NK - 1), ALU.add, ALU.mult).then_inc(stat_ready, 1)
                        dve.wait_ge(t_mm, b + 1)
                        link(nc.vector.tensor_scalar(log_t[0:NQ, :], mb[0:NQ, 0:NH], b3_all[0:NQ, :], LOG_T_MIN, ALU.add, ALU.max))
                        nc.vector.tensor_scalar(log_t[0:NQ, :], log_t[0:NQ, :], LOG_T_MAX, None, ALU.min).then_inc(clip_ready, 1)
                        dve.wait_ge(inv_ready, b + 1)
                        link(nc.vector.tensor_scalar(ratio[0:NQ, :], inv_t[0:NQ, :], 0.5 * float(DH) ** 0.5, None, ALU.mult))
                        nc.vector.tensor_tensor(bias2[0:NQ, :], neg_max[0:NQ, :], ratio[0:NQ, :], ALU.mult).then_inc(ratio_ready, 1)
                        for h in range(NH + 2):
                            if h < NH:
                                invert(h)
                            if h >= 2:
                                probsT_out(h - 2)

                    dve.wait_ge(pv_mm, b + 1)
                    nc.vector.tensor_tensor(OT[:], ob[:, 0:DC * NQ].rearrange("p (c q) -> p c q", c=DC),
                                            bias_v[:].unsqueeze(2).broadcast_to([P, DC, NQ]), ALU.add).then_inc(ot_ready, 1)
                    dve.wait_ge(y_mm, b + 1)
                    link(nc.vector.tensor_tensor(y[0:NQ, :], ob[0:NQ, :], bias_o[0:NQ, :], ALU.add))
                    xb = one(S.X[0:NQ], b)
                    nc.vector.scalar_tensor_tensor(out=xb, in0=y[0:NQ, :].unsqueeze(1), scalar=S.tanh_g[0:NQ, layer:layer + 1], in1=xb,
                                                   op0=ALU.mult, op1=ALU.add).then_inc(x_done, 1)
                link.leave(NB, per)


class State:
    pass


def start_state(nc, ctx):
    S = State()
    m = Mem(nc, ctx, "all")
    S.X = m.sb("x", [P, NB, D])
    S.ident = m.sb("ident", [P, P])
    S.identb = m.sb("identb", [P, P], BF16)
    S.ones = m.sb("ones", [P, P])
    S.tanh_g = m.sb("tanh_g", [P, 4])
    return S


def quantised_stage(nc, S, w_gate, w_up, w_down):
    with ExitStack() as ctx:
        m = Mem(nc, ctx, "ffn0")
        sb, ps, sem = m.sb, m.ps, m.sem
        RB = INNER // P
        PIECE = 4 * D
        w_f = [sb(f"w_{n}", [P, RB * D]) for n in ("even", "odd")]
        w_f.append(w_f[0])
        tern = sb("tern", [P, 2, RB * D], BF16)
        gateT = sb("gateT", [P, DC, INNER], BF16)
        upT = sb("upT", [P, DC, INNER], BF16)
        downT = sb("downT", [P, RB, D], BF16)
        junk = sb("junk", [P, PIECE])
        abs_part, abs_sum = sb("abs_part", [P, 3, 4]), sb("abs_sum", [P, 3])
        w_step, w_scale = sb("w_step", [P, 3]), sb("w_scale", [P, 3])
        stats, mean_var = sb("stats", [P, NB, 6]), sb("mean_var", [P, NB, 2])
        std, rstd = sb("std", [P, NB]), sb("rstd", [P, NB])
        xn, xq = sb("xn", [P, D]), sb("xq", [P, D], BF16)
        xqT = sb("xqT", [P, DC, NQ], BF16)
        x_max, x_step, x_scale = sb("x_max", [P, 1]), sb("x_step", [P, 1]), sb("x_scale", [P, 1])
        gu_step = sb("gu_step", [P, 2])
        sg, hid = sb("sg", [P, 2, BANK]), sb("hid", [P, INNER])
        hq = sb("hq", [P, INNER], BF16)
        hqT = sb("hqT", [P, RB, NQ], BF16)
        h_max, h_step, h_scale, y_step = (sb(n, [P, 1]) for n in ("h_max", "h_step", "h_scale", "y_step"))

        tbank = [ps(f"tbank{i}", [P, 2 * BANK], BF16) for i in range(2)]
        gu = ps("gu", [P, 4, BANK])
        ob = ps("ob", [P, BANK])
        mb = ps("mb", [P, BANK])

        w_in = [sem(f"w_in{i}") for i in range(3)]
        (abs_done, part_sum, sum_mm, tern_ready, wT_mm, wT_act, wT_dve, dve_own, var_ready, std_ready) = (sem(n) for n in (
            "abs_done", "part_sum", "sum_mm", "tern_ready", "wT_mm", "wT_act", "wT_dve", "dve_own", "var_ready", "std_ready"))
        (xq_ready, xqT_mm, xqT_ready, gu_mm, silu_done, h_part, hq_ready, hqT_mm, hqT_act, hqT_dve, y_mm, x_done, step_ready) = (sem(n) for n in (
            "xq_ready", "xqT_mm", "xqT_ready", "gu_mm", "silu_done", "h_part", "hq_ready", "hqT_mm", "hqT_act", "hqT_dve", "y_mm",
            "x_done", "step_ready"))
        NT = RB * D // (2 * BANK)
        NPC = INNER // BANK

        def matrix_part(n, k):
            if n < 2:
                return (gateT, upT)[n][:, k // 2, (k % 2) * 2 * BANK:(k % 2 + 1) * 2 * BANK]
            return downT[:, 2 * k:2 * k + 2, :].rearrange("p k n -> p (k n)")

        with nc.Block() as block:

            @block.sync
            def _(sp):
                sp.dma_start(w_f[0][:].rearrange("p (o i) -> p o i", i=D), w_gate.rearrange("(o p) i -> p o i", p=P)).then_inc(w_in[0], 16)
                sp.dma_start(w_f[1][:].rearrange("p (o i) -> p o i", i=D), w_up.rearrange("(o p) i -> p o i", p=P)).then_inc(w_in[1], 16)
                sp.wait_ge(tern_ready, 4)
                sp.dma_start(w_f[2][:].rearrange("p (o i) -> p o i", i=INNER), w_down.rearrange("(o p) i -> p o i", p=P)).then_inc(w_in[2], 16)

            @block.tensor
            def _(pe):
                for n in range(3):
                    pe.wait_ge(part_sum, n + 1)
                    nc.tensor.matmul(mb[:, n:n + 1], S.ones[:], abs_sum[:, n:n + 1], start=True, stop=True).then_inc(sum_mm, 1)
                    pe.wait_ge(tern_ready, 4 * (n + 1))
                    for k in range(NT):
                        count = NT * n + k
                        if count >= 2:
                            pe.wait_ge(wT_act if k % 2 == 0 else wT_dve, count // 2)
                        for t in range(8):
                            if n < 2:
                                row, col = 8 * (k % 2) + t, k // 2
                                src = tern[:, n % 2, row * D + col * P:row * D + (col + 1) * P]
                            else:
                                row, col = t % 4, 2 * k + t // 4
                                src = tern[:, n % 2, row * INNER + col * P:row * INNER + (col + 1) * P]
                            last = nc.tensor.transpose(tbank[k % 2][:, t * P:(t + 1) * P], src, S.identb[:])
                        last.then_inc(wT_mm, 1)
                pe.wait_ge(wT_act, 3 * NT // 2)
                pe.wait_ge(wT_dve, 3 * NT // 2)

                with pe.Fori(0, NB) as b:
                    pe.wait_ge(xq_ready, b + 1)
                    pe.wait_ge(hqT_act, FREE + b)
                    for c in range(DC):
                        last = nc.tensor.transpose(tbank[0][:, c * P:c * P + NQ], xq[0:NQ, c * P:(c + 1) * P], S.identb[0:NQ, 0:NQ])
                    last.then_inc(xqT_mm, 1)
                    pe.wait_ge(xqT_ready, b + 1)
                    for n in range(NPC):
                        if n < 2:
                            pe.wait_ge(h_part, FREE + b * NPC)
                        else:
                            pe.wait_ge(h_part, FREE + b * NPC + n - 1)
                        for k, wT in enumerate((gateT, upT)):
                            for c in range(DC):
                                last = nc.tensor.matmul(gu[0:NQ, 2 * (n % 2) + k, :], xqT[:, c, :], wT[:, c, n * BANK:(n + 1) * BANK],
                                                        start=(c == 0), stop=(c == DC - 1))
                        last.then_inc(gu_mm, 1)
                    pe.wait_ge(hq_ready, b + 1)
                    for half in range(2):
                        if half == 1:
                            pe.wait_ge(hqT_dve, FREE + b)
                        for t in range(8):
                            last = nc.tensor.transpose(tbank[half][:, t * NQ:(t + 1) * NQ],
                                                       hq[0:NQ, (8 * half + t) * P:(8 * half + t + 1) * P], S.identb[0:NQ, 0:NQ])
                        last.then_inc(hqT_mm, 1)
                    pe.wait_ge(x_done, FREE + b)
                    pe.wait_ge(hqT_act, FREE + b + 1)
                    pe.wait_ge(hqT_dve, FREE + b + 1)
                    for k in range(RB):
                        last = nc.tensor.matmul(ob[0:NQ, :], hqT[:, k, :], downT[:, k, :], start=(k == 0), stop=(k == RB - 1))
                    last.then_inc(y_mm, 1)

            @block.scalar
            def _(act):
                act.sem_inc(hqT_act, FREE)
                def weights_out(n, k):
                    act.wait_ge(wT_mm, NT * n + k + 1)
                    nc.scalar.copy(matrix_part(n, k), tbank[k % 2][:]).then_inc(wT_act, 1)

                for n in range(3):
                    act.wait_ge(w_in[n], 16)
                    for k in range(4):
                        if 4 * n + k >= 1:
                            act.wait_ge(abs_done, 4 * n + k)
                        nc.scalar.activation(junk[:], w_f[n][:, k * PIECE:(k + 1) * PIECE], ACT.Abs,
                                             accum_out=abs_part[:, n, k:k + 1]).then_inc(abs_done, 1)
                    if n >= 1:
                        for k in range(0, NT, 2):
                            weights_out(n - 1, k)
                for k in range(0, NT, 2):
                    weights_out(2, k)
                act.wait_ge(var_ready, 1)
                nc.scalar.activation(std[0:NQ, :], std[0:NQ, :], ACT.Sqrt).then_inc(std_ready, 1)

                with act.Fori(0, NB) as b:
                    act.wait_ge(xqT_mm, b + 1)
                    nc.scalar.copy(xqT[:], tbank[0][:, 0:DC * P].rearrange("p (c k) -> p c k", c=DC)[:, :, 0:NQ]).then_inc(xqT_ready, 1)
                    act.wait_ge(step_ready, b + 1)
                    for n in range(NPC):
                        act.wait_ge(gu_mm, b * NPC + n + 1)
                        if n >= 2:
                            act.wait_ge(h_part, FREE + b * NPC + n - 1)
                        nc.scalar.activation(sg[0:NQ, n % 2, :], gu[0:NQ, 2 * (n % 2), :], ACT.Silu, scale=gu_step[0:NQ, 0:1]).then_inc(silu_done, 1)
                    act.wait_ge(hqT_mm, 2 * b + 1)
                    nc.scalar.copy(hqT[:, 0:8, :], tbank[0][:, 0:8 * NQ].rearrange("p (k q) -> p k q", k=8)).then_inc(hqT_act, 1)

            @block.vector
            def _(dve):
                dve.sem_inc(hqT_dve, FREE)
                dve.sem_inc(x_done, FREE)
                dve.sem_inc(h_part, FREE)
                link = Chain(dve, dve_own)

                def weights_out(n, k):
                    dve.wait_ge(wT_mm, NT * n + k + 1)
                    nc.vector.tensor_copy(matrix_part(n, k), tbank[k % 2][:]).then_inc(wT_dve, 1)

                for n in range(3):
                    dve.wait_ge(abs_done, 4 * (n + 1))
                    nc.vector.tensor_reduce(abs_sum[:, n:n + 1], abs_part[:, n, :], axis=AX, op=ALU.add).then_inc(part_sum, 1)
                    dve.wait_ge(sum_mm, n + 1)
                    link(nc.vector.tensor_scalar(w_step[:, n:n + 1], mb[:, n:n + 1], 1.0 / (INNER * D), 1e-5, ALU.mult, ALU.max))
                    link(nc.vector.reciprocal(w_scale[:, n:n + 1], w_step[:, n:n + 1]))
                    for k in range(4):
                        r = w_f[n][:, k * PIECE:(k + 1) * PIECE]
                        link(nc.vector.tensor_scalar(r, r, w_scale[:, n:n + 1], 1.0, ALU.mult, ALU.min))
                        link(nc.vector.tensor_scalar(r, r, -1.0, ROUND, ALU.max, ALU.add))
                        if n >= 2 and k == 0:
                            dve.wait_ge(wT_mm, NT * (n - 1))
                        nc.vector.tensor_scalar(tern[:, n % 2, k * PIECE:(k + 1) * PIECE], r, -ROUND, None, ALU.add).then_inc(tern_ready, 1)
                        dve.wait_ge(tern_ready, 4 * n + k + 1)
                    for k in range(1, NT, 2):
                        weights_out(n, k)
                for b in range(NB):
                    last = nc.vector.bn_stats(stats[0:NQ, b, :], S.X[0:NQ, b, :])
                link(last)
                for b in range(NB):
                    last = nc.vector.bn_aggr(mean_var[0:NQ, b, :], stats[0:NQ, b, :])
                link(last)
                nc.vector.tensor_scalar(std[0:NQ, :], mean_var[0:NQ, :, 1], LN_EPS, None, ALU.add).then_inc(var_ready, 1)
                dve.wait_ge(std_ready, 1)
                link(nc.vector.reciprocal(rstd[0:NQ, :], std[0:NQ, :]))

                def quantise(out, src, top, step, recip):
                    link(nc.vector.tensor_reduce(top, src, axis=AX, op=ALU.max, apply_absolute_value=True))
                    link(nc.vector.tensor_scalar(step, top, 1e-5, 1.0 / QMAX, ALU.max, ALU.mult))
                    link(nc.vector.reciprocal(recip, step))
                    link(nc.vector.tensor_scalar(src, src, recip, QMAX, ALU.mult, ALU.min))
                    link(nc.vector.tensor_scalar(src, src, -QMAX - 1.0, ROUND, ALU.max, ALU.add))
                    return nc.vector.tensor_scalar(out, src, -ROUND, None, ALU.add)

                link.enter()
                per = 12
                with dve.Fori(0, NB) as b:
                    link.loop(b, per)
                    link(nc.vector.tensor_scalar(xn[0:NQ, :].unsqueeze(1), one(S.X[0:NQ], b),
                                                 one(mean_var[0:NQ], b)[:, :, 0:1].rearrange("p a c -> p (a c)"),
                                                 one(rstd[0:NQ], b), ALU.subtract, ALU.mult))
                    quantise(xq[0:NQ, :], xn[0:NQ, :], x_max[0:NQ, :], x_step[0:NQ, :], x_scale[0:NQ, :]).then_inc(xq_ready, 1)
                    nc.vector.tensor_scalar(gu_step[0:NQ, :], w_step[0:NQ, 0:2], x_step[0:NQ, :], None, ALU.mult).then_inc(step_ready, 1)
                    dve.wait_ge(step_ready, b + 1)
                    for n in range(NPC):
                        dve.wait_ge(silu_done, b * NPC + n + 1)
                        nc.vector.scalar_tensor_tensor(out=hid[0:NQ, n * BANK:(n + 1) * BANK], in0=gu[0:NQ, 2 * (n % 2) + 1, :],
                                                       scalar=gu_step[0:NQ, 1:2], in1=sg[0:NQ, n % 2, :], op0=ALU.mult, op1=ALU.mult).then_inc(h_part, 1)
                    dve.wait_ge(h_part, FREE + b * NPC + NPC)
                    quantise(hq[0:NQ, :], hid[0:NQ, :], h_max[0:NQ, :], h_step[0:NQ, :], h_scale[0:NQ, :]).then_inc(hq_ready, 1)
                    link(nc.vector.tensor_scalar(y_step[0:NQ, :], h_step[0:NQ, :], w_step[0:NQ, 2:3], S.tanh_g[0:NQ, 2:3], ALU.mult, ALU.mult))
                    dve.wait_ge(hqT_mm, 2 * b + 2)
                    nc.vector.tensor_copy(hqT[:, 8:16, :], tbank[1][:, 0:8 * NQ].rearrange("p (k q) -> p k q", k=8)).then_inc(hqT_dve, 1)
                    dve.wait_ge(y_mm, b + 1)
                    xb = one(S.X[0:NQ], b)
                    nc.vector.scalar_tensor_tensor(out=xb, in0=ob[0:NQ, :].unsqueeze(1), scalar=y_step[0:NQ, :], in1=xb,
                                                   op0=ALU.mult, op1=ALU.add).then_inc(x_done, 1)
                link.leave(NB, per)


def mixture_stages(nc, S, gate_w, w_gate, w_up, w_down, out):
    with ExitStack() as ctx:
        m = Mem(nc, ctx, "moe")
        xinT = m.sb("xinT", [P, DC, NE, NB, CAP])
        scatter = m.sb("scatter", [2 * HALF, NB, 2, NQ])
        routing_stage(nc, S, gate_w, xinT, scatter)
        yT = m.sb("yT", [P, DC, NB, NE, CAP])
        experts_stage(nc, S, w_gate, w_up, w_down, xinT, yT)
        combine_stage(nc, S, scatter, yT, out)


HALF = NE // 2 * CAP // 2


def routing_stage(nc, S, gate_w, xinT, scatter):
    PAIRS = NB * NE
    with ExitStack() as ctx:
        m = Mem(nc, ctx, "route")
        sb, ps, sem = m.sb, m.ps, m.sem
        gw, gwT = sb("gw", [NE, D]), sb("gwT", [P, DC, NE])
        stats, mean_var = sb("stats", [P, NB, 6]), sb("mean_var", [P, NB, 2])
        std, rstd = sb("std", [P, NB]), sb("rstd", [P, NB])
        xs = sb("xs", [P, D])
        xT = sb("xT", [P, DC, NQ])
        logits = sb("logits", [P, NB, NE])
        top, total = sb("top", [P, NB]), sb("total", [P, NB])
        aff = sb("aff", [P, PAIRS])
        affT, work = sb("affT", [PAIRS, NQ]), sb("work", [PAIRS, NQ])
        best = sb("best", [PAIRS, 3, 8])
        maskT = sb("maskT", [PAIRS, NQ])
        mask, rank = sb("mask", [P, PAIRS]), sb("rank", [P, PAIRS])
        upto = sb("upto", [P, NQ])
        slot = sb("slot", [P, CAP])
        onehot = sb("onehot", [P, NB, NE * CAP])
        gated = sb("gated", [P, NB, NE * CAP])
        hot_b, gated_b = sb("hot_b", [P, NE * CAP]), sb("gated_b", [P, NE * CAP])
        tb, lb, rb, gb = (ps(n, [P, BANK]) for n in ("tb", "lb", "rb", "gb"))
        xb_ps = ps("xb_ps", [P, 2, BANK])
        (gw_in, gwT_mm, gwT_ready, xs_ready, xT_mm, xT_ready, logit_mm, logit_out, sub_done, exp_done, aff_ready, affT_mm,
         mask_ready, mask_mm, mask_out, rank_mm, hot_ready, batch_ready, gather_mm, gather_out, gatedT_mm, gatedT_out, dve_own,
         pool_own, var_ready, std_ready) = (sem(n) for n in (
             "gw_in", "gwT_mm", "gwT_ready", "xs_ready", "xT_mm", "xT_ready", "logit_mm", "logit_out", "sub_done", "exp_done",
             "aff_ready", "affT_mm", "mask_ready", "mask_mm", "mask_out", "rank_mm", "hot_ready", "batch_ready", "gather_mm",
             "gather_out", "gatedT_mm", "gatedT_out", "dve_own", "pool_own", "var_ready", "std_ready"))

        with nc.Block() as block:

            @block.sync
            def _(sp):
                sp.dma_start(gw[:], gate_w).then_inc(gw_in, 16)

            @block.gpsimd
            def _(pool):
                nc.gpsimd.memset(upto[:], 1.0).then_inc(pool_own, 1)
                pool.wait_ge(pool_own, 1)
                nc.gpsimd.affine_select(out=upto[:], in_=upto[:], compare_op=ALU.is_ge, fill=0.0, base=0,
                                        pattern=[[1, NQ]], channel_multiplier=-1).then_inc(pool_own, 1)
                nc.gpsimd.iota(slot[:], [[1, CAP]], base=1, channel_multiplier=0,
                               allow_small_or_imprecise_dtypes=True).then_inc(pool_own, 1)

            @block.tensor
            def _(pe):
                pe.sem_inc(gatedT_mm, FREE)
                pe.wait_ge(gw_in, 16)
                for c in range(DC):
                    last = nc.tensor.transpose(tb[:, c * NE:(c + 1) * NE], gw[:, c * P:(c + 1) * P], S.ident[0:NE, 0:NE])
                last.then_inc(gwT_mm, 1)
                pe.wait_ge(gwT_ready, 1)
                with pe.Fori(0, NB) as b:
                    pe.wait_ge(xs_ready, b + 1)
                    for c in range(DC):
                        last = nc.tensor.transpose(tb[:, c * NQ:(c + 1) * NQ], xs[0:NQ, c * P:(c + 1) * P], S.ident[0:NQ, 0:NQ])
                    last.then_inc(xT_mm, 1)
                    pe.wait_ge(xT_ready, b + 1)
                    pe.wait_ge(logit_out, FREE + b)
                    for c in range(DC):
                        last = nc.tensor.matmul(lb[0:NQ, 0:NE], xT[:, c, :], gwT[:, c, :], start=(c == 0), stop=(c == DC - 1))
                    last.then_inc(logit_mm, 1)
                pe.wait_ge(aff_ready, 1)
                nc.tensor.transpose(rb[0:PAIRS, 0:NQ], aff[0:NQ, :], S.ident[0:NQ, 0:NQ]).then_inc(affT_mm, 1)
                pe.wait_ge(mask_ready, 1)
                nc.tensor.transpose(lb[0:NQ, 0:PAIRS], maskT[:], S.ident[0:PAIRS, 0:PAIRS]).then_inc(mask_mm, 1)
                pe.wait_ge(mask_out, 1)
                pe.wait_ge(pool_own, 3)
                nc.tensor.matmul(rb[0:NQ, 0:PAIRS], upto[0:NQ, :], mask[0:NQ, :], start=True, stop=True).then_inc(rank_mm, 1)
                with pe.Fori(0, NB) as b:
                    pe.wait_ge(batch_ready, b + 1)
                    pe.wait_ge(gather_out, FREE + b)
                    for c in range(DC):
                        last = nc.tensor.matmul(xb_ps[:, c // 2, (c % 2) * NE * CAP:(c % 2 + 1) * NE * CAP], xs[0:NQ, c * P:(c + 1) * P],
                                                hot_b[0:NQ, :], start=True, stop=True)
                    last.then_inc(gather_mm, 1)
                    pe.wait_ge(gatedT_out, FREE + b)
                    for h in range(2):
                        last = nc.tensor.transpose(gb[0:2 * HALF, h * NQ:(h + 1) * NQ], gated_b[0:NQ, h * 2 * HALF:(h + 1) * 2 * HALF],
                                                   S.ident[0:NQ, 0:NQ])
                    last.then_inc(gatedT_mm, 1)

            @block.scalar
            def _(act):
                act.sem_inc(gatedT_out, FREE)
                act.wait_ge(var_ready, 1)
                nc.scalar.activation(std[0:NQ, :], std[0:NQ, :], ACT.Sqrt).then_inc(std_ready, 1)
                with act.Fori(0, NB) as b:
                    act.wait_ge(xT_mm, b + 1)
                    nc.scalar.copy(xT[:], tb[:, 0:DC * NQ].rearrange("p (c q) -> p c q", c=DC)).then_inc(xT_ready, 1)
                act.wait_ge(sub_done, 1)
                nc.scalar.activation(logits[0:NQ], logits[0:NQ], ACT.Exp).then_inc(exp_done, 1)
                with act.Fori(0, NB) as b:
                    act.wait_ge(gatedT_mm, FREE + b + 1)
                    nc.scalar.copy(one(scatter[:], b), gb[0:2 * HALF, 0:2 * NQ].rearrange("p (a h q) -> p a h q", a=1, h=2)).then_inc(gatedT_out, 1)

            @block.vector
            def _(dve):
                dve.sem_inc(logit_out, FREE)
                dve.sem_inc(gather_out, FREE)
                link = Chain(dve, dve_own)
                dve.wait_ge(gwT_mm, 1)
                nc.vector.tensor_copy(gwT[:], tb[:, 0:DC * NE].rearrange("p (c e) -> p c e", c=DC)).then_inc(gwT_ready, 1)
                for b in range(NB):
                    last = nc.vector.bn_stats(stats[0:NQ, b, :], S.X[0:NQ, b, :])
                link(last)
                for b in range(NB):
                    last = nc.vector.bn_aggr(mean_var[0:NQ, b, :], stats[0:NQ, b, :])
                link(last)
                nc.vector.tensor_scalar(std[0:NQ, :], mean_var[0:NQ, :, 1], LN_EPS, None, ALU.add).then_inc(var_ready, 1)
                dve.wait_ge(std_ready, 1)
                link(nc.vector.reciprocal(rstd[0:NQ, :], std[0:NQ, :]))

                def normalise(b):
                    return nc.vector.tensor_scalar(xs[0:NQ, :].unsqueeze(1), one(S.X[0:NQ], b),
                                                   one(mean_var[0:NQ], b)[:, :, 0:1].rearrange("p a c -> p (a c)"),
                                                   one(rstd[0:NQ], b), ALU.subtract, ALU.mult)

                with dve.Fori(0, NB) as b:
                    normalise(b).then_inc(xs_ready, 1)
                    dve.wait_ge(logit_mm, b + 1)
                    nc.vector.tensor_copy(one(logits[0:NQ], b), lb[0:NQ, 0:NE].unsqueeze(1)).then_inc(logit_out, 1)
                dve.wait_ge(logit_out, FREE + NB)
                link(nc.vector.tensor_reduce(top[0:NQ, :], logits[0:NQ], axis=AX, op=ALU.max))
                nc.vector.tensor_tensor(logits[0:NQ], logits[0:NQ], top[0:NQ, :].unsqueeze(2).broadcast_to([NQ, NB, NE]),
                                        ALU.subtract).then_inc(sub_done, 1)
                dve.wait_ge(exp_done, 1)
                link(nc.vector.tensor_reduce(total[0:NQ, :], logits[0:NQ], axis=AX, op=ALU.add))
                link(nc.vector.reciprocal(total[0:NQ, :], total[0:NQ, :]))
                nc.vector.tensor_tensor(aff[0:NQ, :].rearrange("p (b e) -> p b e", b=NB), logits[0:NQ],
                                        total[0:NQ, :].unsqueeze(2).broadcast_to([NQ, NB, NE]), ALU.mult).then_inc(aff_ready, 1)
                dve.wait_ge(affT_mm, 1)
                nc.vector.tensor_copy(affT[:], rb[0:PAIRS, 0:NQ])
                link(nc.vector.tensor_copy(work[:], rb[0:PAIRS, 0:NQ]))
                for k in range(CAP // 8):
                    link(nc.vector.max(best[:, k, :], work[:]))
                    link(nc.vector.match_replace(work[:], best[:, k, :], work[:], -1.0))
                nc.vector.tensor_scalar(maskT[:], work[:], 0.0, None, ALU.is_lt).then_inc(mask_ready, 1)
                dve.wait_ge(mask_mm, 1)
                nc.vector.tensor_copy(mask[0:NQ, :], lb[0:NQ, 0:PAIRS]).then_inc(mask_out, 1)
                dve.wait_ge(rank_mm, 1)
                dve.wait_ge(mask_out, 1)
                link(nc.vector.tensor_tensor(rank[0:NQ, :], rb[0:NQ, 0:PAIRS], mask[0:NQ, :], ALU.mult))
                hot = onehot[0:NQ].rearrange("p b (e s) -> p (b e) s", e=NE)
                link(nc.vector.tensor_tensor(hot, rank[0:NQ, :].unsqueeze(2).broadcast_to([NQ, PAIRS, CAP]),
                                             slot[0:NQ, :].unsqueeze(1).broadcast_to([NQ, PAIRS, CAP]), ALU.is_equal))
                link(nc.vector.tensor_tensor(gated[0:NQ].rearrange("p b (e s) -> p (b e) s", e=NE), hot,
                                             aff[0:NQ, :].unsqueeze(2).broadcast_to([NQ, PAIRS, CAP]), ALU.mult))
                with dve.Fori(0, NB) as b:
                    dve.wait_ge(gatedT_mm, FREE + b)
                    normalise(b)
                    nc.vector.tensor_copy(hot_b[0:NQ, :].unsqueeze(1), one(onehot[0:NQ], b))
                    nc.vector.tensor_copy(gated_b[0:NQ, :].unsqueeze(1), one(gated[0:NQ], b)).then_inc(batch_ready, 1)
                    dve.wait_ge(gather_mm, b + 1)
                    for c in range(DC):
                        last = nc.vector.tensor_copy(xinT[:, c, :, bass.ds(b, 1), :],
                                                     xb_ps[:, c // 2, (c % 2) * NE * CAP:(c % 2 + 1) * NE * CAP].rearrange(
                                                         "p (e a s) -> p e a s", e=NE, a=1))
                    last.then_inc(gather_out, 1)


def experts_stage(nc, S, w_gate, w_up, w_down, xinT, yT):
    IB = INNER // P
    LOAD = 4
    NL = 3 * IB // LOAD
    NSLOT = 6
    NU = IB + IB // 2
    NGRP = 2 * NU
    with ExitStack() as ctx:
        m = Mem(nc, ctx, "exp")
        sb, ps, sem = m.sb, m.ps, m.sem
        w_nat = sb("w_nat", [P, NSLOT, LOAD * D])
        wT = sb("wT", [P, 4, BANK])
        xe = sb("xe", [P, DC, SLOTS])
        sg = sb("sg", [P, 2, SLOTS])
        hT = sb("hT", [P, IB, SLOTS])
        tb = ps("tb", [P, 4, BANK])
        hb = ps("hb", [P, 2, BANK])
        yb = ps("yb", [P, 2, BANK])
        w_in = [sem(f"w_in{i}") for i in range(NSLOT)]
        (xe_ready, t_mm, wT_act, wT_dve, h_mm, silu_done, h_ready, y_mm, y_out) = (sem(n) for n in (
            "xe_ready", "t_mm", "wT_act", "wT_dve", "h_mm", "silu_done", "h_ready", "y_mm", "y_out"))

        def load_source(e, n):
            if n < 2 * IB // LOAD:
                w = (w_gate, w_up)[n % 2]
                return w[bass.ds(e, 1)].rearrange("a (o p) i -> p (a o) i", p=P)[:, (n // 2) * LOAD:(n // 2 + 1) * LOAD, :]
            return down_source(e * DC + n - 2 * IB // LOAD)

        def down_source(row):
            return w_down.rearrange("e (o p) i -> p (e o) i", p=P)[:, bass.ds(row, 1), :]

        def group_load(g):
            if g < 2 * IB:
                return 2 * (g // 2 // LOAD) + g % 2
            return 2 * IB // LOAD + (g - 2 * IB) // 4

        def last_group(n):
            return max(g for g in range(NGRP) if group_load(g) == n)

        with nc.Block() as block:

            @block.sync
            def _(sp):
                def load(e, n, row=None):
                    k = LOAD if n < 2 * IB // LOAD else 1
                    src = load_source(e, n) if row is None else down_source(row)
                    sp.dma_start(w_nat[:, n % NSLOT].rearrange("p (o i) -> p o i", o=k), src).then_inc(w_in[n % NSLOT], 16)

                for n in range(NSLOT):
                    load(0, n)
                with sp.Fori(0, NE - 1) as e:
                    down_rows = [sp.snap(e * DC + d) for d in range(DC)]
                    for n in range(NSLOT, NL + NSLOT):
                        sp.wait_ge(t_mm, e * NGRP + last_group(n - NSLOT) + 1)
                        if 2 * IB // LOAD <= n < NL:
                            load(e, n, down_rows[n - 2 * IB // LOAD])
                        elif n < NL:
                            load(e, n)
                        else:
                            load(e + 1, n - NL)
                for n in range(NSLOT, NL):
                    sp.wait_ge(t_mm, (NE - 1) * NGRP + last_group(n - NSLOT) + 1)
                    load(NE - 1, n)

            @block.tensor
            def _(pe):
                pe.sem_inc(h_mm, FREE)
                with pe.Fori(0, NE) as e:
                    def transposes(u):
                        for g in (2 * u, 2 * u + 1):
                            n = group_load(g)
                            pe.wait_ge(w_in[n % NSLOT], e * (16 * (NL // NSLOT)) + 16 * (n // NSLOT + 1))
                            done, per = (wT_act if g % 2 == 0 else wT_dve), NGRP // 2
                            pe.wait_ge(done, FREE + e * per + ((g - 4) // 2 + 1 if g >= 4 else 0))
                            for t in range(4):
                                if g < 2 * IB:
                                    at = (u % LOAD) * D + t * P
                                else:
                                    at = ((g - 2 * IB) % 4) * 4 * P + t * P
                                last = nc.tensor.transpose(tb[:, g % 4, t * P:(t + 1) * P], w_nat[:, n % NSLOT, at:at + P], S.ident[:])
                            last.then_inc(t_mm, 1)

                    def products(u):
                        pe.wait_ge(wT_act, FREE + e * (NGRP // 2) + u + 1)
                        if u < IB:
                            if u == 0:
                                pe.wait_ge(xe_ready, e + 1)
                            pe.wait_ge(h_ready, FREE + e * IB + max(u - 1, 0))
                            for k in range(2):
                                if k == 1:
                                    pe.wait_ge(wT_dve, FREE + e * (NGRP // 2) + u + 1)
                                for c in range(DC):
                                    last = nc.tensor.matmul(hb[:, u % 2, k * SLOTS:(k + 1) * SLOTS], wT[:, (2 * u + k) % 4, c * P:(c + 1) * P],
                                                            xe[:, c, :], start=(c == 0), stop=(c == DC - 1))
                            last.then_inc(h_mm, 1)
                        else:
                            d, part = (u - IB) // 2, (u - IB) % 2
                            if part == 0:
                                pe.wait_ge(h_ready, FREE + e * IB + IB)
                                pe.wait_ge(y_out, FREE + e * DC + max(d - 1, 0))
                            for k in range(2):
                                if k == 1:
                                    pe.wait_ge(wT_dve, FREE + e * (NGRP // 2) + u + 1)
                                for t in range(4):
                                    i = 8 * part + 4 * k + t
                                    last = nc.tensor.matmul(yb[:, d % 2, 0:SLOTS], wT[:, (2 * u + k) % 4, t * P:(t + 1) * P], hT[:, i, :],
                                                            start=(i == 0), stop=(i == IB - 1))
                            if part == 1:
                                last.then_inc(y_mm, 1)

                    transposes(0)
                    for u in range(NU):
                        if u + 1 < NU:
                            transposes(u + 1)
                        products(u)

            def weights_out(eng, copy, e, g, done):
                eng.wait_ge(t_mm, e * NGRP + g + 1)
                copy(wT[:, g % 4, :], tb[:, g % 4, :]).then_inc(done, 1)

            @block.scalar
            def _(act):
                act.sem_inc(wT_act, FREE)
                with act.Fori(0, NE) as e:
                    for u in range(NU + 1):
                        if u < NU:
                            weights_out(act, nc.scalar.copy, e, 2 * u, wT_act)
                        if 1 <= u <= IB:
                            k = u - 1
                            act.wait_ge(h_mm, FREE + e * IB + k + 1)
                            act.wait_ge(h_ready, FREE + e * IB + max(k - 1, 0))
                            nc.scalar.activation(sg[:, k % 2, :], hb[:, k % 2, 0:SLOTS], ACT.Silu).then_inc(silu_done, 1)

            @block.vector
            def _(dve):
                dve.sem_inc(wT_dve, FREE)
                dve.sem_inc(h_ready, FREE)
                dve.sem_inc(y_out, FREE)
                def take_tokens(e):
                    nc.vector.tensor_copy(xe[:].rearrange("p c (a n) -> p c a n", a=1),
                                          xinT[:, :, bass.ds(e, 1)].rearrange("p c a b s -> p c a (b s)")).then_inc(xe_ready, 1)

                with dve.Fori(0, NE) as e:
                    dve.wait_ge(h_mm, FREE + e * IB)
                    take_tokens(e)
                    for u in range(NU + 1):
                        if u < NU:
                            weights_out(dve, nc.vector.tensor_copy, e, 2 * u + 1, wT_dve)
                        if 1 <= u <= IB:
                            k = u - 1
                            dve.wait_ge(silu_done, e * IB + k + 1)
                            nc.vector.tensor_tensor(hT[:, k, :], hb[:, k % 2, SLOTS:2 * SLOTS], sg[:, k % 2, :], ALU.mult).then_inc(h_ready, 1)
                        if u > IB and (u - IB) % 2 == 0:
                            d = (u - IB) // 2 - 1
                            dve.wait_ge(y_mm, e * DC + d + 1)
                            nc.vector.tensor_copy(yT[:, d, :, bass.ds(e, 1), :],
                                                  yb[:, d % 2, 0:SLOTS].rearrange("p (b a s) -> p b a s", b=NB, a=1)).then_inc(y_out, 1)


def combine_stage(nc, S, scatter, yT, out):
    with ExitStack() as ctx:
        m = Mem(nc, ctx, "comb")
        sb, ps, sem = m.sb, m.ps, m.sem
        K = 2 * HALF
        y_b = sb("y_b", [P, DC, 2 * K])
        scat_b = sb("scat_b", [K, 2, NQ])
        y_nat = sb("y_nat", [K, 2, D])
        res = sb("res", [P, 2, D])
        tb = ps("tb", [P, 2, BANK])
        ob = ps("ob", [P, BANK])
        batch_ready, yT_mm, y_act, y_dve, o_mm, res_ready = (sem(n) for n in ("batch_ready", "yT_mm", "y_act", "y_dve", "o_mm", "res_ready"))
        out_done = [sem("out_done0"), sem("out_done1")]
        with nc.Block() as block:

            @block.vector
            def _(dve):
                dve.sem_inc(res_ready, FREE)
                with dve.Fori(0, NB // 2) as b2:
                    for r in range(2):
                        b = b2 * 2 + r
                        nc.vector.tensor_copy(y_b[:].rearrange("p c (a n) -> p c a n", a=1),
                                              yT[:, :, bass.ds(b, 1)].rearrange("p c a e s -> p c a (e s)"))
                        nc.vector.tensor_copy(scat_b[:].unsqueeze(1), one(scatter[:], b)).then_inc(batch_ready, 1)
                        dve.wait_ge(yT_mm, b2 * 4 + 2 * r + 2)
                        nc.vector.tensor_copy(y_nat[:, 1, :], tb[0:K, 1, :]).then_inc(y_dve, 1)
                        dve.wait_ge(o_mm, b2 * 2 + r + 1)
                        dve.wait_ge(out_done[r], 16 * FREE + b2 * 16)
                        nc.vector.scalar_tensor_tensor(out=res[0:NQ, r, :].unsqueeze(1), in0=ob[0:NQ, :].unsqueeze(1), scalar=S.tanh_g[0:NQ, 3:4],
                                                       in1=one(S.X[0:NQ], b), op0=ALU.mult, op1=ALU.add).then_inc(res_ready, 1)

            @block.scalar
            def _(act):
                act.sem_inc(out_done[0], 16 * FREE)
                act.sem_inc(out_done[1], 16 * FREE)
                with act.Fori(0, NB // 2) as b2:
                    for r in range(2):
                        act.wait_ge(yT_mm, b2 * 4 + 2 * r + 1)
                        nc.scalar.copy(y_nat[:, 0, :], tb[0:K, 0, :]).then_inc(y_act, 1)
                        act.wait_ge(res_ready, FREE + b2 * 2 + r + 1)
                        act.dma_start(out[bass.ds(b2 * 2 + r, 1)].rearrange("a q d -> q (a d)"), res[0:NQ, r, :]).then_inc(out_done[r], 16)
                act.wait_ge(out_done[0], 16 * FREE + 16 * (NB // 2))
                act.wait_ge(out_done[1], 16 * FREE + 16 * (NB // 2))

            @block.tensor
            def _(pe):
                with pe.Fori(0, NB) as b:
                    pe.wait_ge(batch_ready, b + 1)
                    for h in range(2):
                        for c in range(DC):
                            last = nc.tensor.transpose(tb[0:K, h, c * P:(c + 1) * P], y_b[:, c, h * K:(h + 1) * K], S.ident[:])
                        last.then_inc(yT_mm, 1)
                    pe.wait_ge(y_act, b + 1)
                    pe.wait_ge(res_ready, FREE + b)
                    nc.tensor.matmul(ob[0:NQ, :], scat_b[:, 0, :], y_nat[:, 0, :], start=True, stop=False)
                    pe.wait_ge(y_dve, b + 1)
                    nc.tensor.matmul(ob[0:NQ, :], scat_b[:, 1, :], y_nat[:, 1, :], start=False, stop=True).then_inc(o_mm, 1)


def flamingo(nc, x, ctx_1024, g_xattn, g_ffn, a0, f0, a1, mlp, f1, out):
    with ExitStack() as ctx:
        S = start_state(nc, ctx)
        setup_stage(nc, S, x, g_xattn, g_ffn)
        attention_stage(nc, S, 0, ctx_1024, *a0)
        quantised_stage(nc, S, *f0)
        attention_stage(nc, S, 1, ctx_1024, *a1, mlp=mlp)
        mixture_stages(nc, S, *f1, out)


_A0 = ["L0_xattn_" + n for n in ("wq_w", "wq_b", "wk_w", "wk_b", "wv_w", "wv_b", "dense_w", "dense_b")]
_F0 = ["L0_ffn_" + n for n in ("w_gate", "w_up", "w_down")]
_A1 = ["L1_xattn_" + n for n in ("Wq", "bq", "Wk", "bk", "Wv", "bv", "Wo", "bo")]
_MLP = ["L1_xattn_" + n for n in ("w1", "b1", "w2", "b2", "w3", "b3")]
_F1 = ["L1_ffn_" + n for n in ("gate_w", "w_gate", "w_up", "w_down")]


def kernel(**inputs):
    import numpy as _np
    import concourse.bacc as _bacc
    from concourse import mybir as _mybir
    from concourse.bass_utils import run_bass_kernel_spmd as _run

    nc = _bacc.Bacc("TRN2", target_bir_lowering=False, num_devices=1)
    arrays, args = {}, {}
    for name in ["x", "ctx_1024", "g_xattn", "g_ffn"] + _A0 + _F0 + _A1 + _MLP + _F1:
        a = _np.ascontiguousarray(inputs[name])
        arrays[f"in_{name}_dram"] = a
        args[name] = nc.dram_tensor(f"in_{name}_dram", a.shape, _mybir.dt.from_np(a.dtype), kind="ExternalInput").ap()
    out = nc.dram_tensor("out_0_dram", (NB, NQ, D), F32, kind="ExternalOutput").ap()
    flamingo(nc, args["x"], args["ctx_1024"], args["g_xattn"], args["g_ffn"], *([args[n] for n in g] for g in (_A0, _F0, _A1, _MLP, _F1)), out)
    r = _run(nc, [arrays], core_ids=[0])
    return r.results[0]["out_0_dram"]
```

```python
from contextlib import ExitStack

import concourse.bass as bass
from concourse import mybir

F32 = mybir.dt.float32
F32R = mybir.dt.float32r
BF16 = mybir.dt.bfloat16
ALU = mybir.AluOpType
ACT = mybir.ActivationFunctionType
AX = mybir.AxisListType.X

P = 128
NB, NQ, D = 8, 100, 512
NK = 722
NH, DH = 16, 32
DC = D // P
HPC = P // DH
KC = (NK + P - 1) // P
KFULL = NK // P
KREST = NK - KFULL * P
KHALF = NK // 2
KEVEN = KHALF + KHALF % 2
NKPAD = KHALF + KEVEN
BANK = 512
INNER = 2048
NE = 8
CAP = NQ // NE * 2
SLOTS = NB * CAP
LN_EPS = 1e-5
ROUND = 12582912.0
QMAX = 127.0
LOG_T_MIN, LOG_T_MAX = -2.302585092994046, 2.302585092994046


FREE = 1


def ksize(j):
    return P if j < KFULL else KREST


SPLIT = ((0, 0), (0, 1), (1, 0))


def one(ap, i):
    return ap[:, bass.ds(i, 1)]


def rows(v):
    return v.rearrange("(a n) -> a n", a=1)


def spread(v, n):
    return rows(v).broadcast_to([n, v.shape[0]])


class Mem:

    def __init__(self, nc, ctx, tag):
        self.nc, self.ctx, self.tag, self.sems = nc, ctx, tag, []
        ctx.callback(self.leave)

    def leave(self):
        if self.sems:
            self.nc.clear_and_free_semaphores(self.sems)
            self.nc.all_engine_barrier()

    def sb(self, name, shape, dt=F32):
        return self.ctx.enter_context(self.nc.sbuf_tensor(f"{self.tag}_{name}", shape, dt))

    def ps(self, name, shape, dt=F32):
        return self.ctx.enter_context(self.nc.psum_tensor(f"{self.tag}_{name}", shape, dt))

    def sem(self, name):
        self.sems.append(self.nc.alloc_semaphore(f"{self.tag}_{name}"))
        return self.sems[-1]


class Chain:

    def __init__(self, eng, sem):
        self.eng, self.sem, self.n, self.base = eng, sem, 0, 0

    def __call__(self, ins):
        ins.then_inc(self.sem, 1)
        self.n += 1
        self.eng.wait_ge(self.sem, self.base + self.n)

    def loop(self, i, per):
        self.base, self.n = self.before + i * per, 0

    def enter(self):
        self.before, self.n, self.base = self.n, 0, 0

    def leave(self, passes, per):
        if self.n != per:
            raise ValueError(f"{self.n} results in a pass, {per} were said")
        self.base, self.n = 0, self.before + passes * per


def setup_stage(nc, S, x, g_xattn, g_ffn):
    with ExitStack() as ctx:
        m = Mem(nc, ctx, "setup")
        gates = m.sb("gates", [P, 4])
        x_in, ident_zero, ident_done, gates_done = (m.sem(n) for n in ("x_in", "ident_zero", "ident_done", "gates_done"))
        with nc.Block() as block:

            @block.sync
            def _(sp):
                sp.dma_start(gates[:, 0:2], spread(g_xattn, P)).then_inc(x_in, 16)
                sp.dma_start(gates[:, 2:4], spread(g_ffn, P)).then_inc(x_in, 16)
                sp.dma_start(S.X[0:NQ], x.rearrange("b q d -> q b d")).then_inc(x_in, 16)
                sp.wait_ge(x_in, 48)

            @block.gpsimd
            def _(pool):
                nc.gpsimd.memset(S.ident[:], 0.0).then_inc(ident_zero, 1)
                nc.gpsimd.memset(S.ones[:], 1.0).then_inc(ident_zero, 1)
                pool.wait_ge(ident_zero, 2)
                nc.gpsimd.affine_select(out=S.ident[:], in_=S.ident[:], compare_op=ALU.not_equal, fill=1.0,
                                        base=0, pattern=[[-1, P]], channel_multiplier=1).then_inc(ident_done, 1)

            @block.vector
            def _(dve):
                dve.wait_ge(ident_done, 1)
                nc.vector.tensor_copy(S.identb[:], S.ident[:]).then_inc(gates_done, 1)

            @block.scalar
            def _(act):
                act.wait_ge(x_in, 48)
                nc.scalar.activation(S.tanh_g[:], gates[:], ACT.Tanh).then_inc(gates_done, 1)


def attention_stage(nc, S, layer, ctx_dram, wq, bq, wk, bk, wv, bv, wo, bo, mlp=None):
    L1 = mlp is not None
    tag = f"at{layer}"
    with ExitStack() as ctx:
        m = Mem(nc, ctx, tag)
        sb, ps, sem = m.sb, m.ps, m.sem
        woT = sb("woT", [P, DC, D])
        wkT, wvT = sb("wkT", [P, 2, DC, D], F32R), sb("wvT", [P, 2, DC, D], F32R)
        bias_q, bias_k, bias_v = (sb(f"bias_{n}", [P, DC]) for n in "qkv")
        bias_o = sb("bias_o", [P, D])
        stats, mean_var = sb("stats", [P, NB, 6]), sb("mean_var", [P, NB, 2])
        std, rstd = sb("std", [P, NB]), sb("rstd", [P, NB])
        xn = sb("xn", [P, 2, D])
        ctx_nat = sb("ctx_nat", [P, KC, D])
        ctxT = sb("ctxT", [P, 2, DC, NKPAD], F32R)
        QT = sb("QT", [P, DC, NQ])
        q_dram = nc.dram_tensor(f"{tag}_queries", (NB, P, DC * NQ), F32, kind="Internal").ap()
        Qm = sb("Qm", [P, 2, DC, HPC, NQ], F32R)
        KT = sb("KT", [P, 2, DC, NKPAD], F32R)
        V = sb("V", [P, KC, D])
        group = sb("group", [P, HPC])
        head_rows = sb("head_rows", [NH, D])
        LAG = 3
        NP = NH if L1 else LAG + 2
        probs = sb("probs", [P, NP, NK])
        probsT = sb("probsT", [P, 2, KC, NQ])
        neg_max, denom, rdenom = (sb(n, [P, NH]) for n in ("neg_max", "denom", "rdenom"))
        rdenT, OT = sb("rdenT", [NH, NQ]), sb("OT", [P, DC, NQ])
        ksum = sb("ksum", [P, DC, 2])
        room = probs[:].rearrange("p h k -> p (h k)")
        xnT = room[:, 0:DC * NB * NQ].rearrange("p (c n) -> p c n", c=DC)
        wqT = V[:, 0:DC, :]
        QB = NB // 2
        if L1:
            w1, b1, w2, b2, w3, b3 = mlp
            DM = w1.shape[0]
            scores = probs
            used = DC * NB * NQ
            q_room = room[:, used + 3 * DC * D:used + 3 * DC * D + DC * QB * NQ]
            w_nat = room[:, used:used + 3 * DC * D].rearrange("p (a o i) -> p a o i", a=3, o=DC)
            junk = [probsT[0:NQ].rearrange("p a j q -> p (a j q)")[:, 0:NK], xn[0:NQ].rearrange("p a d -> p (a d)")[:, 0:NK]]
            maxs, denom1, sqsum, varr = (sb(n, [P, NH]) for n in ("maxs", "denom1", "sqsum", "varr"))
            qsum, ksum1, qk4 = sb("qsum", [P, NB, DC]), sb("ksum1", [P, DC]), sb("qk4", [P, DC])
            qk_heads = sb("qk_heads", [P, DC, HPC])
            w1_all = probsT[:, 0].rearrange("p j q -> p (j q)")[:, 0:3 * DM].rearrange("p (o j) -> p o j", j=3)
            w1_scaled = sb("w1_scaled", [P, 3, DM])
            w2_nat, w2T = sb("w2_nat", [DM, DM]), sb("w2T", [DM, P])
            w3_col, w3_all = sb("w3_col", [DM, 1]), sb("w3_all", [DM, P])
            b1_col, b2_col, b3_all = sb("b1_col", [DM, 1]), sb("b2_col", [DM, 1]), sb("b3_all", [P, 1])
            hid1, hid2 = sb("hid1", [DM, NH]), sb("hid2", [DM, NH])
            log_t, inv_t, ratio, bias2 = (sb(n, [P, NH]) for n in ("log_t", "inv_t", "ratio", "bias2"))
        else:
            w_nat = sb("w_nat", [P, 3, DC, D])
            q_room = sb("q_room", [P, DC * QB * NQ])
        Q_half = [q_room[:].rearrange("p (b c q) -> p b c q", b=QB, c=DC), xnT[:, :, 0:QB * NQ].rearrange("p c (b q) -> p b c q", b=QB)]
        wide = ps("wide", [P, 4, BANK])
        tb = ps("tb", [P, 2, BANK])
        ob = ps("ob", [P, BANK])
        mb = ps("mb", [P, BANK])

        w_in = [sem(f"w_in{i}") for i in range(3)]
        whigh_ready, wT_ready, wT_mm = (sem(n) for n in ("whigh_ready", "wT_ready", "wT_mm"))
        small_in, ctx_in, dve_own = (sem(n) for n in ("small_in", "ctx_in", "dve_own"))
        var_ready, std_ready, pre_done = (sem(n) for n in ("var_ready", "std_ready", "pre_done"))
        xn_ready, xnT_mm, xnT_ready, q_mm, q_out = (sem(n) for n in ("xn_ready", "xnT_mm", "xnT_ready", "q_mm", "q_out"))
        front_mm, high_done, front_out = (sem(n) for n in ("front_mm", "high_done", "front_out"))
        q_stored, q_in, pads_done, bias_scaled, bias_added = (sem(n) for n in ("q_stored", "q_in", "pads_done", "bias_scaled", "bias_added"))
        qhigh_done, qm_ready = sem("qhigh_done"), sem("qm_ready")
        v_mm, v_act, v_dve = (sem(n) for n in ("v_mm", "v_act", "v_dve"))
        score_mm, max_ready, exp_done = (sem(n) for n in ("score_mm", "max_ready", "exp_done"))
        rd_ready, rdT_mm, rdT_ready, rdR_mm = (sem(n) for n in ("rd_ready", "rdT_mm", "rdT_ready", "rdR_mm"))
        pT_mm0, pT_mm1, pT_act, pT_dve = (sem(n) for n in ("pT_mm0", "pT_mm1", "pT_act", "pT_dve"))
        pv_mm, ot_ready, y_mm, x_done, group_own, rows_own = (sem(n) for n in ("pv_mm", "ot_ready", "y_mm", "x_done", "group_own", "rows_own"))
        if L1:
            first_exp, square_act, square_dve, score_out, stat_ready, h1_mm, h1_act, h2_mm, h2_act, t_mm, clip_ready, inv_ready, ratio_ready = (
                sem(n) for n in ("first_exp", "square_act", "square_dve", "score_out", "stat_ready", "h1_mm", "h1_act", "h2_mm", "h2_act", "t_mm", "clip_ready",
                                 "inv_ready", "ratio_ready"))
            w2_mm = sem("w2_mm")
        S_FREE = score_out if L1 else exp_done
        NSMALL = 4 + (6 if L1 else 0)
        NF = KC + 2 * DC
        QG = 2 * DC
        sizes = [ksize(j) for j in range(KC)]
        HALVES = (2, KC - 2) if L1 else (3, KC - 3)
        scale = float(DH) ** -0.5
        K_PARTS = [(g, i) for g in range(KC, NF) for i in range(DC)]
        if L1:
            FRONT = {-3: [(g, DC - 1) for g in range(3)], -2: [(g, DC - 1) for g in range(3, KC)], -1: K_PARTS[0:8]}
            for h in range(NH - 1):
                FRONT[h] = K_PARTS[8 + h * 20 // (NH - 1):8 + (h + 1) * 20 // (NH - 1)]
            FRONT[NH] = K_PARTS[28:]
        else:
            FRONT = {k: [(2 * k + n, DC - 1) for n in range(2)] for k in range(3)}
            FRONT[3], FRONT[4] = K_PARTS[0:4], K_PARTS[4:]

        V_AFTER = {2: (0,), 5: (1,), 8: (2,), 11: (3,), NH: (4, 5)}

        def front_units(step):
            return [g for g, i in FRONT.get(step, ()) if i == DC - 1]

        with nc.Block() as block:

            @block.sync
            def _(sp):
                def load_ctx(b):
                    src = ctx_dram[bass.ds(b, 1)].rearrange("a k d -> (a k) d")
                    sp.dma_start(ctx_nat[:, 0:KFULL], src[0:KFULL * P].rearrange("(j p) d -> p j d", p=P)).then_inc(ctx_in, 16)
                    sp.dma_start(ctx_nat[0:KREST, KFULL], src[KFULL * P:NK]).then_inc(ctx_in, 16)

                for n, w in enumerate((wq, wk, wv)):
                    sp.dma_start(w_nat[:, n], w.rearrange("(o p) i -> p o i", p=P)).then_inc(w_in[n], 16)
                for bias, col in ((bq, bias_q), (bk, bias_k), (bv, bias_v)):
                    sp.dma_start(col[:], bias.rearrange("(c p) -> p c", p=P), allow_slow_non_contiguous=True).then_inc(small_in, 16)
                sp.dma_start(bias_o[:], spread(bo, P)).then_inc(small_in, 16)
                if L1:
                    sp.dma_start(w1_all[:], w1.rearrange("(a o) j -> a o j", a=1).broadcast_to([P, DM, 3])).then_inc(small_in, 16)
                    sp.dma_start(w2_nat[:], w2).then_inc(small_in, 16)
                    sp.dma_start(w3_col[:], w3.rearrange("a d -> d a"), allow_slow_non_contiguous=True).then_inc(small_in, 16)
                    sp.dma_start(b1_col[:], b1.rearrange("(d a) -> d a", a=1), allow_slow_non_contiguous=True).then_inc(small_in, 16)
                    sp.dma_start(b2_col[:], b2.rearrange("(d a) -> d a", a=1), allow_slow_non_contiguous=True).then_inc(small_in, 16)
                    sp.dma_start(b3_all[:], spread(b3, P)).then_inc(small_in, 16)
                load_ctx(0)
                sp.wait_ge(wT_mm, DC)
                sp.dma_start(w_nat[:, 0], wo.rearrange("(o p) i -> p o i", p=P)).then_inc(w_in[0], 16)
                for half in range(2):
                    sp.wait_ge(q_out, DC * (half + 1))
                    for b in range(QB):
                        sp.dma_start(q_dram[half * QB + b].rearrange("p (c q) -> p c q", c=DC), Q_half[half][:, b]).then_inc(q_stored, 16)
                sp.wait_ge(q_stored, 16 * NB)

                def load_queries(b):
                    sp.dma_start(QT[:].rearrange("p c q -> p (c q)"), q_dram[bass.ds(b, 1)].rearrange("a p n -> p (a n)")).then_inc(q_in, 16)

                load_queries(0)
                with sp.Fori(0, NB - 1) as b:
                    sp.wait_ge(front_mm, b * NF + KC)
                    load_ctx(b + 1)
                    sp.wait_ge(qm_ready, b + 1)
                    load_queries(b + 1)
                sp.wait_ge(ctx_in, 32 * NB)
                sp.wait_ge(q_in, 16 * NB)

            @block.tensor
            def _(pe):
                pe.sem_inc(pT_mm1, FREE)
                pe.sem_inc(pv_mm, FREE)
                with pe.Fori(0, NB // 2) as b2:
                    for r in range(2):
                        pe.wait_ge(xn_ready, b2 * 2 + r + 1)
                        pe.wait_ge(xnT_ready, FREE + b2 * 2 + max(r - 1, 0))
                        for c in range(DC):
                            last = nc.tensor.transpose(tb[:, r, c * NQ:(c + 1) * NQ], xn[0:NQ, r, c * P:(c + 1) * P], S.ident[0:NQ, 0:NQ])
                        last.then_inc(xnT_mm, 1)

                def transpose_weights(n):
                    pe.wait_ge(w_in[n % 3], 16 * (n // 3 + 1))
                    for i in range(DC):
                        if n == 2:
                            pe.wait_ge(q_out, DC + i + 1)
                        elif n >= 1:
                            pe.wait_ge(wT_ready, DC * (n - 1) + i + 1)
                        for o in range(DC):
                            last = nc.tensor.transpose(wide[:, i, o * P:(o + 1) * P], w_nat[:, n % 3, o, i * P:(i + 1) * P], S.ident[:])
                        last.then_inc(wT_mm, 1)

                transpose_weights(0)
                transpose_weights(1)
                pe.wait_ge(wT_ready, DC)
                pe.wait_ge(xnT_ready, FREE + NB)
                for g in range(QG):
                    if g < 4:
                        pe.wait_ge(wT_ready, DC + g + 1)
                    else:
                        pe.wait_ge(q_out, g - 4 + 1)
                    half, o = g // DC, g % DC
                    for i in range(DC):
                        last = nc.tensor.matmul(wide[:, g % 4, 0:QB * NQ], wqT[:, i, o * P:(o + 1) * P], xnT[:, i, half * QB * NQ:(half + 1) * QB * NQ],
                                                start=(i == 0), stop=(i == DC - 1))
                    last.then_inc(q_mm, 1)
                transpose_weights(2)
                transpose_weights(3)
                pe.wait_ge(wT_ready, 4 * DC)
                pe.wait_ge(rows_own, 3)
                pe.wait_ge(pre_done, 1)
                if L1:
                    nc.tensor.transpose(mb[0:DM, 0:DM], w2_nat[:], S.ident[0:DM, 0:DM]).then_inc(w2_mm, 1)
                    pe.wait_ge(pre_done, 2)

                def front(b, g, part, first=False):
                    if g >= KC and part > 0:
                        pass
                    elif g >= 4:
                        pe.wait_ge(front_out, b * NF + g - 4 + 1)
                    elif not first:
                        pe.wait_ge(S_FREE, b * NH)
                    if g < KC:
                        if g == 0:
                            pe.wait_ge(ctx_in, 32 * b + 32)
                        for c in range(DC):
                            last = nc.tensor.transpose(wide[:, g % 4, c * P:c * P + sizes[g]],
                                                       ctx_nat[0:sizes[g], g, c * P:(c + 1) * P], S.ident[0:sizes[g], 0:sizes[g]])
                    else:
                        if g == KC and part == 0:
                            pe.wait_ge(front_out, b * NF + KC)
                        o, half = (g - KC) // 2, (g - KC) % 2
                        for n, (sw, sc) in enumerate(SPLIT):
                            last = nc.tensor.matmul(wide[:, g % 4, 0:KEVEN], wkT[:, sw, part, o * P:(o + 1) * P],
                                                    ctxT[:, sc, part, half * KHALF:half * KHALF + KEVEN],
                                                    start=(part == 0 and n == 0), stop=(part == DC - 1 and n == 2))
                    if part == DC - 1:
                        last.then_inc(front_mm, 1)

                def batch(b, final):

                    def next_front(step):
                        if not final:
                            for g, part in FRONT.get(step, ()):
                                front(b + 1, g, part)

                    def values(j):
                        if j < 2:
                            pe.wait_ge(pT_act if j == 0 else pT_dve, FREE + b * NH)
                        else:
                            pe.wait_ge(v_act if j % 2 == 0 else v_dve, b * 3 + j // 2)
                        for i in range(DC):
                            for n, (sc, sw) in enumerate(SPLIT):
                                last = nc.tensor.matmul(tb[0:sizes[j], j % 2, :], ctxT[:, sc, i, j * P:j * P + sizes[j]], wvT[:, sw, i, :],
                                                        start=(i == 0 and n == 0), stop=(i == DC - 1 and n == 2))
                        last.then_inc(v_mm, 1)

                    def score(h):
                        if h < 2:
                            pe.wait_ge(qm_ready, b + 1)
                            pe.wait_ge(front_out, b * NF + NF)
                        else:
                            pe.wait_ge(S_FREE, b * NH + h - 1)
                        c, r = h // HPC, h % HPC
                        for half in range(2):
                            for n, (sq, sk) in enumerate(SPLIT):
                                last = nc.tensor.matmul(wide[0:NQ, 2 * (h % 2) + half, 0:KEVEN], Qm[:, sq, c, r, :],
                                                        KT[:, sk, c, half * KHALF:half * KHALF + KEVEN], start=(n == 0), stop=(n == 2))
                        last.then_inc(score_mm, 1)

                    def transpose_probs(h):
                        pe.wait_ge(exp_done, b * NH + h + 1)
                        for half, mm in enumerate((pT_mm0, pT_mm1)):
                            if h == 0:
                                pe.wait_ge(v_act if half == 0 else v_dve, b * 3 + 3)
                            else:
                                pe.wait_ge(pT_act if half == 0 else pT_dve, FREE + b * NH + h)
                            for t in range(HALVES[half]):
                                j = half * HALVES[0] + t
                                last = nc.tensor.transpose(tb[0:sizes[j], half, t * NQ:(t + 1) * NQ],
                                                           probs[0:NQ, h % NP, j * P:j * P + sizes[j]], S.ident[0:NQ, 0:NQ])
                            last.then_inc(mm, 1)

                    def weigh_values(h):
                        pe.wait_ge(pT_act, FREE + b * NH + h + 1)
                        pe.wait_ge(pT_dve, FREE + b * NH + h + 1)
                        if h == 0:
                            pe.wait_ge(x_done, FREE + b)
                        c, r = h // HPC, DH * (h % HPC)
                        for j in range(KC):
                            last = nc.tensor.matmul(ob[r:r + DH, c * NQ:(c + 1) * NQ], V[0:sizes[j], j, h * DH:(h + 1) * DH],
                                                    probsT[0:sizes[j], h % 2, j, :], start=(j == 0), stop=(j == KC - 1))
                        if h == NH - 1:
                            last.then_inc(pv_mm, 1)

                    def transpose_rdenom():
                        pe.wait_ge(rd_ready, b + 1)
                        nc.tensor.transpose(mb[0:NH, 0:NQ], rdenom[0:NQ, :], S.ident[0:NQ, 0:NQ]).then_inc(rdT_mm, 1)

                    def spread_rdenom():
                        pe.wait_ge(rdT_ready, b + 1)
                        for c in range(DC):
                            last = nc.tensor.matmul(mb[:, c * NQ:(c + 1) * NQ], head_rows[:, c * P:(c + 1) * P], rdenT[:], start=True, stop=True)
                        last.then_inc(rdR_mm, 1)

                    if not L1:
                        score(0)
                        score(1)
                        for j in range(KC):
                            values(j)
                        for h in range(2, NH + LAG + 1):
                            if h < NH:
                                score(h)
                            if LAG <= h < NH + LAG:
                                transpose_probs(h - LAG)
                            if h > LAG:
                                weigh_values(h - LAG - 1)
                            if h == NH + 1:
                                transpose_rdenom()
                            if h == NH + 2:
                                spread_rdenom()
                            next_front(h - NH)
                    else:
                        for h in range(NH + 1):
                            if h < NH:
                                score(h)
                            for j in V_AFTER.get(h, ()):
                                values(j)
                        pe.wait_ge(stat_ready, b + 1)
                        nc.tensor.matmul(mb[0:DM, 0:NH], w1_scaled[:, 0, :], qk_heads[:].rearrange("p c g -> p (c g)"), start=True, stop=False)
                        nc.tensor.matmul(mb[0:DM, 0:NH], w1_scaled[0:NQ, 1, :], maxs[0:NQ, :], start=False, stop=False)
                        nc.tensor.matmul(mb[0:DM, 0:NH], w1_scaled[0:NQ, 2, :], varr[0:NQ, :], start=False, stop=True).then_inc(h1_mm, 1)
                        next_front(-3)
                        pe.wait_ge(h1_act, b + 1)
                        nc.tensor.matmul(mb[0:P, 0:NH], w2T[:], hid1[:], start=True, stop=True).then_inc(h2_mm, 1)
                        next_front(-2)
                        pe.wait_ge(h2_act, b + 1)
                        nc.tensor.matmul(mb[0:P, 0:NH], w3_all[:], hid2[:], start=True, stop=True).then_inc(t_mm, 1)
                        next_front(-1)
                        for h in range(NH + 1):
                            if h < NH:
                                transpose_probs(h)
                            if h == NH - 1:
                                transpose_rdenom()
                            if h >= 1:
                                weigh_values(h - 1)
                            if h == NH - 1:
                                spread_rdenom()
                            next_front(h)

                    pe.wait_ge(ot_ready, b + 1)
                    for c in range(DC):
                        last = nc.tensor.matmul(ob[0:NQ, :], OT[:, c, :], woT[:, c, :], start=(c == 0), stop=(c == DC - 1))
                    last.then_inc(y_mm, 1)
                    if not L1:
                        next_front(4)

                for g in range(NF):
                    for part in (range(DC) if g >= KC else (DC - 1,)):
                        front(0, g, part, first=True)
                with pe.Fori(0, NB - 1) as b:
                    batch(b, False)
                batch(NB - 1, True)

            @block.scalar
            def _(act):
                act.sem_inc(pT_act, FREE)
                act.sem_inc(xnT_ready, FREE)
                if L1:
                    act.sem_inc(square_act, FREE)
                    act.sem_inc(square_dve, FREE)
                act.wait_ge(var_ready, 1)
                nc.scalar.activation(std[0:NQ, :], std[0:NQ, :], ACT.Sqrt).then_inc(std_ready, 1)
                with act.Fori(0, NB // 2) as b2:
                    for r in range(2):
                        act.wait_ge(xnT_mm, b2 * 2 + r + 1)
                        nc.scalar.copy(xnT.rearrange("p c (b r q) -> p b r c q", r=2, q=NQ)[:, bass.ds(b2, 1), r],
                                       tb[:, r, 0:DC * NQ].rearrange("p (a c q) -> p a c q", a=1, c=DC)).then_inc(xnT_ready, 1)
                for n in (1, 2):
                    for i in range(DC):
                        act.wait_ge(wT_mm, DC * n + i + 1)
                        nc.scalar.copy((wkT, wvT)[n - 1][:, 0, i, :], wide[:, i, :]).then_inc(whigh_ready, 1)

                def front(b, g, first=False):
                    act.wait_ge(front_mm, b * NF + g + 1)
                    bank = wide[:, g % 4, :]
                    if g == 0 and first:
                        act.wait_ge(pads_done, 1)
                    if g < KC:
                        nc.scalar.copy(ctxT[:, 0, :, g * P:g * P + sizes[g]],
                                       bank.rearrange("p (c k) -> p c k", c=DC)[:, :, 0:sizes[g]]).then_inc(high_done, 1)
                    else:
                        o, half = (g - KC) // 2, (g - KC) % 2
                        nc.scalar.activation(KT[:, 0, o, half * KHALF:(half + 1) * KHALF], bank[:, 0:KHALF], ACT.Identity,
                                             bias=bias_k[:, o:o + 1], accum_out=ksum[:, o, half:half + 1]).then_inc(high_done, 1)

                def batch(b, final):

                    def next_front(step):
                        if not final:
                            for g in front_units(step):
                                front(b + 1, g)

                    def values_out(j):
                        act.wait_ge(v_mm, b * KC + j + 1)
                        nc.scalar.copy(V[0:sizes[j], j, :], tb[0:sizes[j], j % 2, :]).then_inc(v_act, 1)

                    def probsT_out(h):
                        act.wait_ge(pT_mm0, b * NH + h + 1)
                        nc.scalar.activation(probsT[:, h % 2, 0:HALVES[0], :], tb[:, 0, 0:HALVES[0] * NQ].rearrange("p (j q) -> p j q", j=HALVES[0]),
                                             ACT.Relu if L1 else ACT.Copy).then_inc(pT_act, 1)

                    if not L1:
                        for h in range(NH + LAG + 1):
                            if h == 2:
                                for j in range(0, KC, 2):
                                    values_out(j)
                            if LAG <= h < NH + LAG:
                                probsT_out(h - LAG)
                            if h < NH:
                                act.wait_ge(max_ready, b * NH + h + 1)
                                act.wait_ge(pT_mm1, FREE + b * NH + max(h - NP + 1, 0))
                                nc.scalar.activation(probs[0:NQ, h % NP, :].rearrange("p (s k) -> p s k", s=2),
                                                     wide[0:NQ, 2 * (h % 2):2 * (h % 2) + 2, 0:KHALF], ACT.Exp,
                                                     bias=neg_max[0:NQ, h:h + 1], accum_out=denom[0:NQ, h:h + 1]).then_inc(exp_done, 1)
                            next_front(h - NH)
                        next_front(4)
                    else:
                        act.wait_ge(pv_mm, FREE + b)
                        for h in range(NH + 1):
                            if h < NH:
                                act.wait_ge(max_ready, b * NH + h + 1)
                                act.wait_ge(square_dve if h % 2 == 0 else square_act, FREE + b * (NH // 2) + h // 2)
                                nc.scalar.activation(junk[h % 2], scores[0:NQ, h, :], ACT.Exp, bias=neg_max[0:NQ, h:h + 1],
                                                     accum_out=denom1[0:NQ, h:h + 1]).then_inc(first_exp, 1)
                            if h % 2 == 1:
                                act.wait_ge(first_exp, b * NH + h + 1)
                                nc.scalar.activation(junk[1], junk[1], ACT.Square, accum_out=sqsum[0:NQ, h:h + 1]).then_inc(square_act, 1)
                            for j in V_AFTER.get(h, ()):
                                if j % 2 == 0:
                                    values_out(j)
                        act.wait_ge(h1_mm, b + 1)
                        nc.scalar.activation(hid1[:], mb[0:DM, 0:NH], ACT.Gelu, bias=b1_col[:]).then_inc(h1_act, 1)
                        next_front(-3)
                        act.wait_ge(h2_mm, b + 1)
                        nc.scalar.activation(hid2[:], mb[0:DM, 0:NH], ACT.Gelu, bias=b2_col[:]).then_inc(h2_act, 1)
                        next_front(-2)
                        act.wait_ge(clip_ready, b + 1)
                        nc.scalar.activation(inv_t[0:NQ, :], log_t[0:NQ, :], ACT.Exp, scale=-1.0).then_inc(inv_ready, 1)
                        act.wait_ge(ratio_ready, b + 1)
                        AHEAD = 3
                        for h in range(NH):
                            for k in range(h + AHEAD - 1 if h else 0, min(h + AHEAD, NH)):
                                nc.scalar.activation(probs[0:NQ, k, :], scores[0:NQ, k, :], ACT.Exp, bias=bias2[0:NQ, k:k + 1],
                                                     scale=ratio[0:NQ, k:k + 1], accum_out=denom[0:NQ, k:k + 1]).then_inc(exp_done, 1)
                            next_front(h - 1)
                            probsT_out(h)
                        next_front(NH - 1)
                        next_front(NH)

                for g in range(NF):
                    front(0, g, first=True)
                with act.Fori(0, NB - 1) as b:
                    batch(b, False)
                batch(NB - 1, True)

            @block.gpsimd
            def _(pool):
                nc.gpsimd.memset(group[:], 1.0).then_inc(group_own, 1)
                pool.wait_ge(group_own, 1)
                nc.gpsimd.affine_select(out=group[:], in_=group[:], compare_op=ALU.is_ge, fill=0.0, base=0,
                                        pattern=[[-DH, HPC]], channel_multiplier=1).then_inc(group_own, 1)
                pool.wait_ge(group_own, 2)
                nc.gpsimd.affine_select(out=group[:], in_=group[:], compare_op=ALU.is_ge, fill=0.0, base=DH - 1,
                                        pattern=[[DH, HPC]], channel_multiplier=-1).then_inc(group_own, 1)
                nc.gpsimd.memset(head_rows[:], 1.0).then_inc(rows_own, 1)
                pool.wait_ge(rows_own, 1)
                nc.gpsimd.affine_select(out=head_rows[:], in_=head_rows[:], compare_op=ALU.is_ge, fill=0.0, base=0,
                                        pattern=[[1, D]], channel_multiplier=-DH).then_inc(rows_own, 1)
                pool.wait_ge(rows_own, 2)
                nc.gpsimd.affine_select(out=head_rows[:], in_=head_rows[:], compare_op=ALU.is_ge, fill=0.0, base=DH - 1,
                                        pattern=[[-1, D]], channel_multiplier=DH).then_inc(rows_own, 1)

                pool.wait_ge(xn_ready, NB)
                pool.wait_ge(bias_scaled, 1)
                nc.gpsimd.tensor_tensor(S.X[0:NQ], S.X[0:NQ], bias_o[0:NQ, :].unsqueeze(1).broadcast_to([NQ, NB, D]), ALU.add).then_inc(bias_added, 1)

            @block.vector
            def _(dve):
                dve.sem_inc(pT_dve, FREE)
                dve.sem_inc(x_done, FREE)
                link = Chain(dve, dve_own)
                for b in range(NB):
                    last = nc.vector.bn_stats(stats[0:NQ, b, :], S.X[0:NQ, b, :])
                link(last)
                for b in range(NB):
                    last = nc.vector.bn_aggr(mean_var[0:NQ, b, :], stats[0:NQ, b, :])
                link(last)
                nc.vector.tensor_scalar(std[0:NQ, :], mean_var[0:NQ, :, 1], LN_EPS, None, ALU.add).then_inc(var_ready, 1)
                dve.wait_ge(std_ready, 1)
                link(nc.vector.reciprocal(rstd[0:NQ, :], std[0:NQ, :]))
                with dve.Fori(0, NB // 2) as b2:
                    for r in range(2):
                        b = b2 * 2 + r
                        if r == 0:
                            dve.wait_ge(xnT_ready, FREE + b2 * 2)
                        nc.vector.tensor_scalar(xn[0:NQ, r, :].unsqueeze(1), one(S.X[0:NQ], b), one(mean_var[0:NQ], b)[:, :, 0:1].rearrange("p a c -> p (a c)"),
                                                one(rstd[0:NQ], b), ALU.subtract, ALU.mult).then_inc(xn_ready, 1)

                def weights_out(n):
                    for i in range(DC):
                        if n in (1, 2):
                            w = (wkT, wvT)[n - 1]
                            dve.wait_ge(whigh_ready, DC * (n - 1) + i + 1)
                            nc.vector.tensor_tensor(w[:, 1, i, :], wide[:, i, :], w[:, 0, i, :].bitcast(F32), ALU.subtract).then_inc(wT_ready, 1)
                        else:
                            dve.wait_ge(wT_mm, DC * n + i + 1)
                            nc.vector.tensor_copy(woT[:, i, :] if n else wqT[:, i, :], wide[:, i, :]).then_inc(wT_ready, 1)

                weights_out(0)
                dve.wait_ge(small_in, 16 * NSMALL)
                link(nc.vector.tensor_scalar(bias_q[:], bias_q[:], scale, None, ALU.mult))
                weights_out(1)
                for g in range(QG):
                    half, o = g // DC, g % DC
                    dve.wait_ge(q_mm, g + 1)
                    nc.vector.tensor_scalar(Q_half[half][:, :, o, :], wide[:, g % 4, 0:QB * NQ].rearrange("p (b q) -> p b q", b=QB),
                                            scale, bias_q[:, o:o + 1], ALU.mult, ALU.add).then_inc(q_out, 1)
                weights_out(2)
                weights_out(3)
                dve.wait_ge(q_out, QG)
                if L1:
                    for half in range(2):
                        nc.vector.tensor_reduce(qsum[:, half * QB:(half + 1) * QB], Q_half[half], axis=AX, op=ALU.add)
                for n in range(2):
                    nc.vector.memset(ctxT[:, n, :, NK:NKPAD].bitcast(F32), 0.0)
                    last = nc.vector.memset(KT[:, n, :, NK:NKPAD].bitcast(F32), 0.0)
                last.then_inc(pads_done, 1)
                dve.wait_ge(group_own, 3)
                nc.vector.tensor_scalar(bias_o[:], bias_o[:], S.tanh_g[:, layer:layer + 1], None, ALU.mult).then_inc(bias_scaled, 1)
                if L1:
                    for j, f in enumerate((1.0 / (NQ * NK), 1.0 / NQ, 1.0 / NQ)):
                        nc.vector.tensor_scalar(w1_scaled[:, j, :], w1_all[:, :, j], f, None, ALU.mult)
                    last = nc.vector.tensor_copy(w3_all[:], w3_col[:].broadcast_to([DM, P]))
                else:
                    last = nc.vector.memset(rdenom[:], 1.0)
                last.then_inc(pre_done, 1)
                dve.wait_ge(pre_done, 1)
                if L1:
                    dve.wait_ge(w2_mm, 1)
                    nc.vector.memset(w2T[:, DM:P], 0.0)
                    nc.vector.tensor_copy(w2T[:, 0:DM], mb[0:DM, 0:DM]).then_inc(pre_done, 1)

                def front(b, g):
                    dve.wait_ge(high_done, b * NF + g + 1)
                    bank = wide[:, g % 4, :]
                    if g < KC:
                        k = slice(g * P, g * P + sizes[g])
                        nc.vector.tensor_tensor(ctxT[:, 1, :, k], bank.rearrange("p (c k) -> p c k", c=DC)[:, :, 0:sizes[g]],
                                                ctxT[:, 0, :, k].bitcast(F32), ALU.subtract).then_inc(front_out, 1)
                    else:
                        o, half = (g - KC) // 2, (g - KC) % 2
                        k = slice(half * KHALF, (half + 1) * KHALF)
                        nc.vector.scalar_tensor_tensor(out=KT[:, 1, o, k], in0=bank[:, 0:KHALF], scalar=bias_k[:, o:o + 1],
                                                       in1=KT[:, 0, o, k].bitcast(F32), op0=ALU.add, op1=ALU.subtract).then_inc(front_out, 1)
                        r = g - KC - 1
                        if 0 <= r < HPC:
                            if r == 0:
                                dve.wait_ge(q_in, 16 * b + 16)
                            nc.vector.tensor_scalar(Qm[:, 0, :, r, :], QT[:], group[:, r:r + 1], None, ALU.mult).then_inc(qhigh_done, 1)
                            dve.wait_ge(qhigh_done, b * HPC + r + 1)
                            last = nc.vector.scalar_tensor_tensor(out=Qm[:, 1, :, r, :], in0=QT[:], scalar=group[:, r:r + 1],
                                                                  in1=Qm[:, 0, :, r, :].bitcast(F32), op0=ALU.mult, op1=ALU.subtract)
                            if r == HPC - 1:
                                last.then_inc(qm_ready, 1)

                def batch(b, final):

                    def next_front(step):
                        if not final:
                            for g in front_units(step):
                                front(b + 1, g)

                    def values_out(j):
                        dve.wait_ge(v_mm, b * KC + j + 1)
                        nc.vector.tensor_copy(V[0:sizes[j], j, :], tb[0:sizes[j], j % 2, :]).then_inc(v_dve, 1)

                    def probsT_out(h):
                        dve.wait_ge(pT_mm1, FREE + b * NH + h + 1)
                        nc.vector.tensor_scalar(probsT[:, h % 2, HALVES[0]:KC, :], tb[:, 1, 0:HALVES[1] * NQ].rearrange("p (j q) -> p j q", j=HALVES[1]),
                                                0.0, None, ALU.max).then_inc(pT_dve, 1)

                    def invert_denom():
                        dve.wait_ge(exp_done, b * NH + NH)
                        link(nc.vector.reciprocal(rdenom[0:NQ, :], denom[0:NQ, :]))
                        nc.vector.tensor_scalar(rdenom[0:NQ, :], rdenom[0:NQ, :], 0.0, None, ALU.max).then_inc(rd_ready, 1)

                    def rdenT_out():
                        dve.wait_ge(rdT_mm, b + 1)
                        nc.vector.tensor_copy(rdenT[:], mb[0:NH, 0:NQ]).then_inc(rdT_ready, 1)

                    def spread_out():
                        dve.wait_ge(rdR_mm, b + 1)
                        link(nc.vector.tensor_copy(OT[:], mb[:, 0:DC * NQ].rearrange("p (c q) -> p c q", c=DC)))

                    if not L1:
                        for h in range(NH + LAG + 1):
                            if h == NH + 3:
                                spread_out()
                            if h == 2:
                                for j in range(1, KC, 2):
                                    values_out(j)
                            if h < NH:
                                dve.wait_ge(score_mm, b * NH + h + 1)
                                nc.vector.tensor_reduce(neg_max[0:NQ, h:h + 1].unsqueeze(2), wide[0:NQ, 2 * (h % 2):2 * (h % 2) + 2, 0:KHALF],
                                                        axis=mybir.AxisListType.XY, op=ALU.max, negate=True).then_inc(max_ready, 1)
                            if LAG <= h < NH + LAG:
                                probsT_out(h - LAG)
                            if h == NH:
                                invert_denom()
                            if h == NH + 1:
                                rdenT_out()
                            next_front(h - NH)
                    else:
                        def square(h):
                            dve.wait_ge(first_exp, b * NH + h + 1)
                            nc.vector.tensor_tensor_reduce(junk[0], junk[0], junk[0], 1.0, 0.0, ALU.mult, ALU.add,
                                                           sqsum[0:NQ, h:h + 1]).then_inc(square_dve, 1)

                        for h in range(NH + 1):
                            if h < NH:
                                dve.wait_ge(score_mm, b * NH + h + 1)
                                nc.vector.tensor_scalar(scores[0:NQ, h, :].rearrange("p (s k) -> p s k", s=2),
                                                        wide[0:NQ, 2 * (h % 2):2 * (h % 2) + 2, 0:KHALF], 0.0, -3.0e38,
                                                        ALU.add, ALU.max, accum_out=maxs[0:NQ, h:h + 1]).then_inc(score_out, 1)
                            if h >= 1:
                                dve.wait_ge(score_out, b * NH + h)
                                nc.vector.tensor_scalar(neg_max[0:NQ, h - 1:h], maxs[0:NQ, h - 1:h], -1.0, None, ALU.mult).then_inc(max_ready, 1)
                            if h % 2 == 0 and h >= 2:
                                square(h - 2)
                            if h == 3:
                                link(nc.vector.tensor_reduce(ksum1[:], ksum[:], axis=AX, op=ALU.add))
                                link(nc.vector.tensor_tensor(qk4[:].unsqueeze(1), one(qsum[:], b), ksum1[:].unsqueeze(1), ALU.mult))
                                link(nc.vector.tensor_tensor(qk_heads[:], qk4[:].unsqueeze(2).broadcast_to([P, DC, HPC]),
                                                             group[:].unsqueeze(1).broadcast_to([P, DC, HPC]), ALU.mult))
                            for j in V_AFTER.get(h, ()):
                                if j % 2 == 1:
                                    values_out(j)
                        dve.wait_ge(square_act, FREE + (b + 1) * (NH // 2))
                        dve.wait_ge(square_dve, FREE + (b + 1) * (NH // 2))
                        link(nc.vector.reciprocal(denom1[0:NQ, :], denom1[0:NQ, :]))
                        link(nc.vector.tensor_tensor(sqsum[0:NQ, :], sqsum[0:NQ, :], denom1[0:NQ, :], ALU.mult))
                        link(nc.vector.tensor_tensor(sqsum[0:NQ, :], sqsum[0:NQ, :], denom1[0:NQ, :], ALU.mult))
                        nc.vector.tensor_scalar(varr[0:NQ, :], sqsum[0:NQ, :], -1.0 / NK, 1.0 / (NK - 1), ALU.add, ALU.mult).then_inc(stat_ready, 1)
                        next_front(-3)
                        next_front(-2)
                        dve.wait_ge(t_mm, b + 1)
                        link(nc.vector.tensor_scalar(log_t[0:NQ, :], mb[0:NQ, 0:NH], b3_all[0:NQ, :], LOG_T_MIN, ALU.add, ALU.max))
                        nc.vector.tensor_scalar(log_t[0:NQ, :], log_t[0:NQ, :], LOG_T_MAX, None, ALU.min).then_inc(clip_ready, 1)
                        dve.wait_ge(inv_ready, b + 1)
                        link(nc.vector.tensor_scalar(ratio[0:NQ, :], inv_t[0:NQ, :], 0.5 * float(DH) ** 0.5, None, ALU.mult))
                        nc.vector.tensor_tensor(bias2[0:NQ, :], neg_max[0:NQ, :], ratio[0:NQ, :], ALU.mult).then_inc(ratio_ready, 1)
                        for h in range(NH):
                            if h == NH - 2:
                                invert_denom()
                            probsT_out(h)
                            if h == NH - 1:
                                rdenT_out()
                            next_front(h - 1)
                        spread_out()

                    dve.wait_ge(pv_mm, FREE + b + 1)
                    link(nc.vector.tensor_tensor(OT[:], ob[:, 0:DC * NQ].rearrange("p (c q) -> p c q", c=DC), OT[:], ALU.mult))
                    nc.vector.tensor_tensor(OT[:], OT[:], bias_v[:].unsqueeze(2).broadcast_to([P, DC, NQ]), ALU.add).then_inc(ot_ready, 1)
                    if L1:
                        next_front(NH - 1)
                        next_front(NH)
                    dve.wait_ge(y_mm, b + 1)
                    dve.wait_ge(bias_added, 1)
                    xb = one(S.X[0:NQ], b)
                    nc.vector.scalar_tensor_tensor(out=xb, in0=ob[0:NQ, :].unsqueeze(1), scalar=S.tanh_g[0:NQ, layer:layer + 1], in1=xb,
                                                   op0=ALU.mult, op1=ALU.add).then_inc(x_done, 1)
                    if not L1:
                        next_front(4)

                for g in range(NF):
                    front(0, g)
                link.enter()
                per = 3 + (3 + 3 + 2 if L1 else 0)
                with dve.Fori(0, NB - 1) as b:
                    link.loop(b, per)
                    batch(b, False)
                link.leave(NB - 1, per)
                batch(NB - 1, True)


class State:
    pass


def start_state(nc, ctx):
    S = State()
    m = Mem(nc, ctx, "all")
    S.X = m.sb("x", [P, NB, D])
    S.ident = m.sb("ident", [P, P])
    S.identb = m.sb("identb", [P, P], BF16)
    S.ones = m.sb("ones", [P, P])
    S.tanh_g = m.sb("tanh_g", [P, 4])
    return S


def quantised_stage(nc, S, w_gate, w_up, w_down):
    with ExitStack() as ctx:
        m = Mem(nc, ctx, "ffn0")
        sb, ps, sem = m.sb, m.ps, m.sem
        RB = INNER // P
        PIECE = 4 * D
        w_f = [sb(f"w_{n}", [P, RB * D]) for n in ("even", "odd")]
        w_f.append(w_f[0])
        tern = sb("tern", [P, 2, RB * D], BF16)
        gateT = sb("gateT", [P, DC, INNER], BF16)
        upT = sb("upT", [P, DC, INNER], BF16)
        downT = sb("downT", [P, RB, D], BF16)
        junk = sb("junk", [P, PIECE])
        abs_part, abs_sum = sb("abs_part", [P, 3, 4]), sb("abs_sum", [P, 3])
        w_step, w_scale = sb("w_step", [P, 3]), sb("w_scale", [P, 3])
        stats, mean_var = sb("stats", [P, NB, 6]), sb("mean_var", [P, NB, 2])
        std, rstd = sb("std", [P, NB]), sb("rstd", [P, NB])
        xn, xq = sb("xn", [P, D]), sb("xq", [P, D], BF16)
        xqT = sb("xqT", [P, DC, NQ], BF16)
        x_max, x_step, x_scale = sb("x_max", [P, 1]), sb("x_step", [P, 1]), sb("x_scale", [P, 1])
        gu_step = sb("gu_step", [P, 2])
        sg, hid = sb("sg", [P, 2, BANK]), sb("hid", [P, INNER])
        hq = sb("hq", [P, INNER], BF16)
        hqT = sb("hqT", [P, RB, NQ], BF16)
        h_max, h_step, h_scale, y_step = (sb(n, [P, 1]) for n in ("h_max", "h_step", "h_scale", "y_step"))

        tbank = [ps(f"tbank{i}", [P, 2 * BANK], BF16) for i in range(2)]
        gu = ps("gu", [P, 4, BANK])
        ob = ps("ob", [P, BANK])
        mb = ps("mb", [P, BANK])

        w_in = [sem(f"w_in{i}") for i in range(3)]
        (abs_done, part_sum, sum_mm, tern_ready, wT_mm, wT_act, wT_dve, dve_own, var_ready, std_ready) = (sem(n) for n in (
            "abs_done", "part_sum", "sum_mm", "tern_ready", "wT_mm", "wT_act", "wT_dve", "dve_own", "var_ready", "std_ready"))
        (xq_ready, xqT_mm, xqT_ready, gu_mm, silu_done, h_part, hq_ready, hqT_mm, hqT_act, hqT_dve, y_mm, x_done, step_ready) = (sem(n) for n in (
            "xq_ready", "xqT_mm", "xqT_ready", "gu_mm", "silu_done", "h_part", "hq_ready", "hqT_mm", "hqT_act", "hqT_dve", "y_mm",
            "x_done", "step_ready"))
        NT = RB * D // (2 * BANK)
        NPC = INNER // BANK

        def matrix_part(n, k):
            if n < 2:
                return (gateT, upT)[n][:, k // 2, (k % 2) * 2 * BANK:(k % 2 + 1) * 2 * BANK]
            return downT[:, 2 * k:2 * k + 2, :].rearrange("p k n -> p (k n)")

        with nc.Block() as block:

            @block.sync
            def _(sp):
                sp.dma_start(w_f[0][:].rearrange("p (o i) -> p o i", i=D), w_gate.rearrange("(o p) i -> p o i", p=P)).then_inc(w_in[0], 16)
                sp.dma_start(w_f[1][:].rearrange("p (o i) -> p o i", i=D), w_up.rearrange("(o p) i -> p o i", p=P)).then_inc(w_in[1], 16)
                sp.wait_ge(tern_ready, 4)
                sp.dma_start(w_f[2][:].rearrange("p (o i) -> p o i", i=INNER), w_down.rearrange("(o p) i -> p o i", p=P)).then_inc(w_in[2], 16)

            @block.tensor
            def _(pe):
                for n in range(3):
                    pe.wait_ge(part_sum, n + 1)
                    nc.tensor.matmul(mb[:, n:n + 1], S.ones[:], abs_sum[:, n:n + 1], start=True, stop=True).then_inc(sum_mm, 1)
                    pe.wait_ge(tern_ready, 4 * (n + 1))
                    for k in range(NT):
                        count = NT * n + k
                        if count >= 2:
                            pe.wait_ge(wT_act if k % 2 == 0 else wT_dve, count // 2)
                        for t in range(8):
                            if n < 2:
                                row, col = 8 * (k % 2) + t, k // 2
                                src = tern[:, n % 2, row * D + col * P:row * D + (col + 1) * P]
                            else:
                                row, col = t % 4, 2 * k + t // 4
                                src = tern[:, n % 2, row * INNER + col * P:row * INNER + (col + 1) * P]
                            last = nc.tensor.transpose(tbank[k % 2][:, t * P:(t + 1) * P], src, S.identb[:])
                        last.then_inc(wT_mm, 1)
                pe.wait_ge(wT_act, 3 * NT // 2)
                pe.wait_ge(wT_dve, 3 * NT // 2)

                with pe.Fori(0, NB) as b:
                    pe.wait_ge(xq_ready, b + 1)
                    pe.wait_ge(hqT_act, FREE + b)
                    for c in range(DC):
                        last = nc.tensor.transpose(tbank[0][:, c * P:c * P + NQ], xq[0:NQ, c * P:(c + 1) * P], S.identb[0:NQ, 0:NQ])
                    last.then_inc(xqT_mm, 1)
                    pe.wait_ge(xqT_ready, b + 1)
                    for n in range(NPC):
                        if n < 2:
                            pe.wait_ge(h_part, FREE + b * NPC)
                        else:
                            pe.wait_ge(h_part, FREE + b * NPC + n - 1)
                        for k, wT in enumerate((gateT, upT)):
                            for c in range(DC):
                                last = nc.tensor.matmul(gu[0:NQ, 2 * (n % 2) + k, :], xqT[:, c, :], wT[:, c, n * BANK:(n + 1) * BANK],
                                                        start=(c == 0), stop=(c == DC - 1))
                        last.then_inc(gu_mm, 1)
                    pe.wait_ge(hq_ready, b + 1)
                    for half in range(2):
                        if half == 1:
                            pe.wait_ge(hqT_dve, FREE + b)
                        for t in range(8):
                            last = nc.tensor.transpose(tbank[half][:, t * NQ:(t + 1) * NQ],
                                                       hq[0:NQ, (8 * half + t) * P:(8 * half + t + 1) * P], S.identb[0:NQ, 0:NQ])
                        last.then_inc(hqT_mm, 1)
                    pe.wait_ge(x_done, FREE + b)
                    pe.wait_ge(hqT_act, FREE + b + 1)
                    pe.wait_ge(hqT_dve, FREE + b + 1)
                    for k in range(RB):
                        last = nc.tensor.matmul(ob[0:NQ, :], hqT[:, k, :], downT[:, k, :], start=(k == 0), stop=(k == RB - 1))
                    last.then_inc(y_mm, 1)

            @block.scalar
            def _(act):
                act.sem_inc(hqT_act, FREE)
                def weights_out(n, k):
                    act.wait_ge(wT_mm, NT * n + k + 1)
                    nc.scalar.copy(matrix_part(n, k), tbank[k % 2][:]).then_inc(wT_act, 1)

                for n in range(3):
                    act.wait_ge(w_in[n], 16)
                    for k in range(4):
                        if 4 * n + k >= 1:
                            act.wait_ge(abs_done, 4 * n + k)
                        nc.scalar.activation(junk[:], w_f[n][:, k * PIECE:(k + 1) * PIECE], ACT.Abs,
                                             accum_out=abs_part[:, n, k:k + 1]).then_inc(abs_done, 1)
                    if n >= 1:
                        for k in range(0, NT, 2):
                            weights_out(n - 1, k)
                for k in range(0, NT, 2):
                    weights_out(2, k)
                act.wait_ge(var_ready, 1)
                nc.scalar.activation(std[0:NQ, :], std[0:NQ, :], ACT.Sqrt).then_inc(std_ready, 1)

                with act.Fori(0, NB) as b:
                    act.wait_ge(xqT_mm, b + 1)
                    nc.scalar.copy(xqT[:], tbank[0][:, 0:DC * P].rearrange("p (c k) -> p c k", c=DC)[:, :, 0:NQ]).then_inc(xqT_ready, 1)
                    act.wait_ge(step_ready, b + 1)
                    for n in range(NPC):
                        act.wait_ge(gu_mm, b * NPC + n + 1)
                        if n >= 2:
                            act.wait_ge(h_part, FREE + b * NPC + n - 1)
                        nc.scalar.activation(sg[0:NQ, n % 2, :], gu[0:NQ, 2 * (n % 2), :], ACT.Silu, scale=gu_step[0:NQ, 0:1]).then_inc(silu_done, 1)
                    act.wait_ge(hqT_mm, 2 * b + 1)
                    nc.scalar.copy(hqT[:, 0:8, :], tbank[0][:, 0:8 * NQ].rearrange("p (k q) -> p k q", k=8)).then_inc(hqT_act, 1)

            @block.vector
            def _(dve):
                dve.sem_inc(hqT_dve, FREE)
                dve.sem_inc(x_done, FREE)
                dve.sem_inc(h_part, FREE)
                link = Chain(dve, dve_own)

                def weights_out(n, k):
                    dve.wait_ge(wT_mm, NT * n + k + 1)
                    nc.vector.tensor_copy(matrix_part(n, k), tbank[k % 2][:]).then_inc(wT_dve, 1)

                for n in range(3):
                    dve.wait_ge(abs_done, 4 * (n + 1))
                    nc.vector.tensor_reduce(abs_sum[:, n:n + 1], abs_part[:, n, :], axis=AX, op=ALU.add).then_inc(part_sum, 1)
                    dve.wait_ge(sum_mm, n + 1)
                    link(nc.vector.tensor_scalar(w_step[:, n:n + 1], mb[:, n:n + 1], 1.0 / (INNER * D), 1e-5, ALU.mult, ALU.max))
                    link(nc.vector.reciprocal(w_scale[:, n:n + 1], w_step[:, n:n + 1]))
                    for k in range(4):
                        r = w_f[n][:, k * PIECE:(k + 1) * PIECE]
                        link(nc.vector.tensor_scalar(r, r, w_scale[:, n:n + 1], 1.0, ALU.mult, ALU.min))
                        link(nc.vector.tensor_scalar(r, r, -1.0, ROUND, ALU.max, ALU.add))
                        if n >= 2 and k == 0:
                            dve.wait_ge(wT_mm, NT * (n - 1))
                        nc.vector.tensor_scalar(tern[:, n % 2, k * PIECE:(k + 1) * PIECE], r, -ROUND, None, ALU.add).then_inc(tern_ready, 1)
                        dve.wait_ge(tern_ready, 4 * n + k + 1)
                    for k in range(1, NT, 2):
                        weights_out(n, k)
                for b in range(NB):
                    last = nc.vector.bn_stats(stats[0:NQ, b, :], S.X[0:NQ, b, :])
                link(last)
                for b in range(NB):
                    last = nc.vector.bn_aggr(mean_var[0:NQ, b, :], stats[0:NQ, b, :])
                link(last)
                nc.vector.tensor_scalar(std[0:NQ, :], mean_var[0:NQ, :, 1], LN_EPS, None, ALU.add).then_inc(var_ready, 1)
                dve.wait_ge(std_ready, 1)
                link(nc.vector.reciprocal(rstd[0:NQ, :], std[0:NQ, :]))

                def quantise(out, src, top, step, recip):
                    link(nc.vector.tensor_reduce(top, src, axis=AX, op=ALU.max, apply_absolute_value=True))
                    link(nc.vector.tensor_scalar(step, top, 1e-5, 1.0 / QMAX, ALU.max, ALU.mult))
                    link(nc.vector.reciprocal(recip, step))
                    link(nc.vector.tensor_scalar(src, src, recip, QMAX, ALU.mult, ALU.min))
                    link(nc.vector.tensor_scalar(src, src, -QMAX - 1.0, ROUND, ALU.max, ALU.add))
                    return nc.vector.tensor_scalar(out, src, -ROUND, None, ALU.add)

                link.enter()
                per = 12
                with dve.Fori(0, NB) as b:
                    link.loop(b, per)
                    link(nc.vector.tensor_scalar(xn[0:NQ, :].unsqueeze(1), one(S.X[0:NQ], b),
                                                 one(mean_var[0:NQ], b)[:, :, 0:1].rearrange("p a c -> p (a c)"),
                                                 one(rstd[0:NQ], b), ALU.subtract, ALU.mult))
                    quantise(xq[0:NQ, :], xn[0:NQ, :], x_max[0:NQ, :], x_step[0:NQ, :], x_scale[0:NQ, :]).then_inc(xq_ready, 1)
                    nc.vector.tensor_scalar(gu_step[0:NQ, :], w_step[0:NQ, 0:2], x_step[0:NQ, :], None, ALU.mult).then_inc(step_ready, 1)
                    dve.wait_ge(step_ready, b + 1)
                    for n in range(NPC):
                        dve.wait_ge(silu_done, b * NPC + n + 1)
                        nc.vector.scalar_tensor_tensor(out=hid[0:NQ, n * BANK:(n + 1) * BANK], in0=gu[0:NQ, 2 * (n % 2) + 1, :],
                                                       scalar=gu_step[0:NQ, 1:2], in1=sg[0:NQ, n % 2, :], op0=ALU.mult, op1=ALU.mult).then_inc(h_part, 1)
                    dve.wait_ge(h_part, FREE + b * NPC + NPC)
                    quantise(hq[0:NQ, :], hid[0:NQ, :], h_max[0:NQ, :], h_step[0:NQ, :], h_scale[0:NQ, :]).then_inc(hq_ready, 1)
                    link(nc.vector.tensor_scalar(y_step[0:NQ, :], h_step[0:NQ, :], w_step[0:NQ, 2:3], S.tanh_g[0:NQ, 2:3], ALU.mult, ALU.mult))
                    dve.wait_ge(hqT_mm, 2 * b + 2)
                    nc.vector.tensor_copy(hqT[:, 8:16, :], tbank[1][:, 0:8 * NQ].rearrange("p (k q) -> p k q", k=8)).then_inc(hqT_dve, 1)
                    dve.wait_ge(y_mm, b + 1)
                    xb = one(S.X[0:NQ], b)
                    nc.vector.scalar_tensor_tensor(out=xb, in0=ob[0:NQ, :].unsqueeze(1), scalar=y_step[0:NQ, :], in1=xb,
                                                   op0=ALU.mult, op1=ALU.add).then_inc(x_done, 1)
                link.leave(NB, per)


def mixture_stages(nc, S, gate_w, w_gate, w_up, w_down, out):
    with ExitStack() as ctx:
        m = Mem(nc, ctx, "moe")
        xinT = m.sb("xinT", [P, DC, NE, NB, CAP])
        scatter = m.sb("scatter", [2 * HALF, NB, 2, NQ])
        routing_stage(nc, S, gate_w, xinT, scatter)
        yT = m.sb("yT", [P, DC, NB, NE, CAP])
        experts_stage(nc, S, w_gate, w_up, w_down, xinT, yT)
        combine_stage(nc, S, scatter, yT, out)


HALF = NE // 2 * CAP // 2


def routing_stage(nc, S, gate_w, xinT, scatter):
    PAIRS = NB * NE
    with ExitStack() as ctx:
        m = Mem(nc, ctx, "route")
        sb, ps, sem = m.sb, m.ps, m.sem
        gw, gwT = sb("gw", [NE, D]), sb("gwT", [P, DC, NE])
        stats, mean_var = sb("stats", [P, NB, 6]), sb("mean_var", [P, NB, 2])
        std, rstd = sb("std", [P, NB]), sb("rstd", [P, NB])
        xs = sb("xs", [P, D])
        xT = sb("xT", [P, DC, NQ])
        logits = sb("logits", [P, NB, NE])
        top, total = sb("top", [P, NB]), sb("total", [P, NB])
        aff = sb("aff", [P, PAIRS])
        affT, work = sb("affT", [PAIRS, NQ]), sb("work", [PAIRS, NQ])
        best = sb("best", [PAIRS, 3, 8])
        maskT = sb("maskT", [PAIRS, NQ])
        mask, rank = sb("mask", [P, PAIRS]), sb("rank", [P, PAIRS])
        upto = sb("upto", [P, NQ])
        slot = sb("slot", [P, CAP])
        onehot = sb("onehot", [P, NB, NE * CAP])
        gated = sb("gated", [P, NB, NE * CAP])
        hot_b, gated_b = sb("hot_b", [P, NE * CAP]), sb("gated_b", [P, NE * CAP])
        tb, lb, rb, gb = (ps(n, [P, BANK]) for n in ("tb", "lb", "rb", "gb"))
        xb_ps = ps("xb_ps", [P, 2, BANK])
        (gw_in, gwT_mm, gwT_ready, xs_ready, xT_mm, xT_ready, logit_mm, logit_out, sub_done, exp_done, aff_ready, affT_mm,
         mask_ready, mask_mm, mask_out, rank_mm, hot_ready, batch_ready, gather_mm, gather_out, gatedT_mm, gatedT_out, dve_own,
         pool_own, var_ready, std_ready) = (sem(n) for n in (
             "gw_in", "gwT_mm", "gwT_ready", "xs_ready", "xT_mm", "xT_ready", "logit_mm", "logit_out", "sub_done", "exp_done",
             "aff_ready", "affT_mm", "mask_ready", "mask_mm", "mask_out", "rank_mm", "hot_ready", "batch_ready", "gather_mm",
             "gather_out", "gatedT_mm", "gatedT_out", "dve_own", "pool_own", "var_ready", "std_ready"))

        with nc.Block() as block:

            @block.sync
            def _(sp):
                sp.dma_start(gw[:], gate_w).then_inc(gw_in, 16)

            @block.gpsimd
            def _(pool):
                nc.gpsimd.memset(upto[:], 1.0).then_inc(pool_own, 1)
                pool.wait_ge(pool_own, 1)
                nc.gpsimd.affine_select(out=upto[:], in_=upto[:], compare_op=ALU.is_ge, fill=0.0, base=0,
                                        pattern=[[1, NQ]], channel_multiplier=-1).then_inc(pool_own, 1)
                nc.gpsimd.iota(slot[:], [[1, CAP]], base=1, channel_multiplier=0,
                               allow_small_or_imprecise_dtypes=True).then_inc(pool_own, 1)

            @block.tensor
            def _(pe):
                pe.sem_inc(gatedT_mm, FREE)
                pe.wait_ge(gw_in, 16)
                for c in range(DC):
                    last = nc.tensor.transpose(tb[:, c * NE:(c + 1) * NE], gw[:, c * P:(c + 1) * P], S.ident[0:NE, 0:NE])
                last.then_inc(gwT_mm, 1)
                pe.wait_ge(gwT_ready, 1)
                with pe.Fori(0, NB) as b:
                    pe.wait_ge(xs_ready, b + 1)
                    for c in range(DC):
                        last = nc.tensor.transpose(tb[:, c * NQ:(c + 1) * NQ], xs[0:NQ, c * P:(c + 1) * P], S.ident[0:NQ, 0:NQ])
                    last.then_inc(xT_mm, 1)
                    pe.wait_ge(xT_ready, b + 1)
                    pe.wait_ge(logit_out, FREE + b)
                    for c in range(DC):
                        last = nc.tensor.matmul(lb[0:NQ, 0:NE], xT[:, c, :], gwT[:, c, :], start=(c == 0), stop=(c == DC - 1))
                    last.then_inc(logit_mm, 1)
                pe.wait_ge(aff_ready, 1)
                nc.tensor.transpose(rb[0:PAIRS, 0:NQ], aff[0:NQ, :], S.ident[0:NQ, 0:NQ]).then_inc(affT_mm, 1)
                pe.wait_ge(mask_ready, 1)
                nc.tensor.transpose(lb[0:NQ, 0:PAIRS], maskT[:], S.ident[0:PAIRS, 0:PAIRS]).then_inc(mask_mm, 1)
                pe.wait_ge(mask_out, 1)
                pe.wait_ge(pool_own, 3)
                nc.tensor.matmul(rb[0:NQ, 0:PAIRS], upto[0:NQ, :], mask[0:NQ, :], start=True, stop=True).then_inc(rank_mm, 1)
                with pe.Fori(0, NB) as b:
                    pe.wait_ge(batch_ready, b + 1)
                    pe.wait_ge(gather_out, FREE + b)
                    for c in range(DC):
                        last = nc.tensor.matmul(xb_ps[:, c // 2, (c % 2) * NE * CAP:(c % 2 + 1) * NE * CAP], xs[0:NQ, c * P:(c + 1) * P],
                                                hot_b[0:NQ, :], start=True, stop=True)
                    last.then_inc(gather_mm, 1)
                    pe.wait_ge(gatedT_out, FREE + b)
                    for h in range(2):
                        last = nc.tensor.transpose(gb[0:2 * HALF, h * NQ:(h + 1) * NQ], gated_b[0:NQ, h * 2 * HALF:(h + 1) * 2 * HALF],
                                                   S.ident[0:NQ, 0:NQ])
                    last.then_inc(gatedT_mm, 1)

            @block.scalar
            def _(act):
                act.sem_inc(gatedT_out, FREE)
                act.wait_ge(var_ready, 1)
                nc.scalar.activation(std[0:NQ, :], std[0:NQ, :], ACT.Sqrt).then_inc(std_ready, 1)
                with act.Fori(0, NB) as b:
                    act.wait_ge(xT_mm, b + 1)
                    nc.scalar.copy(xT[:], tb[:, 0:DC * NQ].rearrange("p (c q) -> p c q", c=DC)).then_inc(xT_ready, 1)
                act.wait_ge(sub_done, 1)
                nc.scalar.activation(logits[0:NQ], logits[0:NQ], ACT.Exp).then_inc(exp_done, 1)
                with act.Fori(0, NB) as b:
                    act.wait_ge(gatedT_mm, FREE + b + 1)
                    nc.scalar.copy(one(scatter[:], b), gb[0:2 * HALF, 0:2 * NQ].rearrange("p (a h q) -> p a h q", a=1, h=2)).then_inc(gatedT_out, 1)

            @block.vector
            def _(dve):
                dve.sem_inc(logit_out, FREE)
                dve.sem_inc(gather_out, FREE)
                link = Chain(dve, dve_own)
                dve.wait_ge(gwT_mm, 1)
                nc.vector.tensor_copy(gwT[:], tb[:, 0:DC * NE].rearrange("p (c e) -> p c e", c=DC)).then_inc(gwT_ready, 1)
                for b in range(NB):
                    last = nc.vector.bn_stats(stats[0:NQ, b, :], S.X[0:NQ, b, :])
                link(last)
                for b in range(NB):
                    last = nc.vector.bn_aggr(mean_var[0:NQ, b, :], stats[0:NQ, b, :])
                link(last)
                nc.vector.tensor_scalar(std[0:NQ, :], mean_var[0:NQ, :, 1], LN_EPS, None, ALU.add).then_inc(var_ready, 1)
                dve.wait_ge(std_ready, 1)
                link(nc.vector.reciprocal(rstd[0:NQ, :], std[0:NQ, :]))

                def normalise(b):
                    return nc.vector.tensor_scalar(xs[0:NQ, :].unsqueeze(1), one(S.X[0:NQ], b),
                                                   one(mean_var[0:NQ], b)[:, :, 0:1].rearrange("p a c -> p (a c)"),
                                                   one(rstd[0:NQ], b), ALU.subtract, ALU.mult)

                with dve.Fori(0, NB) as b:
                    normalise(b).then_inc(xs_ready, 1)
                    dve.wait_ge(logit_mm, b + 1)
                    nc.vector.tensor_copy(one(logits[0:NQ], b), lb[0:NQ, 0:NE].unsqueeze(1)).then_inc(logit_out, 1)
                dve.wait_ge(logit_out, FREE + NB)
                link(nc.vector.tensor_reduce(top[0:NQ, :], logits[0:NQ], axis=AX, op=ALU.max))
                nc.vector.tensor_tensor(logits[0:NQ], logits[0:NQ], top[0:NQ, :].unsqueeze(2).broadcast_to([NQ, NB, NE]),
                                        ALU.subtract).then_inc(sub_done, 1)
                dve.wait_ge(exp_done, 1)
                link(nc.vector.tensor_reduce(total[0:NQ, :], logits[0:NQ], axis=AX, op=ALU.add))
                link(nc.vector.reciprocal(total[0:NQ, :], total[0:NQ, :]))
                nc.vector.tensor_tensor(aff[0:NQ, :].rearrange("p (b e) -> p b e", b=NB), logits[0:NQ],
                                        total[0:NQ, :].unsqueeze(2).broadcast_to([NQ, NB, NE]), ALU.mult).then_inc(aff_ready, 1)
                dve.wait_ge(affT_mm, 1)
                nc.vector.tensor_copy(affT[:], rb[0:PAIRS, 0:NQ])
                link(nc.vector.tensor_copy(work[:], rb[0:PAIRS, 0:NQ]))
                for k in range(CAP // 8):
                    link(nc.vector.max(best[:, k, :], work[:]))
                    link(nc.vector.match_replace(work[:], best[:, k, :], work[:], -1.0))
                nc.vector.tensor_scalar(maskT[:], work[:], 0.0, None, ALU.is_lt).then_inc(mask_ready, 1)
                dve.wait_ge(mask_mm, 1)
                nc.vector.tensor_copy(mask[0:NQ, :], lb[0:NQ, 0:PAIRS]).then_inc(mask_out, 1)
                dve.wait_ge(rank_mm, 1)
                dve.wait_ge(mask_out, 1)
                link(nc.vector.tensor_tensor(rank[0:NQ, :], rb[0:NQ, 0:PAIRS], mask[0:NQ, :], ALU.mult))
                hot = onehot[0:NQ].rearrange("p b (e s) -> p (b e) s", e=NE)
                link(nc.vector.tensor_tensor(hot, rank[0:NQ, :].unsqueeze(2).broadcast_to([NQ, PAIRS, CAP]),
                                             slot[0:NQ, :].unsqueeze(1).broadcast_to([NQ, PAIRS, CAP]), ALU.is_equal))
                link(nc.vector.tensor_tensor(gated[0:NQ].rearrange("p b (e s) -> p (b e) s", e=NE), hot,
                                             aff[0:NQ, :].unsqueeze(2).broadcast_to([NQ, PAIRS, CAP]), ALU.mult))
                with dve.Fori(0, NB) as b:
                    dve.wait_ge(gatedT_mm, FREE + b)
                    normalise(b)
                    nc.vector.tensor_copy(hot_b[0:NQ, :].unsqueeze(1), one(onehot[0:NQ], b))
                    nc.vector.tensor_copy(gated_b[0:NQ, :].unsqueeze(1), one(gated[0:NQ], b)).then_inc(batch_ready, 1)
                    dve.wait_ge(gather_mm, b + 1)
                    for c in range(DC):
                        last = nc.vector.tensor_copy(xinT[:, c, :, bass.ds(b, 1), :],
                                                     xb_ps[:, c // 2, (c % 2) * NE * CAP:(c % 2 + 1) * NE * CAP].rearrange(
                                                         "p (e a s) -> p e a s", e=NE, a=1))
                    last.then_inc(gather_out, 1)


def experts_stage(nc, S, w_gate, w_up, w_down, xinT, yT):
    IB = INNER // P
    LOAD = 4
    NL = 3 * IB // LOAD
    NSLOT = 6
    NU = IB + IB // 2
    NGRP = 2 * NU
    with ExitStack() as ctx:
        m = Mem(nc, ctx, "exp")
        sb, ps, sem = m.sb, m.ps, m.sem
        w_nat = sb("w_nat", [P, NSLOT, LOAD * D])
        wT = sb("wT", [P, 4, BANK])
        xe = sb("xe", [P, DC, SLOTS])
        sg = sb("sg", [P, 2, SLOTS])
        hT = sb("hT", [P, IB, SLOTS])
        tb = ps("tb", [P, 4, BANK])
        hb = ps("hb", [P, 2, BANK])
        yb = ps("yb", [P, 2, BANK])
        w_in = [sem(f"w_in{i}") for i in range(NSLOT)]
        (xe_ready, t_mm, wT_act, wT_dve, h_mm, silu_done, h_ready, y_mm, y_out) = (sem(n) for n in (
            "xe_ready", "t_mm", "wT_act", "wT_dve", "h_mm", "silu_done", "h_ready", "y_mm", "y_out"))

        def load_source(e, n):
            if n < 2 * IB // LOAD:
                w = (w_gate, w_up)[n % 2]
                return w[bass.ds(e, 1)].rearrange("a (o p) i -> p (a o) i", p=P)[:, (n // 2) * LOAD:(n // 2 + 1) * LOAD, :]
            return down_source(e * DC + n - 2 * IB // LOAD)

        def down_source(row):
            return w_down.rearrange("e (o p) i -> p (e o) i", p=P)[:, bass.ds(row, 1), :]

        def group_load(g):
            if g < 2 * IB:
                return 2 * (g // 2 // LOAD) + g % 2
            return 2 * IB // LOAD + (g - 2 * IB) // 4

        def last_group(n):
            return max(g for g in range(NGRP) if group_load(g) == n)

        with nc.Block() as block:

            @block.sync
            def _(sp):
                def load(e, n, row=None):
                    k = LOAD if n < 2 * IB // LOAD else 1
                    src = load_source(e, n) if row is None else down_source(row)
                    sp.dma_start(w_nat[:, n % NSLOT].rearrange("p (o i) -> p o i", o=k), src).then_inc(w_in[n % NSLOT], 16)

                for n in range(NSLOT):
                    load(0, n)
                with sp.Fori(0, NE - 1) as e:
                    down_rows = [sp.snap(e * DC + d) for d in range(DC)]
                    for n in range(NSLOT, NL + NSLOT):
                        sp.wait_ge(t_mm, e * NGRP + last_group(n - NSLOT) + 1)
                        if 2 * IB // LOAD <= n < NL:
                            load(e, n, down_rows[n - 2 * IB // LOAD])
                        elif n < NL:
                            load(e, n)
                        else:
                            load(e + 1, n - NL)
                for n in range(NSLOT, NL):
                    sp.wait_ge(t_mm, (NE - 1) * NGRP + last_group(n - NSLOT) + 1)
                    load(NE - 1, n)

            @block.tensor
            def _(pe):
                pe.sem_inc(h_mm, FREE)
                with pe.Fori(0, NE) as e:
                    def transposes(u):
                        for g in (2 * u, 2 * u + 1):
                            n = group_load(g)
                            pe.wait_ge(w_in[n % NSLOT], e * (16 * (NL // NSLOT)) + 16 * (n // NSLOT + 1))
                            done, per = (wT_act if g % 2 == 0 else wT_dve), NGRP // 2
                            pe.wait_ge(done, FREE + e * per + ((g - 4) // 2 + 1 if g >= 4 else 0))
                            for t in range(4):
                                if g < 2 * IB:
                                    at = (u % LOAD) * D + t * P
                                else:
                                    at = ((g - 2 * IB) % 4) * 4 * P + t * P
                                last = nc.tensor.transpose(tb[:, g % 4, t * P:(t + 1) * P], w_nat[:, n % NSLOT, at:at + P], S.ident[:])
                            last.then_inc(t_mm, 1)

                    def products(u):
                        pe.wait_ge(wT_act, FREE + e * (NGRP // 2) + u + 1)
                        if u < IB:
                            if u == 0:
                                pe.wait_ge(xe_ready, e + 1)
                            pe.wait_ge(h_ready, FREE + e * IB + max(u - 1, 0))
                            for k in range(2):
                                if k == 1:
                                    pe.wait_ge(wT_dve, FREE + e * (NGRP // 2) + u + 1)
                                for c in range(DC):
                                    last = nc.tensor.matmul(hb[:, u % 2, k * SLOTS:(k + 1) * SLOTS], wT[:, (2 * u + k) % 4, c * P:(c + 1) * P],
                                                            xe[:, c, :], start=(c == 0), stop=(c == DC - 1))
                            last.then_inc(h_mm, 1)
                        else:
                            d, part = (u - IB) // 2, (u - IB) % 2
                            if part == 0:
                                pe.wait_ge(h_ready, FREE + e * IB + IB)
                                pe.wait_ge(y_out, FREE + e * DC + max(d - 1, 0))
                            for k in range(2):
                                if k == 1:
                                    pe.wait_ge(wT_dve, FREE + e * (NGRP // 2) + u + 1)
                                for t in range(4):
                                    i = 8 * part + 4 * k + t
                                    last = nc.tensor.matmul(yb[:, d % 2, 0:SLOTS], wT[:, (2 * u + k) % 4, t * P:(t + 1) * P], hT[:, i, :],
                                                            start=(i == 0), stop=(i == IB - 1))
                            if part == 1:
                                last.then_inc(y_mm, 1)

                    transposes(0)
                    for u in range(NU):
                        if u + 1 < NU:
                            transposes(u + 1)
                        products(u)

            def weights_out(eng, copy, e, g, done):
                eng.wait_ge(t_mm, e * NGRP + g + 1)
                copy(wT[:, g % 4, :], tb[:, g % 4, :]).then_inc(done, 1)

            @block.scalar
            def _(act):
                act.sem_inc(wT_act, FREE)
                with act.Fori(0, NE) as e:
                    for u in range(NU + 1):
                        if u < NU:
                            weights_out(act, nc.scalar.copy, e, 2 * u, wT_act)
                        if 1 <= u <= IB:
                            k = u - 1
                            act.wait_ge(h_mm, FREE + e * IB + k + 1)
                            act.wait_ge(h_ready, FREE + e * IB + max(k - 1, 0))
                            nc.scalar.activation(sg[:, k % 2, :], hb[:, k % 2, 0:SLOTS], ACT.Silu).then_inc(silu_done, 1)

            @block.vector
            def _(dve):
                dve.sem_inc(wT_dve, FREE)
                dve.sem_inc(h_ready, FREE)
                dve.sem_inc(y_out, FREE)
                def take_tokens(e):
                    nc.vector.tensor_copy(xe[:].rearrange("p c (a n) -> p c a n", a=1),
                                          xinT[:, :, bass.ds(e, 1)].rearrange("p c a b s -> p c a (b s)")).then_inc(xe_ready, 1)

                with dve.Fori(0, NE) as e:
                    dve.wait_ge(h_mm, FREE + e * IB)
                    take_tokens(e)
                    for u in range(NU + 1):
                        if u < NU:
                            weights_out(dve, nc.vector.tensor_copy, e, 2 * u + 1, wT_dve)
                        if 1 <= u <= IB:
                            k = u - 1
                            dve.wait_ge(silu_done, e * IB + k + 1)
                            nc.vector.tensor_tensor(hT[:, k, :], hb[:, k % 2, SLOTS:2 * SLOTS], sg[:, k % 2, :], ALU.mult).then_inc(h_ready, 1)
                        if u > IB and (u - IB) % 2 == 0:
                            d = (u - IB) // 2 - 1
                            dve.wait_ge(y_mm, e * DC + d + 1)
                            nc.vector.tensor_copy(yT[:, d, :, bass.ds(e, 1), :],
                                                  yb[:, d % 2, 0:SLOTS].rearrange("p (b a s) -> p b a s", b=NB, a=1)).then_inc(y_out, 1)


def combine_stage(nc, S, scatter, yT, out):
    with ExitStack() as ctx:
        m = Mem(nc, ctx, "comb")
        sb, ps, sem = m.sb, m.ps, m.sem
        K = 2 * HALF
        y_b = sb("y_b", [P, DC, 2 * K])
        scat_b = sb("scat_b", [K, 2, NQ])
        y_nat = sb("y_nat", [K, 2, D])
        res = sb("res", [P, 2, D])
        tb = ps("tb", [P, 2, BANK])
        ob = ps("ob", [P, BANK])
        batch_ready, yT_mm, y_act, y_dve, o_mm, res_ready = (sem(n) for n in ("batch_ready", "yT_mm", "y_act", "y_dve", "o_mm", "res_ready"))
        out_done = [sem("out_done0"), sem("out_done1")]
        with nc.Block() as block:

            @block.vector
            def _(dve):
                dve.sem_inc(res_ready, FREE)
                with dve.Fori(0, NB // 2) as b2:
                    for r in range(2):
                        b = b2 * 2 + r
                        nc.vector.tensor_copy(y_b[:].rearrange("p c (a n) -> p c a n", a=1),
                                              yT[:, :, bass.ds(b, 1)].rearrange("p c a e s -> p c a (e s)"))
                        nc.vector.tensor_copy(scat_b[:].unsqueeze(1), one(scatter[:], b)).then_inc(batch_ready, 1)
                        dve.wait_ge(yT_mm, b2 * 4 + 2 * r + 2)
                        nc.vector.tensor_copy(y_nat[:, 1, :], tb[0:K, 1, :]).then_inc(y_dve, 1)
                        dve.wait_ge(o_mm, b2 * 2 + r + 1)
                        dve.wait_ge(out_done[r], 16 * FREE + b2 * 16)
                        nc.vector.scalar_tensor_tensor(out=res[0:NQ, r, :].unsqueeze(1), in0=ob[0:NQ, :].unsqueeze(1), scalar=S.tanh_g[0:NQ, 3:4],
                                                       in1=one(S.X[0:NQ], b), op0=ALU.mult, op1=ALU.add).then_inc(res_ready, 1)

            @block.scalar
            def _(act):
                act.sem_inc(out_done[0], 16 * FREE)
                act.sem_inc(out_done[1], 16 * FREE)
                with act.Fori(0, NB // 2) as b2:
                    for r in range(2):
                        act.wait_ge(yT_mm, b2 * 4 + 2 * r + 1)
                        nc.scalar.copy(y_nat[:, 0, :], tb[0:K, 0, :]).then_inc(y_act, 1)
                        act.wait_ge(res_ready, FREE + b2 * 2 + r + 1)
                        act.dma_start(out[bass.ds(b2 * 2 + r, 1)].rearrange("a q d -> q (a d)"), res[0:NQ, r, :]).then_inc(out_done[r], 16)
                act.wait_ge(out_done[0], 16 * FREE + 16 * (NB // 2))
                act.wait_ge(out_done[1], 16 * FREE + 16 * (NB // 2))

            @block.tensor
            def _(pe):
                with pe.Fori(0, NB) as b:
                    pe.wait_ge(batch_ready, b + 1)
                    for h in range(2):
                        for c in range(DC):
                            last = nc.tensor.transpose(tb[0:K, h, c * P:(c + 1) * P], y_b[:, c, h * K:(h + 1) * K], S.ident[:])
                        last.then_inc(yT_mm, 1)
                    pe.wait_ge(y_act, b + 1)
                    pe.wait_ge(res_ready, FREE + b)
                    nc.tensor.matmul(ob[0:NQ, :], scat_b[:, 0, :], y_nat[:, 0, :], start=True, stop=False)
                    pe.wait_ge(y_dve, b + 1)
                    nc.tensor.matmul(ob[0:NQ, :], scat_b[:, 1, :], y_nat[:, 1, :], start=False, stop=True).then_inc(o_mm, 1)


def flamingo(nc, x, ctx_1024, g_xattn, g_ffn, a0, f0, a1, mlp, f1, out):
    with ExitStack() as ctx:
        S = start_state(nc, ctx)
        setup_stage(nc, S, x, g_xattn, g_ffn)
        attention_stage(nc, S, 0, ctx_1024, *a0)
        quantised_stage(nc, S, *f0)
        attention_stage(nc, S, 1, ctx_1024, *a1, mlp=mlp)
        mixture_stages(nc, S, *f1, out)


_A0 = ["L0_xattn_" + n for n in ("wq_w", "wq_b", "wk_w", "wk_b", "wv_w", "wv_b", "dense_w", "dense_b")]
_F0 = ["L0_ffn_" + n for n in ("w_gate", "w_up", "w_down")]
_A1 = ["L1_xattn_" + n for n in ("Wq", "bq", "Wk", "bk", "Wv", "bv", "Wo", "bo")]
_MLP = ["L1_xattn_" + n for n in ("w1", "b1", "w2", "b2", "w3", "b3")]
_F1 = ["L1_ffn_" + n for n in ("gate_w", "w_gate", "w_up", "w_down")]


def kernel(**inputs):
    import numpy as _np
    import concourse.bacc as _bacc
    from concourse import mybir as _mybir
    from concourse.bass_utils import run_bass_kernel_spmd as _run

    nc = _bacc.Bacc("TRN2", target_bir_lowering=False, num_devices=1)
    arrays, args = {}, {}
    for name in ["x", "ctx_1024", "g_xattn", "g_ffn"] + _A0 + _F0 + _A1 + _MLP + _F1:
        a = _np.ascontiguousarray(inputs[name])
        arrays[f"in_{name}_dram"] = a
        args[name] = nc.dram_tensor(f"in_{name}_dram", a.shape, _mybir.dt.from_np(a.dtype), kind="ExternalInput").ap()
    out = nc.dram_tensor("out_0_dram", (NB, NQ, D), F32, kind="ExternalOutput").ap()
    flamingo(nc, args["x"], args["ctx_1024"], args["g_xattn"], args["g_ffn"], *([args[n] for n in g] for g in (_A0, _F0, _A1, _MLP, _F1)), out)
    r = _run(nc, [arrays], core_ids=[0])
    return r.results[0]["out_0_dram"]
```

```python
from contextlib import ExitStack

import concourse.bass as bass
from concourse import mybir

F32 = mybir.dt.float32
F32R = mybir.dt.float32r
BF16 = mybir.dt.bfloat16
ALU = mybir.AluOpType
ACT = mybir.ActivationFunctionType
AX = mybir.AxisListType.X

P = 128
NB, NQ, D = 8, 100, 512
NK = 722
NH, DH = 16, 32
DC = D // P
HPC = P // DH
KC = (NK + P - 1) // P
KFULL = NK // P
KREST = NK - KFULL * P
KHALF = NK // 2
KEVEN = KHALF + KHALF % 2
NKPAD = KHALF + KEVEN
BANK = 512
INNER = 2048
NE = 8
CAP = NQ // NE * 2
SLOTS = NB * CAP
LN_EPS = 1e-5
ROUND = 12582912.0
QMAX = 127.0
LOG_T_MIN, LOG_T_MAX = -2.302585092994046, 2.302585092994046


FREE = 1


def ksize(j):
    return P if j < KFULL else KREST


SPLIT = ((0, 0), (0, 1), (1, 0))


def one(ap, i):
    return ap[:, bass.ds(i, 1)]


def rows(v):
    return v.rearrange("(a n) -> a n", a=1)


def spread(v, n):
    return rows(v).broadcast_to([n, v.shape[0]])


class Mem:

    def __init__(self, nc, ctx, tag):
        self.nc, self.ctx, self.tag, self.sems = nc, ctx, tag, []
        ctx.callback(self.leave)

    def leave(self):
        if self.sems:
            self.nc.clear_and_free_semaphores(self.sems)
            self.nc.all_engine_barrier()

    def sb(self, name, shape, dt=F32):
        return self.ctx.enter_context(self.nc.sbuf_tensor(f"{self.tag}_{name}", shape, dt))

    def ps(self, name, shape, dt=F32):
        return self.ctx.enter_context(self.nc.psum_tensor(f"{self.tag}_{name}", shape, dt))

    def sem(self, name):
        self.sems.append(self.nc.alloc_semaphore(f"{self.tag}_{name}"))
        return self.sems[-1]


class Chain:

    def __init__(self, eng, sem):
        self.eng, self.sem, self.n, self.base = eng, sem, 0, 0

    def __call__(self, ins):
        ins.then_inc(self.sem, 1)
        self.n += 1
        self.eng.wait_ge(self.sem, self.base + self.n)

    def loop(self, i, per):
        self.base, self.n = self.before + i * per, 0

    def enter(self):
        self.before, self.n, self.base = self.n, 0, 0

    def leave(self, passes, per):
        if self.n != per:
            raise ValueError(f"{self.n} results in a pass, {per} were said")
        self.base, self.n = 0, self.before + passes * per


def setup_stage(nc, S, x, g_xattn, g_ffn, following):
    with ExitStack() as ctx:
        m = Mem(nc, ctx, "setup")
        gates = m.sb("gates", [P, 4])
        x_in, ident_zero, ident_done, gates_done = (m.sem(n) for n in ("x_in", "ident_zero", "ident_done", "gates_done"))
        with nc.Block() as block:

            @block.sync
            def _(sp):
                sp.dma_start(gates[:, 0:2], spread(g_xattn, P)).then_inc(x_in, 16)
                sp.dma_start(gates[:, 2:4], spread(g_ffn, P)).then_inc(x_in, 16)
                sp.dma_start(S.X[0:NQ], x.rearrange("b q d -> q b d")).then_inc(x_in, 16)
                S.load_room(sp, following)
                sp.wait_ge(x_in, 48)

            @block.gpsimd
            def _(pool):
                nc.gpsimd.memset(S.ident[:], 0.0).then_inc(ident_zero, 1)
                nc.gpsimd.memset(S.ones[:], 1.0).then_inc(ident_zero, 1)
                pool.wait_ge(ident_zero, 2)
                nc.gpsimd.affine_select(out=S.ident[:], in_=S.ident[:], compare_op=ALU.not_equal, fill=1.0,
                                        base=0, pattern=[[-1, P]], channel_multiplier=1).then_inc(ident_done, 1)

            @block.vector
            def _(dve):
                dve.wait_ge(ident_done, 1)
                nc.vector.tensor_copy(S.identb[:], S.ident[:]).then_inc(gates_done, 1)

            @block.scalar
            def _(act):
                act.wait_ge(x_in, 48)
                nc.scalar.activation(S.tanh_g[:], gates[:], ACT.Tanh).then_inc(gates_done, 1)


def attention_stage(nc, S, layer, ctx_dram, wq, bq, wk, bk, wv, bv, wo, bo, mlp=None, following=()):
    L1 = mlp is not None
    tag = f"at{layer}"
    with ExitStack() as ctx:
        m = Mem(nc, ctx, tag)
        sb, ps, sem = m.sb, m.ps, m.sem
        woT = sb("woT", [P, DC, D])
        wkT, wvT = sb("wkT", [P, 2, DC, D], F32R), sb("wvT", [P, 2, DC, D], F32R)
        bias_q, bias_k, bias_v = (sb(f"bias_{n}", [P, DC]) for n in "qkv")
        bias_o = sb("bias_o", [P, D])
        stats, mean_var = sb("stats", [P, NB, 6]), sb("mean_var", [P, NB, 2])
        std, rstd = sb("std", [P, NB]), sb("rstd", [P, NB])
        xn = sb("xn", [P, 2, D])
        ctx_nat = sb("ctx_nat", [P, KC, D])
        ctxT = sb("ctxT", [P, 2, DC, NKPAD], F32R)
        QT = sb("QT", [P, DC, NQ])
        q_dram = nc.dram_tensor(f"{tag}_queries", (NB, P, DC * NQ), F32, kind="Internal").ap()
        Qm = sb("Qm", [P, 2, DC, HPC, NQ], F32R)
        KT = sb("KT", [P, 2, DC, NKPAD], F32R)
        V = sb("V", [P, KC, D])
        group = sb("group", [P, HPC])
        head_rows = sb("head_rows", [NH, D])
        QB = NB // 2
        LAG = 3
        NP = NH if L1 else LAG + 2
        n_w, n_q = 3 * DC * D, DC * QB * NQ
        w_nat = [S.place(n) for n in range(3)]
        q_room = S.room[:, n_w:n_w + n_q]
        xnT = S.room[:, n_w + n_q:n_w + 3 * n_q].rearrange("p (c n) -> p c n", c=DC)
        at = 0 if L1 else n_w + n_q
        probs = S.room[:, at:at + NP * NK].rearrange("p (h k) -> p h k", h=NP)
        probsT = sb("probsT", [P, 2, KC, NQ])
        neg_max, denom, rdenom = (sb(n, [P, NH]) for n in ("neg_max", "denom", "rdenom"))
        rdenT, OT = sb("rdenT", [NH, NQ]), sb("OT", [P, DC, NQ])
        ksum = sb("ksum", [P, DC, 2])
        wqT = V[:, 0:DC, :]
        if L1:
            w1, b1, w2, b2, w3, b3 = mlp
            DM = w1.shape[0]
            scores = probs
            v_bias = sb("v_bias", [P, DC, NQ])
            junk = [probsT[0:NQ].rearrange("p a j q -> p (a j q)")[:, 0:NK], xn[0:NQ].rearrange("p a d -> p (a d)")[:, 0:NK]]
            maxs, denom1, sqsum, varr = (sb(n, [P, NH]) for n in ("maxs", "denom1", "sqsum", "varr"))
            qsum, ksum1, qk4 = sb("qsum", [P, NB, DC]), sb("ksum1", [P, DC]), sb("qk4", [P, DC])
            qk_heads = sb("qk_heads", [P, DC, HPC])
            w1_all = probsT[:, 0].rearrange("p j q -> p (j q)")[:, 0:3 * DM].rearrange("p (o j) -> p o j", j=3)
            w1_scaled = sb("w1_scaled", [P, 3, DM])
            w2_nat, w2T = sb("w2_nat", [DM, DM]), sb("w2T", [DM, P])
            w3_col, w3_all = sb("w3_col", [DM, 1]), sb("w3_all", [DM, P])
            b1_col, b2_col, b3_all = sb("b1_col", [DM, 1]), sb("b2_col", [DM, 1]), sb("b3_all", [P, 1])
            hid1, hid2 = sb("hid1", [DM, NH]), sb("hid2", [DM, NH])
            log_t, inv_t, ratio, bias2 = (sb(n, [P, NH]) for n in ("log_t", "inv_t", "ratio", "bias2"))
        Q_half = [q_room.rearrange("p (b c q) -> p b c q", b=QB, c=DC), xnT[:, :, 0:QB * NQ].rearrange("p c (b q) -> p b c q", b=QB)]
        wide = ps("wide", [P, 4, BANK])
        tb = ps("tb", [P, 2, BANK])
        ob = ps("ob", [P, BANK])
        mb = ps("mb", [P, BANK])

        w_in = list(S.loads)
        wo_in = w_in[0] + 16
        S.loads[0] += 16
        whigh_ready, wT_ready, wT_copied, wT_mm = (sem(n) for n in ("whigh_ready", "wT_ready", "wT_copied", "wT_mm"))
        small_in, ctx_in, dve_own = (sem(n) for n in ("small_in", "ctx_in", "dve_own"))
        var_ready, std_ready, pre_done = (sem(n) for n in ("var_ready", "std_ready", "pre_done"))
        xn_ready, xnT_mm, xnT_ready, q_mm, q_out = (sem(n) for n in ("xn_ready", "xnT_mm", "xnT_ready", "q_mm", "q_out"))
        front_mm, high_done, front_out = (sem(n) for n in ("front_mm", "high_done", "front_out"))
        q_stored, q_in, pads_done, bias_added = (sem(n) for n in ("q_stored", "q_in", "pads_done", "bias_added"))
        qhigh_done, qm_ready = sem("qhigh_done"), sem("qm_ready")
        v_mm, v_act, v_dve = (sem(n) for n in ("v_mm", "v_act", "v_dve"))
        score_mm, max_ready, exp_done = (sem(n) for n in ("score_mm", "max_ready", "exp_done"))
        rd_ready, rdT_mm, rdT_ready, rdR_mm = (sem(n) for n in ("rd_ready", "rdT_mm", "rdT_ready", "rdR_mm"))
        pT_mm0, pT_mm1, pT_act, pT_dve = (sem(n) for n in ("pT_mm0", "pT_mm1", "pT_act", "pT_dve"))
        pv_mm, ot_ready, y_mm, x_done, group_own, rows_own = (sem(n) for n in ("pv_mm", "ot_ready", "y_mm", "x_done", "group_own", "rows_own"))
        if L1:
            first_exp, square_act, square_dve, score_out, stat_ready, h1_mm, h1_act, h2_mm, h2_act, t_mm, clip_ready, inv_ready, ratio_ready = (
                sem(n) for n in ("first_exp", "square_act", "square_dve", "score_out", "stat_ready", "h1_mm", "h1_act", "h2_mm", "h2_act", "t_mm", "clip_ready",
                                 "inv_ready", "ratio_ready"))
            w2_mm = sem("w2_mm")
        S_FREE = score_out if L1 else exp_done
        NSMALL = 4 + (6 if L1 else 0)
        NF = KC + 2 * DC
        QG = 2 * DC
        sizes = [ksize(j) for j in range(KC)]
        HALVES = (3, KC - 3)
        scale = float(DH) ** -0.5
        K_PARTS = [(g, i) for g in range(KC, NF) for i in range(DC)]
        if L1:
            FRONT = {-4: [(g, DC - 1) for g in range(4)], -3: [(g, DC - 1) for g in range(4, KC)], -1: K_PARTS[0:8]}
            for h in range(NH - 1):
                FRONT[h] = K_PARTS[8 + h * 18 // (NH - 1):8 + (h + 1) * 18 // (NH - 1)]
            FRONT[NH] = K_PARTS[26:]
        else:
            FRONT = {k: [(3 * k + n, DC - 1) for n in range(3)] for k in range(2)}
            FRONT[2], FRONT[3], FRONT[4] = K_PARTS[0:4], K_PARTS[4:10], K_PARTS[10:]

        V_AFTER = {4: (0,), 8: (1,), 12: (2,), NH: (3, 4)}

        def front_units(step):
            return [g for g, i in FRONT.get(step, ()) if i == DC - 1]

        with nc.Block() as block:

            @block.sync
            def _(sp):
                def load_ctx(b):
                    src = ctx_dram[bass.ds(b, 1)].rearrange("a k d -> (a k) d")
                    sp.dma_start(ctx_nat[:, 0:KFULL], src[0:KFULL * P].rearrange("(j p) d -> p j d", p=P)).then_inc(ctx_in, 16)
                    sp.dma_start(ctx_nat[0:KREST, KFULL], src[KFULL * P:NK]).then_inc(ctx_in, 16)

                for bias, col in ((bq, bias_q), (bk, bias_k), (bv, bias_v)):
                    sp.dma_start(col[:], bias.rearrange("(c p) -> p c", p=P), allow_slow_non_contiguous=True).then_inc(small_in, 16)
                sp.dma_start(bias_o[:], spread(bo, P)).then_inc(small_in, 16)
                if L1:
                    sp.dma_start(w1_all[:], w1.rearrange("(a o) j -> a o j", a=1).broadcast_to([P, DM, 3])).then_inc(small_in, 16)
                    sp.dma_start(w2_nat[:], w2).then_inc(small_in, 16)
                    sp.dma_start(w3_col[:], w3.rearrange("a d -> d a"), allow_slow_non_contiguous=True).then_inc(small_in, 16)
                    sp.dma_start(b1_col[:], b1.rearrange("(d a) -> d a", a=1), allow_slow_non_contiguous=True).then_inc(small_in, 16)
                    sp.dma_start(b2_col[:], b2.rearrange("(d a) -> d a", a=1), allow_slow_non_contiguous=True).then_inc(small_in, 16)
                    sp.dma_start(b3_all[:], spread(b3, P)).then_inc(small_in, 16)
                load_ctx(0)
                sp.wait_ge(wT_mm, DC)
                sp.dma_start(w_nat[0], square(wo)).then_inc(S.room_in[0], 16)
                for half in range(2):
                    sp.wait_ge(q_out, DC * (half + 1))
                    for b in range(QB):
                        sp.dma_start(q_dram[half * QB + b].rearrange("p (c q) -> p c q", c=DC), Q_half[half][:, b]).then_inc(q_stored, 16)
                sp.wait_ge(q_stored, 16 * NB)

                def load_queries(b):
                    sp.dma_start(QT[:].rearrange("p c q -> p (c q)"), q_dram[bass.ds(b, 1)].rearrange("a p n -> p (a n)")).then_inc(q_in, 16)

                load_queries(0)
                if following:
                    sp.wait_ge(wT_mm, 4 * DC)
                    S.load_room(sp, following)
                with sp.Fori(0, NB - 1) as b:
                    sp.wait_ge(front_mm, b * NF + KC)
                    load_ctx(b + 1)
                    sp.wait_ge(qm_ready, b + 1)
                    load_queries(b + 1)
                sp.wait_ge(ctx_in, 32 * NB)
                sp.wait_ge(q_in, 16 * NB)

            @block.tensor
            def _(pe):
                pe.sem_inc(pT_mm1, FREE)
                pe.sem_inc(pv_mm, FREE)
                pe.sem_inc(xnT_mm, 2 * FREE)
                def transpose_weights(n):
                    pe.wait_ge(S.room_in[n % 3], w_in[n] if n < 3 else wo_in)
                    for i in range(DC):
                        if n == 2:
                            pe.wait_ge(q_out, DC + i + 1)
                        elif n == 1:
                            pe.wait_ge(wT_copied, i + 1)
                        elif n == 3:
                            pe.wait_ge(wT_ready, DC + i + 1)
                        for o in range(DC):
                            last = nc.tensor.transpose(wide[:, i, o * P:(o + 1) * P], w_nat[n % 3][:, o, i * P:(i + 1) * P], S.ident[:])
                        last.then_inc(wT_mm, 1)

                transpose_weights(0)
                with pe.Fori(0, NB // 2) as b2:
                    for r in range(2):
                        pe.wait_ge(xn_ready, b2 * 2 + r + 1)
                        pe.wait_ge(xnT_ready, FREE + b2 * 2 + max(r - 1, 0))
                        for c in range(DC):
                            last = nc.tensor.transpose(tb[:, r, c * NQ:(c + 1) * NQ], xn[0:NQ, r, c * P:(c + 1) * P], S.ident[0:NQ, 0:NQ])
                        last.then_inc(xnT_mm, 1)

                transpose_weights(1)
                if L1:
                    pe.wait_ge(small_in, 16 * NSMALL)
                    nc.tensor.transpose(mb[0:DM, 0:DM], w2_nat[:], S.ident[0:DM, 0:DM]).then_inc(w2_mm, 1)
                pe.wait_ge(wT_copied, DC)
                pe.wait_ge(xnT_ready, FREE + NB)
                for g in range(QG):
                    if g < 4:
                        pe.wait_ge(wT_ready, g + 1)
                    else:
                        pe.wait_ge(q_out, g - 4 + 1)
                    half, o = g // DC, g % DC
                    for i in range(DC):
                        last = nc.tensor.matmul(wide[:, g % 4, 0:QB * NQ], wqT[:, i, o * P:(o + 1) * P], xnT[:, i, half * QB * NQ:(half + 1) * QB * NQ],
                                                start=(i == 0), stop=(i == DC - 1))
                    last.then_inc(q_mm, 1)
                transpose_weights(2)
                transpose_weights(3)
                pe.wait_ge(wT_ready, 2 * DC)
                pe.wait_ge(wT_copied, 2 * DC)

                def front(b, g, part, first=False):
                    if g >= KC and part > 0:
                        pass
                    elif g >= 4:
                        pe.wait_ge(front_out, b * NF + g - 4 + 1)
                    elif not first:
                        pe.wait_ge(S_FREE, b * NH)
                    if g < KC:
                        if g == 0:
                            pe.wait_ge(ctx_in, 32 * b + 32)
                        for c in range(DC):
                            last = nc.tensor.transpose(wide[:, g % 4, c * P:c * P + sizes[g]],
                                                       ctx_nat[0:sizes[g], g, c * P:(c + 1) * P], S.ident[0:sizes[g], 0:sizes[g]])
                    else:
                        if g == KC and part == 0:
                            pe.wait_ge(front_out, b * NF + KC)
                        o, half = (g - KC) // 2, (g - KC) % 2
                        for n, (sw, sc) in enumerate(SPLIT):
                            last = nc.tensor.matmul(wide[:, g % 4, 0:KEVEN], wkT[:, sw, part, o * P:(o + 1) * P],
                                                    ctxT[:, sc, part, half * KHALF:half * KHALF + KEVEN],
                                                    start=(part == 0 and n == 0), stop=(part == DC - 1 and n == 2))
                    if part == DC - 1:
                        last.then_inc(front_mm, 1)

                def batch(b, final):

                    def next_front(step):
                        if not final:
                            for g, part in FRONT.get(step, ()):
                                front(b + 1, g, part)

                    def values(j, parts=range(DC)):
                        if parts[0] > 0:
                            pass
                        elif j < 2:
                            pe.wait_ge(pT_act if j == 0 else pT_dve, FREE + b * NH)
                        else:
                            pe.wait_ge(v_act if j % 2 == 0 else v_dve, b * 3 + j // 2)
                        for i in parts:
                            for n, (sc, sw) in enumerate(SPLIT):
                                last = nc.tensor.matmul(tb[0:sizes[j], j % 2, :], ctxT[:, sc, i, j * P:j * P + sizes[j]], wvT[:, sw, i, :],
                                                        start=(i == 0 and n == 0), stop=(i == DC - 1 and n == 2))
                        if parts[-1] == DC - 1:
                            last.then_inc(v_mm, 1)

                    def score(h):
                        if h < 2:
                            pe.wait_ge(qm_ready, b + 1)
                            pe.wait_ge(front_out, b * NF + NF)
                        else:
                            pe.wait_ge(S_FREE, b * NH + h - 1)
                        c, r = h // HPC, h % HPC
                        for half in range(2):
                            for n, (sq, sk) in enumerate(SPLIT):
                                last = nc.tensor.matmul(wide[0:NQ, 2 * (h % 2) + half, 0:KEVEN], Qm[:, sq, c, r, :],
                                                        KT[:, sk, c, half * KHALF:half * KHALF + KEVEN], start=(n == 0), stop=(n == 2))
                        last.then_inc(score_mm, 1)

                    def transpose_probs(h):
                        pe.wait_ge(exp_done, b * NH + h + 1)
                        for half, mm in enumerate((pT_mm0, pT_mm1)):
                            if h == 0:
                                pe.wait_ge(v_act if half == 0 else v_dve, b * 3 + 3)
                            else:
                                pe.wait_ge(pT_act if half == 0 else pT_dve, FREE + b * NH + h)
                            for t in range(HALVES[half]):
                                j = half * HALVES[0] + t
                                last = nc.tensor.transpose(tb[0:sizes[j], half, t * NQ:(t + 1) * NQ],
                                                           probs[0:NQ, h % NP, j * P:j * P + sizes[j]], S.ident[0:NQ, 0:NQ])
                            last.then_inc(mm, 1)

                    def weigh_values(h):
                        pe.wait_ge(pT_act, FREE + b * NH + h + 1)
                        pe.wait_ge(pT_dve, FREE + b * NH + h + 1)
                        if h == 0:
                            pe.wait_ge(x_done, FREE + b)
                        c, r = h // HPC, DH * (h % HPC)
                        for j in range(KC):
                            last = nc.tensor.matmul(ob[r:r + DH, c * NQ:(c + 1) * NQ], V[0:sizes[j], j, h * DH:(h + 1) * DH],
                                                    probsT[0:sizes[j], h % 2, j, :], start=(j == 0), stop=(j == KC - 1))
                        if h == NH - 1:
                            last.then_inc(pv_mm, 1)

                    def transpose_rdenom():
                        pe.wait_ge(rd_ready, b + 1)
                        nc.tensor.transpose(mb[0:NH, 0:NQ], rdenom[0:NQ, :], S.ident[0:NQ, 0:NQ]).then_inc(rdT_mm, 1)

                    def spread_rdenom():
                        pe.wait_ge(rdT_ready, b + 1)
                        for c in range(DC):
                            last = nc.tensor.matmul(mb[:, c * NQ:(c + 1) * NQ], head_rows[:, c * P:(c + 1) * P], rdenT[:], start=True, stop=True)
                        last.then_inc(rdR_mm, 1)

                    if not L1:
                        values(0)
                        score(0)
                        score(1)
                        for j in range(1, KC):
                            values(j)
                        for h in range(2, NH + LAG + 1):
                            if h < NH:
                                score(h)
                            if LAG <= h < NH + LAG:
                                transpose_probs(h - LAG)
                            if h > LAG:
                                weigh_values(h - LAG - 1)
                            if h == NH + 1:
                                transpose_rdenom()
                            if h == NH + 2:
                                spread_rdenom()
                            next_front(h - NH)
                    else:
                        for h in range(NH):
                            score(h)
                            values(h // DC, range(h % DC, h % DC + 1))
                        values(KC - 2)
                        next_front(-4)
                        pe.wait_ge(stat_ready, b + 1)
                        nc.tensor.matmul(mb[0:DM, 0:NH], w1_scaled[:, 0, :], qk_heads[:].rearrange("p c g -> p (c g)"), start=True, stop=False)
                        nc.tensor.matmul(mb[0:DM, 0:NH], w1_scaled[0:NQ, 1, :], maxs[0:NQ, :], start=False, stop=False)
                        nc.tensor.matmul(mb[0:DM, 0:NH], w1_scaled[0:NQ, 2, :], varr[0:NQ, :], start=False, stop=True).then_inc(h1_mm, 1)
                        values(KC - 1)
                        pe.wait_ge(h1_act, b + 1)
                        nc.tensor.matmul(mb[0:P, 0:NH], w2T[:], hid1[:], start=True, stop=True).then_inc(h2_mm, 1)
                        next_front(-3)
                        pe.wait_ge(h2_act, b + 1)
                        nc.tensor.matmul(mb[0:P, 0:NH], w3_all[:], hid2[:], start=True, stop=True).then_inc(t_mm, 1)
                        next_front(-1)
                        for h in range(NH + 1):
                            if h < NH:
                                transpose_probs(h)
                            if h == NH - 1:
                                transpose_rdenom()
                            if h >= 1:
                                weigh_values(h - 1)
                            if h == NH - 1:
                                spread_rdenom()
                            next_front(h)

                    pe.wait_ge(ot_ready, b + 1)
                    for c in range(DC):
                        last = nc.tensor.matmul(ob[0:NQ, :], OT[:, c, :], woT[:, c, :], start=(c == 0), stop=(c == DC - 1))
                    last.then_inc(y_mm, 1)
                    if not L1:
                        next_front(4)

                for g in range(NF):
                    for part in (range(DC) if g >= KC else (DC - 1,)):
                        front(0, g, part, first=True)
                pe.wait_ge(rows_own, 3)
                pe.wait_ge(pre_done, 2 if L1 else 1)
                with pe.Fori(0, NB - 1) as b:
                    batch(b, False)
                batch(NB - 1, True)

            @block.scalar
            def _(act):
                act.sem_inc(pT_act, FREE)
                act.sem_inc(xnT_ready, FREE)
                if L1:
                    act.sem_inc(square_act, FREE)
                    act.sem_inc(square_dve, FREE)

                def weights_out(n, wT):
                    for i in range(DC):
                        act.wait_ge(wT_mm, DC * n + i + 1)
                        nc.scalar.copy(wT[:, i, :], wide[:, i, :]).then_inc(wT_copied if n in (0, 3) else whigh_ready, 1)

                weights_out(0, wqT)
                act.wait_ge(var_ready, 1)
                nc.scalar.activation(std[0:NQ, :], std[0:NQ, :], ACT.Sqrt).then_inc(std_ready, 1)
                with act.Fori(0, NB // 2) as b2:
                    for r in range(2):
                        act.wait_ge(xnT_mm, 2 * FREE + b2 * 2 + r + 1)
                        nc.scalar.copy(xnT.rearrange("p c (b r q) -> p b r c q", r=2, q=NQ)[:, bass.ds(b2, 1), r],
                                       tb[:, r, 0:DC * NQ].rearrange("p (a c q) -> p a c q", a=1, c=DC)).then_inc(xnT_ready, 1)
                weights_out(1, wkT[:, 0])
                weights_out(2, wvT[:, 0])
                weights_out(3, woT)

                def front(b, g, first=False):
                    act.wait_ge(front_mm, b * NF + g + 1)
                    bank = wide[:, g % 4, :]
                    if g == 0 and first:
                        act.wait_ge(pads_done, 1)
                    if g < KC:
                        nc.scalar.copy(ctxT[:, 0, :, g * P:g * P + sizes[g]],
                                       bank.rearrange("p (c k) -> p c k", c=DC)[:, :, 0:sizes[g]]).then_inc(high_done, 1)
                    else:
                        o, half = (g - KC) // 2, (g - KC) % 2
                        nc.scalar.activation(KT[:, 0, o, half * KHALF:(half + 1) * KHALF], bank[:, 0:KHALF], ACT.Identity,
                                             bias=bias_k[:, o:o + 1], accum_out=ksum[:, o, half:half + 1]).then_inc(high_done, 1)

                def batch(b, final):

                    def next_front(step):
                        if not final:
                            for g in front_units(step):
                                front(b + 1, g)

                    def values_out(j):
                        act.wait_ge(v_mm, b * KC + j + 1)
                        nc.scalar.copy(V[0:sizes[j], j, :], tb[0:sizes[j], j % 2, :]).then_inc(v_act, 1)

                    def probsT_out(h):
                        act.wait_ge(pT_mm0, b * NH + h + 1)
                        nc.scalar.activation(probsT[:, h % 2, 0:HALVES[0], :], tb[:, 0, 0:HALVES[0] * NQ].rearrange("p (j q) -> p j q", j=HALVES[0]),
                                             ACT.Relu if L1 else ACT.Copy).then_inc(pT_act, 1)

                    if not L1:
                        values_out(0)
                        for h in range(NH + LAG + 1):
                            if h == 2:
                                for j in range(2, KC, 2):
                                    values_out(j)
                            if LAG <= h < NH + LAG:
                                probsT_out(h - LAG)
                            if h < NH:
                                act.wait_ge(max_ready, b * NH + h + 1)
                                act.wait_ge(pT_mm1, FREE + b * NH + max(h - NP + 1, 0))
                                nc.scalar.activation(probs[0:NQ, h % NP, :].rearrange("p (s k) -> p s k", s=2),
                                                     wide[0:NQ, 2 * (h % 2):2 * (h % 2) + 2, 0:KHALF], ACT.Exp,
                                                     bias=neg_max[0:NQ, h:h + 1], accum_out=denom[0:NQ, h:h + 1]).then_inc(exp_done, 1)
                            next_front(h - NH)
                        next_front(4)
                    else:
                        act.wait_ge(pv_mm, FREE + b)
                        for h in range(NH + 1):
                            if h < NH:
                                act.wait_ge(max_ready, b * NH + h + 1)
                                act.wait_ge(square_dve if h % 2 == 0 else square_act, FREE + b * (NH // 2) + h // 2)
                                nc.scalar.activation(junk[h % 2], scores[0:NQ, h, :], ACT.Exp, bias=neg_max[0:NQ, h:h + 1],
                                                     accum_out=denom1[0:NQ, h:h + 1]).then_inc(first_exp, 1)
                            if h % 2 == 1:
                                act.wait_ge(first_exp, b * NH + h + 1)
                                nc.scalar.activation(junk[1], junk[1], ACT.Square, accum_out=sqsum[0:NQ, h:h + 1]).then_inc(square_act, 1)
                            for j in V_AFTER.get(h, ()):
                                if j % 2 == 0:
                                    values_out(j)
                        next_front(-4)
                        act.wait_ge(h1_mm, b + 1)
                        nc.scalar.activation(hid1[:], mb[0:DM, 0:NH], ACT.Gelu, bias=b1_col[:]).then_inc(h1_act, 1)
                        act.wait_ge(h2_mm, b + 1)
                        nc.scalar.activation(hid2[:], mb[0:DM, 0:NH], ACT.Gelu, bias=b2_col[:]).then_inc(h2_act, 1)
                        next_front(-3)
                        act.wait_ge(clip_ready, b + 1)
                        nc.scalar.activation(inv_t[0:NQ, :], log_t[0:NQ, :], ACT.Exp, scale=-1.0).then_inc(inv_ready, 1)
                        act.wait_ge(ratio_ready, b + 1)
                        AHEAD = 2
                        for h in range(NH):
                            for k in range(h + AHEAD - 1 if h else 0, min(h + AHEAD, NH)):
                                nc.scalar.activation(probs[0:NQ, k, :], scores[0:NQ, k, :], ACT.Exp, bias=bias2[0:NQ, k:k + 1],
                                                     scale=ratio[0:NQ, k:k + 1], accum_out=denom[0:NQ, k:k + 1]).then_inc(exp_done, 1)
                            next_front(h - 1)
                            probsT_out(h)
                        next_front(NH - 1)
                        next_front(NH)

                for g in range(NF):
                    front(0, g, first=True)
                with act.Fori(0, NB - 1) as b:
                    batch(b, False)
                batch(NB - 1, True)

            @block.gpsimd
            def _(pool):
                for n in range(2):
                    nc.gpsimd.memset(ctxT[:, n, :, NK:NKPAD].bitcast(F32), 0.0)
                    last = nc.gpsimd.memset(KT[:, n, :, NK:NKPAD].bitcast(F32), 0.0)
                last.then_inc(pads_done, 1)
                nc.gpsimd.memset(group[:], 1.0).then_inc(group_own, 1)
                pool.wait_ge(group_own, 1)
                nc.gpsimd.affine_select(out=group[:], in_=group[:], compare_op=ALU.is_ge, fill=0.0, base=0,
                                        pattern=[[-DH, HPC]], channel_multiplier=1).then_inc(group_own, 1)
                pool.wait_ge(group_own, 2)
                nc.gpsimd.affine_select(out=group[:], in_=group[:], compare_op=ALU.is_ge, fill=0.0, base=DH - 1,
                                        pattern=[[DH, HPC]], channel_multiplier=-1).then_inc(group_own, 1)
                nc.gpsimd.memset(head_rows[:], 1.0).then_inc(rows_own, 1)
                pool.wait_ge(rows_own, 1)
                nc.gpsimd.affine_select(out=head_rows[:], in_=head_rows[:], compare_op=ALU.is_ge, fill=0.0, base=0,
                                        pattern=[[1, D]], channel_multiplier=-DH).then_inc(rows_own, 1)
                pool.wait_ge(rows_own, 2)
                nc.gpsimd.affine_select(out=head_rows[:], in_=head_rows[:], compare_op=ALU.is_ge, fill=0.0, base=DH - 1,
                                        pattern=[[-1, D]], channel_multiplier=DH).then_inc(rows_own, 1)

                pool.wait_ge(xn_ready, NB)
                pool.wait_ge(pre_done, 1)
                nc.gpsimd.tensor_tensor(S.X[0:NQ], S.X[0:NQ], bias_o[0:NQ, :].unsqueeze(1).broadcast_to([NQ, NB, D]), ALU.add).then_inc(bias_added, 1)

            @block.vector
            def _(dve):
                dve.sem_inc(pT_dve, FREE)
                dve.sem_inc(x_done, FREE)
                link = Chain(dve, dve_own)
                for b in range(NB):
                    last = nc.vector.bn_stats(stats[0:NQ, b, :], S.X[0:NQ, b, :])
                link(last)
                for b in range(NB):
                    last = nc.vector.bn_aggr(mean_var[0:NQ, b, :], stats[0:NQ, b, :])
                link(last)
                nc.vector.tensor_scalar(std[0:NQ, :], mean_var[0:NQ, :, 1], LN_EPS, None, ALU.add).then_inc(var_ready, 1)
                dve.wait_ge(std_ready, 1)
                link(nc.vector.reciprocal(rstd[0:NQ, :], std[0:NQ, :]))
                with dve.Fori(0, NB // 2) as b2:
                    for r in range(2):
                        b = b2 * 2 + r
                        dve.wait_ge(xnT_mm, b2 * 2 + r + 1)
                        nc.vector.tensor_scalar(xn[0:NQ, r, :].unsqueeze(1), one(S.X[0:NQ], b), one(mean_var[0:NQ], b)[:, :, 0:1].rearrange("p a c -> p (a c)"),
                                                one(rstd[0:NQ], b), ALU.subtract, ALU.mult).then_inc(xn_ready, 1)

                def weights_out(n, w):
                    for i in range(DC):
                        dve.wait_ge(whigh_ready, DC * (n - 1) + i + 1)
                        nc.vector.tensor_tensor(w[:, 1, i, :], wide[:, i, :], w[:, 0, i, :].bitcast(F32), ALU.subtract).then_inc(wT_ready, 1)

                dve.wait_ge(small_in, 16 * NSMALL)
                link(nc.vector.tensor_scalar(bias_q[:], bias_q[:], scale, None, ALU.mult))
                weights_out(1, wkT)
                for g in range(QG):
                    half, o = g // DC, g % DC
                    dve.wait_ge(q_mm, g + 1)
                    nc.vector.tensor_scalar(Q_half[half][:, :, o, :], wide[:, g % 4, 0:QB * NQ].rearrange("p (b q) -> p b q", b=QB),
                                            scale, bias_q[:, o:o + 1], ALU.mult, ALU.add).then_inc(q_out, 1)
                    if g == DC:
                        last = nc.vector.tensor_scalar(bias_o[:], bias_o[:], S.tanh_g[:, layer:layer + 1], None, ALU.mult)
                        if L1:
                            for j, f in enumerate((1.0 / (NQ * NK), 1.0 / NQ, 1.0 / NQ)):
                                nc.vector.tensor_scalar(w1_scaled[:, j, :], w1_all[:, :, j], f, None, ALU.mult)
                            last = nc.vector.tensor_copy(w3_all[:], w3_col[:].broadcast_to([DM, P]))
                        last.then_inc(pre_done, 1)
                        dve.wait_ge(pre_done, 1)
                        if L1:
                            dve.wait_ge(w2_mm, 1)
                            nc.vector.memset(w2T[:, DM:P], 0.0)
                            nc.vector.tensor_copy(w2T[:, 0:DM], mb[0:DM, 0:DM]).then_inc(pre_done, 1)
                weights_out(2, wvT)

                def front(b, g):
                    dve.wait_ge(high_done, b * NF + g + 1)
                    bank = wide[:, g % 4, :]
                    if g < KC:
                        k = slice(g * P, g * P + sizes[g])
                        nc.vector.tensor_tensor(ctxT[:, 1, :, k], bank.rearrange("p (c k) -> p c k", c=DC)[:, :, 0:sizes[g]],
                                                ctxT[:, 0, :, k].bitcast(F32), ALU.subtract).then_inc(front_out, 1)
                    else:
                        o, half = (g - KC) // 2, (g - KC) % 2
                        k = slice(half * KHALF, (half + 1) * KHALF)
                        nc.vector.scalar_tensor_tensor(out=KT[:, 1, o, k], in0=bank[:, 0:KHALF], scalar=bias_k[:, o:o + 1],
                                                       in1=KT[:, 0, o, k].bitcast(F32), op0=ALU.add, op1=ALU.subtract).then_inc(front_out, 1)
                        r = g - KC - 1
                        if 0 <= r < HPC:
                            if r == 0:
                                dve.wait_ge(q_in, 16 * b + 16)
                            nc.vector.tensor_scalar(Qm[:, 0, :, r, :], QT[:], group[:, r:r + 1], None, ALU.mult).then_inc(qhigh_done, 1)
                            dve.wait_ge(qhigh_done, b * HPC + r + 1)
                            last = nc.vector.scalar_tensor_tensor(out=Qm[:, 1, :, r, :], in0=QT[:], scalar=group[:, r:r + 1],
                                                                  in1=Qm[:, 0, :, r, :].bitcast(F32), op0=ALU.mult, op1=ALU.subtract)
                            if r == HPC - 1:
                                last.then_inc(qm_ready, 1)

                def batch(b, final):

                    def next_front(step):
                        if not final:
                            for g in front_units(step):
                                front(b + 1, g)

                    def values_out(j):
                        dve.wait_ge(v_mm, b * KC + j + 1)
                        nc.vector.tensor_copy(V[0:sizes[j], j, :], tb[0:sizes[j], j % 2, :]).then_inc(v_dve, 1)

                    def probsT_out(h):
                        dve.wait_ge(pT_mm1, FREE + b * NH + h + 1)
                        nc.vector.tensor_scalar(probsT[:, h % 2, HALVES[0]:KC, :], tb[:, 1, 0:HALVES[1] * NQ].rearrange("p (j q) -> p j q", j=HALVES[1]),
                                                0.0, None, ALU.max).then_inc(pT_dve, 1)

                    def invert_denom():
                        dve.wait_ge(exp_done, b * NH + NH)
                        link(nc.vector.reciprocal(rdenom[0:NQ, :], denom[0:NQ, :]))
                        nc.vector.tensor_scalar(rdenom[0:NQ, :], rdenom[0:NQ, :], 0.0, None, ALU.max).then_inc(rd_ready, 1)

                    def rdenT_out():
                        dve.wait_ge(rdT_mm, b + 1)
                        nc.vector.tensor_copy(rdenT[:], mb[0:NH, 0:NQ]).then_inc(rdT_ready, 1)

                    def spread_out():
                        dve.wait_ge(rdR_mm, b + 1)
                        link(nc.vector.tensor_copy(OT[:], mb[:, 0:DC * NQ].rearrange("p (c q) -> p c q", c=DC)))
                        if L1:
                            link(nc.vector.scalar_tensor_tensor(out=v_bias[:], in0=OT[:], scalar=0.0, in1=bias_v[:].unsqueeze(2).broadcast_to([P, DC, NQ]),
                                                                op0=ALU.is_gt, op1=ALU.mult))

                    if not L1:
                        for h in range(NH + LAG + 1):
                            if h == NH + 3:
                                spread_out()
                            if h == 2:
                                for j in range(1, KC, 2):
                                    values_out(j)
                            if h < NH:
                                dve.wait_ge(score_mm, b * NH + h + 1)
                                nc.vector.tensor_reduce(neg_max[0:NQ, h:h + 1].unsqueeze(2), wide[0:NQ, 2 * (h % 2):2 * (h % 2) + 2, 0:KHALF],
                                                        axis=mybir.AxisListType.XY, op=ALU.max, negate=True).then_inc(max_ready, 1)
                            if LAG <= h < NH + LAG:
                                probsT_out(h - LAG)
                            if h == NH:
                                invert_denom()
                            if h == NH + 1:
                                rdenT_out()
                            if h < NH + 3:
                                next_front(h - NH)
                    else:
                        def square(h):
                            dve.wait_ge(first_exp, b * NH + h + 1)
                            nc.vector.tensor_tensor_reduce(junk[0], junk[0], junk[0], 1.0, 0.0, ALU.mult, ALU.add,
                                                           sqsum[0:NQ, h:h + 1]).then_inc(square_dve, 1)

                        for h in range(NH + 1):
                            if h < NH:
                                dve.wait_ge(score_mm, b * NH + h + 1)
                                nc.vector.tensor_scalar(scores[0:NQ, h, :].rearrange("p (s k) -> p s k", s=2),
                                                        wide[0:NQ, 2 * (h % 2):2 * (h % 2) + 2, 0:KHALF], 0.0, -3.0e38,
                                                        ALU.add, ALU.max, accum_out=maxs[0:NQ, h:h + 1]).then_inc(score_out, 1)
                            if h >= 1:
                                dve.wait_ge(score_out, b * NH + h)
                                nc.vector.tensor_scalar(neg_max[0:NQ, h - 1:h], maxs[0:NQ, h - 1:h], -1.0, None, ALU.mult).then_inc(max_ready, 1)
                            if h % 2 == 0 and h >= 2:
                                square(h - 2)
                            if h == 3:
                                link(nc.vector.tensor_reduce(ksum1[:], ksum[:], axis=AX, op=ALU.add))
                                link(nc.vector.tensor_tensor(qk4[:].unsqueeze(1), one(qsum[:], b), ksum1[:].unsqueeze(1), ALU.mult))
                                link(nc.vector.tensor_tensor(qk_heads[:], qk4[:].unsqueeze(2).broadcast_to([P, DC, HPC]),
                                                             group[:].unsqueeze(1).broadcast_to([P, DC, HPC]), ALU.mult))
                            for j in V_AFTER.get(h, ()):
                                if j % 2 == 1:
                                    values_out(j)
                        dve.wait_ge(square_act, FREE + (b + 1) * (NH // 2))
                        dve.wait_ge(square_dve, FREE + (b + 1) * (NH // 2))
                        link(nc.vector.reciprocal(denom1[0:NQ, :], denom1[0:NQ, :]))
                        link(nc.vector.tensor_tensor(sqsum[0:NQ, :], sqsum[0:NQ, :], denom1[0:NQ, :], ALU.mult))
                        link(nc.vector.tensor_tensor(sqsum[0:NQ, :], sqsum[0:NQ, :], denom1[0:NQ, :], ALU.mult))
                        nc.vector.tensor_scalar(varr[0:NQ, :], sqsum[0:NQ, :], -1.0 / NK, 1.0 / (NK - 1), ALU.add, ALU.mult).then_inc(stat_ready, 1)
                        next_front(-4)
                        values_out(KC - 1)
                        next_front(-3)
                        dve.wait_ge(t_mm, b + 1)
                        link(nc.vector.tensor_scalar(log_t[0:NQ, :], mb[0:NQ, 0:NH], b3_all[0:NQ, :], LOG_T_MIN, ALU.add, ALU.max))
                        nc.vector.tensor_scalar(log_t[0:NQ, :], log_t[0:NQ, :], LOG_T_MAX, None, ALU.min).then_inc(clip_ready, 1)
                        dve.wait_ge(inv_ready, b + 1)
                        link(nc.vector.tensor_scalar(ratio[0:NQ, :], inv_t[0:NQ, :], 0.5 * float(DH) ** 0.5, None, ALU.mult))
                        nc.vector.tensor_tensor(bias2[0:NQ, :], neg_max[0:NQ, :], ratio[0:NQ, :], ALU.mult).then_inc(ratio_ready, 1)
                        for h in range(NH):
                            if h == NH - 2:
                                invert_denom()
                            probsT_out(h)
                            if h == NH - 1:
                                rdenT_out()
                            next_front(h - 1)
                        spread_out()

                    dve.wait_ge(pv_mm, FREE + b + 1)
                    link(nc.vector.tensor_tensor(OT[:], ob[:, 0:DC * NQ].rearrange("p (c q) -> p c q", c=DC), OT[:], ALU.mult))
                    nc.vector.tensor_tensor(OT[:], OT[:], v_bias[:] if L1 else bias_v[:].unsqueeze(2).broadcast_to([P, DC, NQ]), ALU.add).then_inc(ot_ready, 1)
                    if L1:
                        next_front(NH - 1)
                        next_front(NH)
                    else:
                        next_front(3)
                    dve.wait_ge(y_mm, b + 1)
                    dve.wait_ge(bias_added, 1)
                    xb = one(S.X[0:NQ], b)
                    nc.vector.scalar_tensor_tensor(out=xb, in0=ob[0:NQ, :].unsqueeze(1), scalar=S.tanh_g[0:NQ, layer:layer + 1], in1=xb,
                                                   op0=ALU.mult, op1=ALU.add).then_inc(x_done, 1)
                    if not L1:
                        next_front(4)

                dve.wait_ge(group_own, 3)
                for g in range(NF):
                    front(0, g)
                if L1:
                    dve.wait_ge(q_out, QG)
                    for half in range(2):
                        last = nc.vector.tensor_reduce(qsum[:, half * QB:(half + 1) * QB], Q_half[half], axis=AX, op=ALU.add)
                    link(last)
                link.enter()
                per = 3 + (3 + 3 + 2 + 1 if L1 else 0)
                with dve.Fori(0, NB - 1) as b:
                    link.loop(b, per)
                    batch(b, False)
                link.leave(NB - 1, per)
                batch(NB - 1, True)


class State:

    def load_room(self, sp, sources):
        for n, src in enumerate(sources):
            sp.dma_start(self.place(n), src).then_inc(self.room_in[n], 16)
            self.loads[n] += 16

    def place(self, n):
        return self.room[:, n * DC * D:(n + 1) * DC * D].rearrange("p (o i) -> p o i", o=DC)


def square(w):
    return w.rearrange("(o p) i -> p o i", p=P)


def start_state(nc, ctx):
    S = State()
    m = Mem(nc, ctx, "all")
    S.X = m.sb("x", [P, NB, D])
    S.ident = m.sb("ident", [P, P])
    S.identb = m.sb("identb", [P, P], BF16)
    S.ones = m.sb("ones", [P, P])
    S.room = m.sb("room", [P, NH * NK])
    S.room_in = [m.sem(f"room_in{n}") for n in range(3)]
    S.loads = [0, 0, 0]
    S.tanh_g = m.sb("tanh_g", [P, 4])
    return S


def quantised_stage(nc, S, w_gate, w_up, w_down, following):
    with ExitStack() as ctx:
        m = Mem(nc, ctx, "ffn0")
        sb, ps, sem = m.sb, m.ps, m.sem
        RB = INNER // P
        PIECE = 4 * D
        w_f = [S.room[:, 0:RB * D], sb("w_odd", [P, RB * D])]
        w_f.append(w_f[0])
        tern = sb("tern", [P, 2, RB * D], BF16)
        gateT = sb("gateT", [P, DC, INNER], BF16)
        upT = sb("upT", [P, DC, INNER], BF16)
        downT = sb("downT", [P, RB, D], BF16)
        abs_part, abs_sum = sb("abs_part", [P, 3, 4]), sb("abs_sum", [P, 3])
        w_step, w_scale = sb("w_step", [P, 3]), sb("w_scale", [P, 3])
        stats, mean_var = sb("stats", [P, NB, 6]), sb("mean_var", [P, NB, 2])
        std, rstd = sb("std", [P, NB]), sb("rstd", [P, NB])
        xn, xq = sb("xn", [P, D]), sb("xq", [P, D], BF16)
        xqT = sb("xqT", [P, DC, NQ], BF16)
        x_max, x_step, x_scale = sb("x_max", [P, 1]), sb("x_step", [P, 1]), sb("x_scale", [P, 1])
        gu_step = sb("gu_step", [P, 2])
        sg, hid, hz = sb("sg", [P, 2, BANK]), sb("hid", [P, INNER]), sb("hz", [P, INNER])
        hq = sb("hq", [P, INNER], BF16)
        junk = hz
        hqT = sb("hqT", [P, RB, NQ], BF16)
        h_max, h_step, h_scale, y_step = (sb(n, [P, 1]) for n in ("h_max", "h_step", "h_scale", "y_step"))

        tbank = [ps(f"tbank{i}", [P, 2 * BANK], BF16) for i in range(2)]
        gu = ps("gu", [P, 4, BANK])
        ob = ps("ob", [P, BANK])
        mb = ps("mb", [P, BANK])

        gate_in = list(S.loads)
        w_in = [[sem(f"w_in{n}_{k}") if n or k == 3 else None for k in range(4)] for n in range(3)]
        (abs_done, part_sum, sum_mm, tern_ready, wT_mm, wT_act, wT_dve, dve_own, var_ready, std_ready) = (sem(n) for n in (
            "abs_done", "part_sum", "sum_mm", "tern_ready", "wT_mm", "wT_act", "wT_dve", "dve_own", "var_ready", "std_ready"))
        (xq_ready, xqT_mm, xqT_ready, gu_mm, silu_done, h_part, hq_ready, hqT_mm, hqT_out, y_mm, x_done, step_ready) = (sem(n) for n in (
            "xq_ready", "xqT_mm", "xqT_ready", "gu_mm", "silu_done", "h_part", "hq_ready", "hqT_mm", "hqT_out", "y_mm",
            "x_done", "step_ready"))
        NT = RB * D // (2 * BANK)
        NPC = INNER // BANK

        def matrix_part(n, k):
            if n < 2:
                return (gateT, upT)[n][:, k // 2, (k % 2) * 2 * BANK:(k % 2 + 1) * 2 * BANK]
            return downT[:, 2 * k:2 * k + 2, :].rearrange("p k n -> p (k n)")

        with nc.Block() as block:

            @block.sync
            def _(sp):
                sp.dma_start(S.place(3), square(w_gate[3 * D:4 * D])).then_inc(w_in[0][3], 16)
                for k in range(4):
                    sp.dma_start(w_f[1][:, k * PIECE:(k + 1) * PIECE].rearrange("p (o i) -> p o i", i=D),
                                 square(w_up[k * D:(k + 1) * D])).then_inc(w_in[1][k], 16)
                for k in range(4):
                    sp.wait_ge(tern_ready, k + 1)
                    sp.dma_start(w_f[2][:, k * PIECE:(k + 1) * PIECE], w_down[k * P:(k + 1) * P]).then_inc(w_in[2][k], 16)
                sp.wait_ge(tern_ready, 12)
                S.load_room(sp, following)

            @block.tensor
            def _(pe):
                def sum_partitions(n):
                    pe.wait_ge(part_sum, n + 1)
                    nc.tensor.matmul(mb[:, n:n + 1], S.ones[:], abs_sum[:, n:n + 1], start=True, stop=True).then_inc(sum_mm, 1)

                sum_partitions(0)
                for n in range(3):
                    if n < 2:
                        sum_partitions(n + 1)
                    pe.wait_ge(tern_ready, 4 * (n + 1))
                    for k in range(NT):
                        count = NT * n + k
                        if n == 2 and k >= 2:
                            pe.wait_ge(wT_act if k % 2 == 0 else wT_dve, (2 * NT if k % 2 == 0 else 0) + k // 2)
                        elif count >= 2:
                            pe.wait_ge(wT_act, count - 1)
                        for t in range(8):
                            if n < 2:
                                row, col = 8 * (k % 2) + t, k // 2
                                src = tern[:, n % 2, row * D + col * P:row * D + (col + 1) * P]
                            else:
                                row, col = t % 4, 2 * k + t // 4
                                src = tern[:, n % 2, row * INNER + col * P:row * INNER + (col + 1) * P]
                            last = nc.tensor.transpose(tbank[k % 2][:, t * P:(t + 1) * P], src, S.identb[:])
                        last.then_inc(wT_mm, 1)
                pe.wait_ge(wT_act, 2 * NT + NT // 2)
                pe.wait_ge(wT_dve, NT // 2)

                def hidden(b, before=0):
                    pe.wait_ge(xq_ready, b + 1)
                    pe.wait_ge(hqT_out, FREE + 2 * before)
                    for c in range(DC):
                        last = nc.tensor.transpose(tbank[0][:, c * P:c * P + NQ], xq[0:NQ, c * P:(c + 1) * P], S.identb[0:NQ, 0:NQ])
                    last.then_inc(xqT_mm, 1)
                    pe.wait_ge(xqT_ready, b + 1)
                    for n in range(NPC):
                        pe.wait_ge(h_part, FREE + b * NPC + max(n - 1, 0))
                        for k, wT in enumerate((gateT, upT)):
                            for c in range(DC):
                                last = nc.tensor.matmul(gu[0:NQ, 2 * (n % 2) + k, :], xqT[:, c, :], wT[:, c, n * BANK:(n + 1) * BANK],
                                                        start=(c == 0), stop=(c == DC - 1))
                        last.then_inc(gu_mm, 1)

                def down(b):
                    pe.wait_ge(hq_ready, b + 1)
                    for half in range(2):
                        pe.wait_ge(hqT_out, FREE + 2 * b)
                        for t in range(8):
                            last = nc.tensor.transpose(tbank[half][:, t * NQ:(t + 1) * NQ],
                                                       hq[0:NQ, (8 * half + t) * P:(8 * half + t + 1) * P], S.identb[0:NQ, 0:NQ])
                        last.then_inc(hqT_mm, 1)
                    pe.wait_ge(x_done, FREE + b)
                    for k in range(RB):
                        if k % 8 == 0:
                            pe.wait_ge(hqT_out, FREE + 2 * b + k // 8 + 1)
                        last = nc.tensor.matmul(ob[0:NQ, :], hqT[:, k, :], downT[:, k, :], start=(k == 0), stop=(k == RB - 1))
                    last.then_inc(y_mm, 1)

                hidden(0)
                with pe.Fori(0, NB - 1) as b:
                    hidden(b + 1, b)
                    down(b)
                down(NB - 1)

            @block.scalar
            def _(act):
                act.sem_inc(hqT_out, FREE)

                def weights_out(n, k):
                    act.wait_ge(wT_mm, NT * n + k + 1)
                    nc.scalar.copy(matrix_part(n, k), tbank[k % 2][:]).then_inc(wT_act, 1)

                for n in range(3):
                    for k in range(4):
                        if n == 0 and k < 3:
                            act.wait_ge(S.room_in[k], gate_in[k])
                        else:
                            act.wait_ge(w_in[n][k], 16)
                        if 4 * n + k >= 1:
                            act.wait_ge(abs_done, 4 * n + k)
                        nc.scalar.activation(junk[:], w_f[n][:, k * PIECE:(k + 1) * PIECE], ACT.Abs,
                                             accum_out=abs_part[:, n, k:k + 1]).then_inc(abs_done, 1)
                    if n == 0:
                        act.wait_ge(var_ready, 1)
                        nc.scalar.activation(std[0:NQ, :], std[0:NQ, :], ACT.Sqrt).then_inc(std_ready, 1)
                    else:
                        for k in range(NT):
                            weights_out(n - 1, k)
                for k in range(0, NT, 2):
                    weights_out(2, k)

                def hidden(b):
                    act.wait_ge(xqT_mm, b + 1)
                    nc.scalar.copy(xqT[:], tbank[0][:, 0:DC * P].rearrange("p (c k) -> p c k", c=DC)[:, :, 0:NQ]).then_inc(xqT_ready, 1)
                    act.wait_ge(step_ready, b + 1)
                    for n in range(NPC):
                        act.wait_ge(gu_mm, b * NPC + n + 1)
                        act.wait_ge(h_part, FREE + b * NPC + max(n - 1, 0))
                        nc.scalar.activation(sg[0:NQ, n % 2, :], gu[0:NQ, 2 * (n % 2), :], ACT.Silu, scale=gu_step[0:NQ, 0:1]).then_inc(silu_done, 1)

                def down(b):
                    for half in range(2):
                        act.wait_ge(hqT_mm, 2 * b + half + 1)
                        if half == 0:
                            act.wait_ge(y_mm, FREE + b)
                        nc.scalar.copy(hqT[:, 8 * half:8 * half + 8, :], tbank[half][:, 0:8 * NQ].rearrange("p (k q) -> p k q", k=8)).then_inc(hqT_out, 1)

                hidden(0)
                with act.Fori(0, NB - 1) as b:
                    hidden(b + 1)
                    down(b)
                down(NB - 1)

            @block.vector
            def _(dve):
                dve.sem_inc(x_done, FREE)
                dve.sem_inc(y_mm, FREE)
                dve.sem_inc(h_part, FREE)
                link = Chain(dve, dve_own)

                def weights_out(n, k):
                    dve.wait_ge(wT_mm, NT * n + k + 1)
                    nc.vector.tensor_copy(matrix_part(n, k), tbank[k % 2][:]).then_inc(wT_dve, 1)

                for b in range(NB):
                    last = nc.vector.bn_stats(stats[0:NQ, b, :], S.X[0:NQ, b, :])
                link(last)
                for b in range(NB):
                    last = nc.vector.bn_aggr(mean_var[0:NQ, b, :], stats[0:NQ, b, :])
                link(last)
                nc.vector.tensor_scalar(std[0:NQ, :], mean_var[0:NQ, :, 1], LN_EPS, None, ALU.add).then_inc(var_ready, 1)
                def steps(src, top, step, recip):
                    link(nc.vector.tensor_reduce(top, src, axis=AX, op=ALU.max, apply_absolute_value=True))
                    link(nc.vector.tensor_scalar(step, top, 1e-5, 1.0 / QMAX, ALU.max, ALU.mult))
                    link(nc.vector.reciprocal(recip, step))

                def quantise_rows(b):
                    link(nc.vector.tensor_scalar(xn[0:NQ, :].unsqueeze(1), one(S.X[0:NQ], b),
                                                 one(mean_var[0:NQ], b)[:, :, 0:1].rearrange("p a c -> p (a c)"),
                                                 one(rstd[0:NQ], b), ALU.subtract, ALU.mult))
                    steps(xn[0:NQ, :], x_max[0:NQ, :], x_step[0:NQ, :], x_scale[0:NQ, :])
                    link(nc.vector.tensor_scalar(xn[0:NQ, :], xn[0:NQ, :], x_scale[0:NQ, :], QMAX, ALU.mult, ALU.min))
                    link(nc.vector.tensor_scalar(xn[0:NQ, :], xn[0:NQ, :], -QMAX - 1.0, ROUND, ALU.max, ALU.add))
                    nc.vector.tensor_scalar(xq[0:NQ, :], xn[0:NQ, :], -ROUND, None, ALU.add).then_inc(xq_ready, 1)
                    nc.vector.tensor_scalar(gu_step[0:NQ, :], w_step[0:NQ, 0:2], x_step[0:NQ, :], None, ALU.mult).then_inc(step_ready, 1)

                def hidden_part(b, n):
                    dve.wait_ge(step_ready, b + 1)
                    dve.wait_ge(silu_done, b * NPC + n + 1)
                    nc.vector.scalar_tensor_tensor(out=hid[0:NQ, n * BANK:(n + 1) * BANK], in0=gu[0:NQ, 2 * (n % 2) + 1, :],
                                                   scalar=gu_step[0:NQ, 1:2], in1=sg[0:NQ, n % 2, :], op0=ALU.mult, op1=ALU.mult).then_inc(h_part, 1)

                def batch(b, left):
                    dve.wait_ge(h_part, FREE + b * NPC + NPC)
                    steps(hid[0:NQ, :], h_max[0:NQ, :], h_step[0:NQ, :], h_scale[0:NQ, :])
                    link(nc.vector.tensor_scalar(hz[0:NQ, :], hid[0:NQ, :], h_scale[0:NQ, :], QMAX, ALU.mult, ALU.min))
                    if left >= 1:
                        hidden_part(b + 1, 0)
                    link(nc.vector.tensor_scalar(hz[0:NQ, :], hz[0:NQ, :], -QMAX - 1.0, ROUND, ALU.max, ALU.add))
                    if left >= 1:
                        hidden_part(b + 1, 1)
                    nc.vector.tensor_scalar(hq[0:NQ, :], hz[0:NQ, :], -ROUND, None, ALU.add).then_inc(hq_ready, 1)
                    link(nc.vector.tensor_scalar(y_step[0:NQ, :], h_step[0:NQ, :], w_step[0:NQ, 2:3], S.tanh_g[0:NQ, 2:3], ALU.mult, ALU.mult))
                    if left >= 1:
                        hidden_part(b + 1, 2)
                        hidden_part(b + 1, 3)
                    if left >= 2:
                        dve.wait_ge(h_part, FREE + (b + 2) * NPC)
                        quantise_rows(b + 2)
                    dve.wait_ge(y_mm, FREE + b + 1)
                    xb = one(S.X[0:NQ], b)
                    nc.vector.scalar_tensor_tensor(out=xb, in0=ob[0:NQ, :].unsqueeze(1), scalar=y_step[0:NQ, :], in1=xb,
                                                   op0=ALU.mult, op1=ALU.add).then_inc(x_done, 1)

                for n in range(3):
                    dve.wait_ge(abs_done, 4 * (n + 1))
                    nc.vector.tensor_reduce(abs_sum[:, n:n + 1], abs_part[:, n, :], axis=AX, op=ALU.add).then_inc(part_sum, 1)
                    dve.wait_ge(sum_mm, n + 1)
                    link(nc.vector.tensor_scalar(w_step[:, n:n + 1], mb[:, n:n + 1], 1.0 / (INNER * D), 1e-5, ALU.mult, ALU.max))
                    link(nc.vector.reciprocal(w_scale[:, n:n + 1], w_step[:, n:n + 1]))
                    for k in range(4):
                        r = w_f[n][:, k * PIECE:(k + 1) * PIECE]
                        link(nc.vector.tensor_scalar(r, r, w_scale[:, n:n + 1], 1.0, ALU.mult, ALU.min))
                        link(nc.vector.tensor_scalar(r, r, -1.0, ROUND, ALU.max, ALU.add))
                        if n >= 2 and k == 0:
                            dve.wait_ge(wT_mm, NT * (n - 1))
                        nc.vector.tensor_scalar(tern[:, n % 2, k * PIECE:(k + 1) * PIECE], r, -ROUND, None, ALU.add).then_inc(tern_ready, 1)
                        dve.wait_ge(tern_ready, 4 * n + k + 1)
                    if n == 0:
                        dve.wait_ge(std_ready, 1)
                        link(nc.vector.reciprocal(rstd[0:NQ, :], std[0:NQ, :]))
                quantise_rows(0)
                for k in range(1, NT, 2):
                    weights_out(2, k)
                for n in range(NPC):
                    hidden_part(0, n)
                dve.wait_ge(h_part, FREE + NPC)
                quantise_rows(1)
                link.enter()
                per = 6 + 6
                with dve.Fori(0, NB - 2) as b:
                    link.loop(b, per)
                    batch(b, 2)
                link.leave(NB - 2, per)
                batch(NB - 2, 1)
                batch(NB - 1, 0)


def mixture_stages(nc, S, gate_w, w_gate, w_up, w_down, out):
    with ExitStack() as ctx:
        m = Mem(nc, ctx, "moe")
        xinT = m.sb("xinT", [P, DC, NE, NB, CAP])
        scatter = m.sb("scatter", [2 * HALF, NB, 2, NQ])
        W = ExpertWeights(m, S, w_gate, w_up, w_down)
        routing_stage(nc, S, gate_w, xinT, scatter, W)
        yT = m.sb("yT", [P, DC, NB, NE, CAP])
        experts_stage(nc, S, W, xinT, yT)
        combine_stage(nc, S, scatter, yT, out)


HALF = NE // 2 * CAP // 2


IB = INNER // P
LOAD = 4
NL = 3 * IB // LOAD
NSLOT = 6


class ExpertWeights:

    def __init__(self, m, S, w_gate, w_up, w_down):
        self.w_gate, self.w_up, self.w_down = w_gate, w_up, w_down
        size = LOAD * D
        self.places = [S.room[:, n * size:(n + 1) * size] for n in range(NSLOT - 1)] + [m.sb("w_last", [P, size])[:]]
        self.w_in = [m.sem(f"w_in{i}") for i in range(NSLOT)]

    def down_source(self, row):
        return self.w_down.rearrange("e (o p) i -> p (e o) i", p=P)[:, bass.ds(row, 1), :]

    def load(self, sp, e, n, row=None):
        if n < 2 * IB // LOAD:
            w, k = (self.w_gate, self.w_up)[n % 2], LOAD
            src = w[bass.ds(e, 1)].rearrange("a (o p) i -> p (a o) i", p=P)[:, (n // 2) * LOAD:(n // 2 + 1) * LOAD, :]
        else:
            src, k = self.down_source(e * DC + n - 2 * IB // LOAD if row is None else row), 1
        sp.dma_start(self.places[n % NSLOT].rearrange("p (o i) -> p o i", o=k), src).then_inc(self.w_in[n % NSLOT], 16)


def routing_stage(nc, S, gate_w, xinT, scatter, W):
    PAIRS = NB * NE
    with ExitStack() as ctx:
        m = Mem(nc, ctx, "route")
        sb, ps, sem = m.sb, m.ps, m.sem
        gw, gwT = sb("gw", [NE, D]), sb("gwT", [P, DC, NE])
        stats, mean_var = sb("stats", [P, NB, 6]), sb("mean_var", [P, NB, 2])
        std, rstd = sb("std", [P, NB]), sb("rstd", [P, NB])
        xs = sb("xs", [P, 2, D])
        xT = sb("xT", [P, 2, DC, NQ])
        logits = sb("logits", [P, NB, NE])
        top, total = sb("top", [P, NB]), sb("total", [P, NB])
        aff = sb("aff", [P, PAIRS])
        affT, work = sb("affT", [PAIRS, NQ]), sb("work", [PAIRS, NQ])
        best = sb("best", [PAIRS, 3, 8])
        maskT = sb("maskT", [PAIRS, NQ])
        mask, rank = sb("mask", [P, PAIRS]), sb("rank", [P, PAIRS])
        upto = sb("upto", [P, NQ])
        slot = sb("slot", [P, CAP])
        onehot = sb("onehot", [P, NB, NE * CAP])
        gated = sb("gated", [P, NB, NE * CAP])
        hot_b, gated_b = sb("hot_b", [P, 2, NE * CAP]), sb("gated_b", [P, 2, NE * CAP])
        tb = ps("tb", [P, 2, BANK])
        lb, rb, gb0 = (ps(n, [P, BANK]) for n in ("lb", "rb", "gb"))
        gb = [gb0, rb]
        xb_ps = [ps("xb_ps", [P, 2, BANK]), tb]
        (gw_in, gwT_mm, gwT_ready, xs_ready, xT_mm, xT_ready, logit_mm, logit_out, sub_done, exp_done, aff_ready, affT_mm,
         mask_ready, mask_mm, mask_out, rank_mm, batch_ready, gather_mm, gather_dve, gather_act, gatedT_mm, gatedT_out, dve_own,
         pool_own, var_ready, std_ready) = (sem(n) for n in (
             "gw_in", "gwT_mm", "gwT_ready", "xs_ready", "xT_mm", "xT_ready", "logit_mm", "logit_out", "sub_done", "exp_done",
             "aff_ready", "affT_mm", "mask_ready", "mask_mm", "mask_out", "rank_mm", "batch_ready", "gather_mm",
             "gather_dve", "gather_act", "gatedT_mm", "gatedT_out", "dve_own", "pool_own", "var_ready", "std_ready"))

        with nc.Block() as block:

            @block.sync
            def _(sp):
                sp.dma_start(gw[:], gate_w).then_inc(gw_in, 16)
                for n in range(NSLOT):
                    W.load(sp, 0, n)

            @block.gpsimd
            def _(pool):
                nc.gpsimd.memset(upto[:], 1.0).then_inc(pool_own, 1)
                pool.wait_ge(pool_own, 1)
                nc.gpsimd.affine_select(out=upto[:], in_=upto[:], compare_op=ALU.is_ge, fill=0.0, base=0,
                                        pattern=[[1, NQ]], channel_multiplier=-1).then_inc(pool_own, 1)
                nc.gpsimd.iota(slot[:], [[1, CAP]], base=1, channel_multiplier=0,
                               allow_small_or_imprecise_dtypes=True).then_inc(pool_own, 1)

            @block.tensor
            def _(pe):
                pe.sem_inc(gatedT_mm, 2 * FREE)
                pe.wait_ge(gw_in, 16)
                for c in range(DC):
                    last = nc.tensor.transpose(rb[:, c * NE:(c + 1) * NE], gw[:, c * P:(c + 1) * P], S.ident[0:NE, 0:NE])
                last.then_inc(gwT_mm, 1)
                pe.wait_ge(gwT_ready, 1)
                with pe.Fori(0, NB // 2) as b2:
                    for r in range(2):
                        pe.wait_ge(xs_ready, b2 * 2 + r + 1)
                        for c in range(DC):
                            last = nc.tensor.transpose(tb[:, r, c * NQ:(c + 1) * NQ], xs[0:NQ, r, c * P:(c + 1) * P], S.ident[0:NQ, 0:NQ])
                        last.then_inc(xT_mm, 1)
                    pe.wait_ge(logit_out, FREE + b2)
                    for r in range(2):
                        pe.wait_ge(xT_ready, b2 * 2 + r + 1)
                        for c in range(DC):
                            last = nc.tensor.matmul(lb[0:NQ, r * NE:(r + 1) * NE], xT[:, r, c, :], gwT[:, c, :], start=(c == 0), stop=(c == DC - 1))
                    last.then_inc(logit_mm, 1)
                pe.wait_ge(aff_ready, 1)
                nc.tensor.transpose(rb[0:PAIRS, 0:NQ], aff[0:NQ, :], S.ident[0:NQ, 0:NQ]).then_inc(affT_mm, 1)
                pe.wait_ge(mask_ready, 1)
                nc.tensor.transpose(lb[0:NQ, 0:PAIRS], maskT[:], S.ident[0:PAIRS, 0:PAIRS]).then_inc(mask_mm, 1)
                pe.wait_ge(mask_out, 1)
                pe.wait_ge(pool_own, 3)
                nc.tensor.matmul(rb[0:NQ, 0:PAIRS], upto[0:NQ, :], mask[0:NQ, :], start=True, stop=True).then_inc(rank_mm, 1)
                with pe.Fori(0, NB // 2) as b2:
                    for r in range(2):
                        b = b2 * 2 + r
                        pe.wait_ge(batch_ready, b + 1)
                        pe.wait_ge(gather_dve, b + 1)
                        pe.wait_ge(gather_act, b + 1)
                        for c in range(DC):
                            last = nc.tensor.matmul(xb_ps[r][:, c // 2, (c % 2) * NE * CAP:(c % 2 + 1) * NE * CAP], xs[0:NQ, r, c * P:(c + 1) * P],
                                                    hot_b[0:NQ, r, :], start=True, stop=True)
                        last.then_inc(gather_mm, 1)
                        pe.wait_ge(gatedT_out, b + 1)
                        for h in range(2):
                            last = nc.tensor.transpose(gb[r][0:2 * HALF, h * NQ:(h + 1) * NQ],
                                                       gated_b[0:NQ, r, h * 2 * HALF:(h + 1) * 2 * HALF], S.ident[0:NQ, 0:NQ])
                        last.then_inc(gatedT_mm, 1)

            def gather_half(copy, b, r, half):
                for c in (2 * half, 2 * half + 1):
                    last = copy(xinT[:, c, :, bass.ds(b, 1), :],
                                xb_ps[r][:, half, (c % 2) * NE * CAP:(c % 2 + 1) * NE * CAP].rearrange("p (e a s) -> p e a s", e=NE, a=1))
                return last

            @block.scalar
            def _(act):
                act.sem_inc(gatedT_out, 2 * FREE)
                act.sem_inc(gather_act, 2 * FREE)
                act.wait_ge(var_ready, 1)
                nc.scalar.activation(std[0:NQ, :], std[0:NQ, :], ACT.Sqrt).then_inc(std_ready, 1)
                with act.Fori(0, NB // 2) as b2:
                    for r in range(2):
                        act.wait_ge(xT_mm, b2 * 2 + r + 1)
                        nc.scalar.copy(xT[:, r], tb[:, r, 0:DC * NQ].rearrange("p (c q) -> p c q", c=DC)).then_inc(xT_ready, 1)
                act.wait_ge(sub_done, 1)
                nc.scalar.activation(logits[0:NQ], logits[0:NQ], ACT.Exp).then_inc(exp_done, 1)
                with act.Fori(0, NB // 2) as b2:
                    for r in range(2):
                        b = b2 * 2 + r
                        act.wait_ge(gather_mm, b + 1)
                        gather_half(nc.scalar.copy, b, r, 1).then_inc(gather_act, 1)
                        act.wait_ge(gatedT_mm, 2 * FREE + b + 1)
                        nc.scalar.copy(one(scatter[:], b), gb[r][0:2 * HALF, 0:2 * NQ].rearrange("p (a h q) -> p a h q", a=1, h=2)).then_inc(gatedT_out, 1)

            @block.vector
            def _(dve):
                dve.sem_inc(logit_out, FREE)
                dve.sem_inc(gather_dve, 2 * FREE)
                link = Chain(dve, dve_own)
                dve.wait_ge(gwT_mm, 1)
                nc.vector.tensor_copy(gwT[:], rb[:, 0:DC * NE].rearrange("p (c e) -> p c e", c=DC)).then_inc(gwT_ready, 1)
                for b in range(NB):
                    last = nc.vector.bn_stats(stats[0:NQ, b, :], S.X[0:NQ, b, :])
                link(last)
                for b in range(NB):
                    last = nc.vector.bn_aggr(mean_var[0:NQ, b, :], stats[0:NQ, b, :])
                link(last)
                nc.vector.tensor_scalar(std[0:NQ, :], mean_var[0:NQ, :, 1], LN_EPS, None, ALU.add).then_inc(var_ready, 1)
                dve.wait_ge(std_ready, 1)
                link(nc.vector.reciprocal(rstd[0:NQ, :], std[0:NQ, :]))

                def normalise(b, r):
                    return nc.vector.tensor_scalar(xs[0:NQ, r, :].unsqueeze(1), one(S.X[0:NQ], b),
                                                   one(mean_var[0:NQ], b)[:, :, 0:1].rearrange("p a c -> p (a c)"),
                                                   one(rstd[0:NQ], b), ALU.subtract, ALU.mult)

                with dve.Fori(0, NB // 2) as b2:
                    for r in range(2):
                        normalise(b2 * 2 + r, r).then_inc(xs_ready, 1)
                    dve.wait_ge(logit_mm, b2 + 1)
                    nc.vector.tensor_copy(logits[0:NQ, bass.ds(b2 * 2, 2), :], lb[0:NQ, 0:2 * NE].rearrange("p (r e) -> p r e", r=2)).then_inc(logit_out, 1)
                dve.wait_ge(logit_out, FREE + NB // 2)
                link(nc.vector.tensor_reduce(top[0:NQ, :], logits[0:NQ], axis=AX, op=ALU.max))
                nc.vector.tensor_tensor(logits[0:NQ], logits[0:NQ], top[0:NQ, :].unsqueeze(2).broadcast_to([NQ, NB, NE]),
                                        ALU.subtract).then_inc(sub_done, 1)
                dve.wait_ge(exp_done, 1)
                link(nc.vector.tensor_reduce(total[0:NQ, :], logits[0:NQ], axis=AX, op=ALU.add))
                link(nc.vector.reciprocal(total[0:NQ, :], total[0:NQ, :]))
                nc.vector.tensor_tensor(aff[0:NQ, :].rearrange("p (b e) -> p b e", b=NB), logits[0:NQ],
                                        total[0:NQ, :].unsqueeze(2).broadcast_to([NQ, NB, NE]), ALU.mult).then_inc(aff_ready, 1)
                dve.wait_ge(affT_mm, 1)
                nc.vector.tensor_copy(affT[:], rb[0:PAIRS, 0:NQ])
                link(nc.vector.tensor_copy(work[:], rb[0:PAIRS, 0:NQ]))
                for k in range(CAP // 8):
                    link(nc.vector.max(best[:, k, :], work[:]))
                    link(nc.vector.match_replace(work[:], best[:, k, :], work[:], -1.0))
                nc.vector.tensor_scalar(maskT[:], work[:], 0.0, None, ALU.is_lt).then_inc(mask_ready, 1)
                dve.wait_ge(mask_mm, 1)
                nc.vector.tensor_copy(mask[0:NQ, :], lb[0:NQ, 0:PAIRS]).then_inc(mask_out, 1)
                dve.wait_ge(rank_mm, 1)
                dve.wait_ge(mask_out, 1)
                link(nc.vector.tensor_tensor(rank[0:NQ, :], rb[0:NQ, 0:PAIRS], mask[0:NQ, :], ALU.mult))
                hot = onehot[0:NQ].rearrange("p b (e s) -> p (b e) s", e=NE)
                link(nc.vector.tensor_tensor(hot, rank[0:NQ, :].unsqueeze(2).broadcast_to([NQ, PAIRS, CAP]),
                                             slot[0:NQ, :].unsqueeze(1).broadcast_to([NQ, PAIRS, CAP]), ALU.is_equal))
                link(nc.vector.tensor_tensor(gated[0:NQ].rearrange("p b (e s) -> p (b e) s", e=NE), hot,
                                             aff[0:NQ, :].unsqueeze(2).broadcast_to([NQ, PAIRS, CAP]), ALU.mult))
                with dve.Fori(0, NB // 2) as b2:
                    for r in range(2):
                        b = b2 * 2 + r
                        dve.wait_ge(gatedT_mm, b + 1)
                        normalise(b, r)
                        nc.vector.tensor_copy(hot_b[0:NQ, r, :].unsqueeze(1), one(onehot[0:NQ], b))
                        nc.vector.tensor_copy(gated_b[0:NQ, r, :].unsqueeze(1), one(gated[0:NQ], b)).then_inc(batch_ready, 1)
                    for r in range(2):
                        b = b2 * 2 + r
                        dve.wait_ge(gather_mm, b + 1)
                        gather_half(nc.vector.tensor_copy, b, r, 0).then_inc(gather_dve, 1)


def experts_stage(nc, S, W, xinT, yT):
    NGU = 2 * IB
    NGRP = NGU + DC * IB // 4
    AHEAD = 2
    NT, NHB, NW = 3, 3, 4
    with ExitStack() as ctx:
        m = Mem(nc, ctx, "exp")
        sb, ps, sem = m.sb, m.ps, m.sem
        w_nat = W.places
        wT = sb("wT", [P, 2, NW, BANK], F32R)
        xe = sb("xe", [P, DC, 2, SLOTS], F32R)
        hT = sb("hT", [P, IB, 2, SLOTS], F32R)
        gate_sum, up_sum, sg, hid = (sb(n, [P, 2, SLOTS]) for n in ("gate_sum", "up_sum", "sg", "hid"))
        part, y_rest = sb("part", [P, NHB, SLOTS]), sb("y_rest", [P, SLOTS])
        tb = ps("tb", [P, NT, BANK])
        hb = ps("hb", [P, NHB, BANK])
        yb = ps("yb", [P, 2, BANK])
        (xe_high, xe_ready, t_mm, w_high, w_rest, p_mm, part_out, sum_out, silu_done, hid_ready, h_high, h_ready, y_mm, y_part, y_out) = (
            sem(n) for n in ("xe_high", "xe_ready", "t_mm", "w_high", "w_rest", "p_mm", "part_out", "sum_out", "silu_done", "hid_ready",
                             "h_high", "h_ready", "y_mm", "y_part", "y_out"))

        def group_load(g):
            if g < NGU:
                return 2 * (g // 2 // LOAD) + g % 2
            return 2 * IB // LOAD + (g - NGU) // 4

        def last_group(n):
            return max(g for g in range(NGRP) if group_load(g) == n)

        with nc.Block() as block:

            @block.sync
            def _(sp):
                with sp.Fori(0, NE - 1) as e:
                    down_rows = [sp.snap(e * DC + d) for d in range(DC)]
                    for n in range(NSLOT, NL + NSLOT):
                        sp.wait_ge(t_mm, e * NGRP + last_group(n - NSLOT) + 1)
                        if 2 * IB // LOAD <= n < NL:
                            W.load(sp, e, n, down_rows[n - 2 * IB // LOAD])
                        elif n < NL:
                            W.load(sp, e, n)
                        else:
                            W.load(sp, e + 1, n - NL)
                for n in range(NSLOT, NL):
                    sp.wait_ge(t_mm, (NE - 1) * NGRP + last_group(n - NSLOT) + 1)
                    W.load(sp, NE - 1, n)

            @block.tensor
            def _(pe):
                pe.sem_inc(w_rest, FREE)

                def transposes(e, g, first=False):
                    n = group_load(g) if g < NGRP else NL + group_load(g - NGRP)
                    pe.wait_ge(W.w_in[n % NSLOT], e * (16 * (NL // NSLOT)) + 16 * (n // NSLOT + 1))
                    if not first:
                        pe.wait_ge(w_rest, FREE + e * NGRP + g - NT + 1)
                    k = g % NGRP
                    at = (k // 2 % LOAD) * D if k < NGU else ((k - NGU) % 4) * 4 * P
                    for t in range(4):
                        last = nc.tensor.transpose(tb[:, g % NT, t * P:(t + 1) * P], w_nat[n % NSLOT][:, at + t * P:at + (t + 1) * P], S.ident[:])
                    last.then_inc(t_mm, 1)

                def product(e, g, bank, operand, start, stop):
                    def one_of(part, t, start, stop):
                        n = 2 * SLOTS if part == 0 else SLOTS
                        x = operand(t)
                        return nc.tensor.matmul(bank[:, 0:n], wT[:, part, g % NW, t * P:(t + 1) * P],
                                                x.rearrange("p a s -> p (a s)") if part == 0 else x[:, 0, :], start=start, stop=stop)
                    pe.wait_ge(w_high, e * NGRP + g + 1)
                    for t in range(3):
                        one_of(0, t, start and t == 0, False)
                    pe.wait_ge(w_rest, FREE + e * NGRP + g + 1)
                    for t in range(4):
                        one_of(1, t, False, False)
                    return one_of(0, 3, False, stop)

                def products(e, g):
                    if g < NGU:
                        if g == 0:
                            pe.wait_ge(xe_ready, e + 1)
                        pe.wait_ge(sum_out, FREE + e * NGU + max(g - NHB + 1, 0))
                        product(e, g, hb[:, g % NHB], lambda c: xe[:, c], True, True).then_inc(p_mm, 1)
                    else:
                        d, k = (g - NGU) // 4, (g - NGU) % 4
                        pe.wait_ge(h_ready, e * IB + 4 * k + 4)
                        if k == 0:
                            pe.wait_ge(y_out, FREE + e * DC + max(d - 1, 0))
                        last = product(e, g, yb[:, d % 2], lambda t: hT[:, 4 * k + t], k == 0, k == 3)
                        if k == 3:
                            last.then_inc(y_mm, 1)

                def expert(e, final):
                    for g in range(NGRP):
                        if not (final and g + AHEAD >= NGRP):
                            transposes(e, g + AHEAD)
                        products(e, g)

                for g in range(AHEAD):
                    transposes(0, g, first=True)
                with pe.Fori(0, NE - 1) as e:
                    expert(e, False)
                expert(NE - 1, True)

            @block.scalar
            def _(act):
                def high_bits(e, g):
                    act.wait_ge(t_mm, e * NGRP + g + 1)
                    nc.scalar.copy(wT[:, 0, g % NW, :], tb[:, g % NT, :]).then_inc(w_high, 1)

                def tokens(e):
                    nc.scalar.copy(xe[:, :, 0, :].rearrange("p c (a n) -> p c a n", a=1),
                                   xinT[:, :, bass.ds(e, 1)].rearrange("p c a b s -> p c a (b s)")).then_inc(xe_high, 1)

                def expert(e, final):
                    for g in range(NGRP + 1):
                        if 1 <= g <= NGU:
                            act.wait_ge(p_mm, e * NGU + g)
                            nc.scalar.copy(part[:, (g - 1) % NHB, :], hb[:, (g - 1) % NHB, SLOTS:2 * SLOTS]).then_inc(part_out, 1)
                        if g > NGU and (g - NGU) % 4 == 0:
                            d = (g - NGU) // 4 - 1
                            act.wait_ge(y_mm, e * DC + d + 1)
                            act.wait_ge(y_out, FREE + e * DC + d)
                            nc.scalar.copy(y_rest[:], yb[:, d % 2, SLOTS:2 * SLOTS]).then_inc(y_part, 1)
                        if g < NGRP and not (final and g + AHEAD >= NGRP):
                            high_bits(e, g + AHEAD)
                        if 3 <= g <= NGU + 1 and g % 2 == 1:
                            u = (g - 3) // 2
                            act.wait_ge(sum_out, FREE + e * NGU + 2 * u + 1)
                            nc.scalar.activation(sg[:, u % 2, :], gate_sum[:, u % 2, :], ACT.Silu).then_inc(silu_done, 1)
                        for u in ((g - 6) // 2, IB - 1) if g == NGU + 2 else ((g - 6) // 2,) if 6 <= g <= NGU and g % 2 == 0 else ():
                            act.wait_ge(hid_ready, e * IB + u + 1)
                            nc.scalar.copy(hT[:, u, 0, :], hid[:, u % 2, :]).then_inc(h_high, 1)
                        if g == NGU + 2 and not final:
                            act.wait_ge(p_mm, e * NGU + NGU)
                            tokens(e + 1)

                tokens(0)
                for g in range(AHEAD):
                    high_bits(0, g)
                with act.Fori(0, NE - 1) as e:
                    expert(e, False)
                expert(NE - 1, True)

            @block.vector
            def _(dve):
                dve.sem_inc(sum_out, FREE)
                dve.sem_inc(y_out, FREE)

                def rest(e, g):
                    dve.wait_ge(w_high, e * NGRP + g + 1)
                    nc.vector.tensor_tensor(wT[:, 1, g % NW, :], tb[:, g % NT, :], wT[:, 0, g % NW, :].bitcast(F32), ALU.subtract).then_inc(w_rest, 1)

                def tokens(e):
                    dve.wait_ge(xe_high, e + 1)
                    nc.vector.tensor_tensor(xe[:, :, 1, :].rearrange("p c (a n) -> p c a n", a=1),
                                            xinT[:, :, bass.ds(e, 1)].rearrange("p c a b s -> p c a (b s)"),
                                            xe[:, :, 0, :].rearrange("p c (a n) -> p c a n", a=1).bitcast(F32), ALU.subtract).then_inc(xe_ready, 1)

                def hidden(e, u):
                    dve.wait_ge(sum_out, FREE + e * NGU + 2 * u + 2)
                    dve.wait_ge(silu_done, e * IB + u + 1)
                    nc.vector.tensor_tensor(hid[:, u % 2, :], up_sum[:, u % 2, :], sg[:, u % 2, :], ALU.mult).then_inc(hid_ready, 1)

                def hidden_rest(e, u):
                    dve.wait_ge(h_high, e * IB + u + 1)
                    nc.vector.tensor_tensor(hT[:, u, 1, :], hid[:, u % 2, :], hT[:, u, 0, :].bitcast(F32), ALU.subtract).then_inc(h_ready, 1)

                def expert(e, final):
                    for g in range(NGRP + 2):
                        if 7 <= g <= NGU + 1 and g % 2 == 1:
                            hidden_rest(e, (g - 7) // 2)
                        if 2 <= g <= NGU + 1:
                            k, u = g - 2, (g - 2) // 2
                            dve.wait_ge(part_out, e * NGU + k + 1)
                            nc.vector.tensor_tensor((gate_sum, up_sum)[k % 2][:, u % 2, :], hb[:, k % NHB, 0:SLOTS], part[:, k % NHB, :],
                                                    ALU.add).then_inc(sum_out, 1)
                        if 4 <= g <= NGU and g % 2 == 0:
                            hidden(e, (g - 4) // 2)
                        if g > NGU + 1 and (g - NGU) % 4 == 1:
                            d = (g - NGU) // 4 - 1
                            dve.wait_ge(y_part, e * DC + d + 1)
                            nc.vector.tensor_tensor(yT[:, d, :, bass.ds(e, 1), :], yb[:, d % 2, 0:SLOTS].rearrange("p (b a s) -> p b a s", b=NB, a=1),
                                                    y_rest[:].rearrange("p (b a s) -> p b a s", b=NB, a=1), ALU.add).then_inc(y_out, 1)
                        if g < NGRP and not (final and g + AHEAD >= NGRP):
                            rest(e, g + AHEAD)
                        if g == NGU + 1:
                            hidden(e, IB - 1)
                        if g == NGU + 2:
                            hidden_rest(e, IB - 2)
                            hidden_rest(e, IB - 1)
                        if g == NGU + 2 and not final:
                            tokens(e + 1)

                tokens(0)
                for g in range(AHEAD):
                    rest(0, g)
                with dve.Fori(0, NE - 1) as e:
                    expert(e, False)
                expert(NE - 1, True)


def combine_stage(nc, S, scatter, yT, out):
    with ExitStack() as ctx:
        m = Mem(nc, ctx, "comb")
        sb, ps, sem = m.sb, m.ps, m.sem
        K = 2 * HALF
        y_b = sb("y_b", [P, 2, DC, 2 * K])
        scat_b = sb("scat_b", [K, 2, 2, NQ])
        y_nat = sb("y_nat", [K, 2, 2, D])
        res = sb("res", [P, 2, D])
        tb = ps("tb", [P, 2, 2, BANK])
        ob = ps("ob", [P, 2, BANK])
        batch_ready, yT_mm, y_act, y_dve, o_mm, res_ready = (sem(n) for n in ("batch_ready", "yT_mm", "y_act", "y_dve", "o_mm", "res_ready"))
        out_done = [sem("out_done0"), sem("out_done1")]
        with nc.Block() as block:

            @block.vector
            def _(dve):
                dve.sem_inc(res_ready, 2 * FREE)
                with dve.Fori(0, NB // 2) as b2:
                    for r in range(2):
                        b = b2 * 2 + r
                        nc.vector.tensor_copy(y_b[:, r].rearrange("p c (a n) -> p c a n", a=1),
                                              yT[:, :, bass.ds(b, 1)].rearrange("p c a e s -> p c a (e s)"))
                        nc.vector.tensor_copy(scat_b[:, r].unsqueeze(1), one(scatter[:], b)).then_inc(batch_ready, 1)
                    for r in range(2):
                        dve.wait_ge(yT_mm, b2 * 4 + 2 * r + 2)
                        nc.vector.tensor_copy(y_nat[:, r, 1, :], tb[0:K, r, 1, :]).then_inc(y_dve, 1)
                    for r in range(2):
                        b = b2 * 2 + r
                        dve.wait_ge(o_mm, b + 1)
                        dve.wait_ge(out_done[r], 16 * FREE + b2 * 16)
                        nc.vector.scalar_tensor_tensor(out=res[0:NQ, r, :].unsqueeze(1), in0=ob[0:NQ, r, :].unsqueeze(1), scalar=S.tanh_g[0:NQ, 3:4],
                                                       in1=one(S.X[0:NQ], b), op0=ALU.mult, op1=ALU.add).then_inc(res_ready, 1)

            @block.scalar
            def _(act):
                act.sem_inc(out_done[0], 16 * FREE)
                act.sem_inc(out_done[1], 16 * FREE)
                with act.Fori(0, NB // 2) as b2:
                    for r in range(2):
                        act.wait_ge(yT_mm, b2 * 4 + 2 * r + 1)
                        nc.scalar.copy(y_nat[:, r, 0, :], tb[0:K, r, 0, :]).then_inc(y_act, 1)
                    for r in range(2):
                        act.wait_ge(res_ready, 2 * FREE + b2 * 2 + r + 1)
                        act.dma_start(out[bass.ds(b2 * 2 + r, 1)].rearrange("a q d -> q (a d)"), res[0:NQ, r, :]).then_inc(out_done[r], 16)
                act.wait_ge(out_done[0], 16 * FREE + 16 * (NB // 2))
                act.wait_ge(out_done[1], 16 * FREE + 16 * (NB // 2))

            @block.tensor
            def _(pe):
                with pe.Fori(0, NB // 2) as b2:
                    for r in range(2):
                        b = b2 * 2 + r
                        pe.wait_ge(batch_ready, b + 1)
                        for h in range(2):
                            for c in range(DC):
                                last = nc.tensor.transpose(tb[0:K, r, h, c * P:(c + 1) * P], y_b[:, r, c, h * K:(h + 1) * K], S.ident[:])
                            last.then_inc(yT_mm, 1)
                    for r in range(2):
                        b = b2 * 2 + r
                        pe.wait_ge(y_act, b + 1)
                        pe.wait_ge(res_ready, b + 1)
                        nc.tensor.matmul(ob[0:NQ, r, :], scat_b[:, r, 0, :], y_nat[:, r, 0, :], start=True, stop=False)
                        pe.wait_ge(y_dve, b + 1)
                        nc.tensor.matmul(ob[0:NQ, r, :], scat_b[:, r, 1, :], y_nat[:, r, 1, :], start=False, stop=True).then_inc(o_mm, 1)


def flamingo(nc, x, ctx_1024, g_xattn, g_ffn, a0, f0, a1, mlp, f1, out):
    with ExitStack() as ctx:
        S = start_state(nc, ctx)
        weights = lambda a: [square(w) for w in (a[0], a[2], a[4])]
        setup_stage(nc, S, x, g_xattn, g_ffn, weights(a0))
        attention_stage(nc, S, 0, ctx_1024, *a0, following=[square(f0[0][n * D:(n + 1) * D]) for n in range(3)])
        quantised_stage(nc, S, *f0, weights(a1))
        attention_stage(nc, S, 1, ctx_1024, *a1, mlp=mlp)
        mixture_stages(nc, S, *f1, out)


_A0 = ["L0_xattn_" + n for n in ("wq_w", "wq_b", "wk_w", "wk_b", "wv_w", "wv_b", "dense_w", "dense_b")]
_F0 = ["L0_ffn_" + n for n in ("w_gate", "w_up", "w_down")]
_A1 = ["L1_xattn_" + n for n in ("Wq", "bq", "Wk", "bk", "Wv", "bv", "Wo", "bo")]
_MLP = ["L1_xattn_" + n for n in ("w1", "b1", "w2", "b2", "w3", "b3")]
_F1 = ["L1_ffn_" + n for n in ("gate_w", "w_gate", "w_up", "w_down")]


def kernel(**inputs):
    import numpy as _np
    import concourse.bacc as _bacc
    from concourse import mybir as _mybir
    from concourse.bass_utils import run_bass_kernel_spmd as _run

    nc = _bacc.Bacc("TRN2", target_bir_lowering=False, num_devices=1)
    arrays, args = {}, {}
    for name in ["x", "ctx_1024", "g_xattn", "g_ffn"] + _A0 + _F0 + _A1 + _MLP + _F1:
        a = _np.ascontiguousarray(inputs[name])
        arrays[f"in_{name}_dram"] = a
        args[name] = nc.dram_tensor(f"in_{name}_dram", a.shape, _mybir.dt.from_np(a.dtype), kind="ExternalInput").ap()
    out = nc.dram_tensor("out_0_dram", (NB, NQ, D), F32, kind="ExternalOutput").ap()
    flamingo(nc, args["x"], args["ctx_1024"], args["g_xattn"], args["g_ffn"], *([args[n] for n in g] for g in (_A0, _F0, _A1, _MLP, _F1)), out)
    r = _run(nc, [arrays], core_ids=[0])
    return r.results[0]["out_0_dram"]
```
